# Optimizing a Trainium2 kernel written in Bass

```python
import numpy as np
import jax
import jax.numpy as jnp

def _softmax(x, axis=-1):
    return jax.nn.softmax(x, axis=axis)

def _gelu(x):
    return jax.nn.gelu(x, approximate=True)

def _silu(x):
    return jax.nn.silu(x)

def _sigmoid(x):
    return jax.nn.sigmoid(x)

def _layernorm(x, axis=-1, eps=1e-05):
    m = jnp.mean(x, axis=axis, keepdims=True)
    v = jnp.var(x, axis=axis, keepdims=True)
    return (x - m) / jnp.sqrt(v + eps)

def _scatter_add(tgt, idx, src, axis=0):
    return tgt.at[idx].add(src)

def _segment_sum(src, seg, n):
    return jax.ops.segment_sum(src, seg, n)
kernel_name = 'mk_metaformer_d2_conv_nhwc768_r4_f30307'

def setup_inputs(seed: int=0):
    np.random.seed(seed)
    _w = jnp.asarray

    def _rec_inputs():
        import jax
        import jax.numpy as jnp
        _gk = jax.random.key(seed)
        x = -0.0005963 + 1.001 * jax.random.normal(jax.random.fold_in(_gk, 1), (4, 32, 32, 192), jnp.float32)
        return x
    x = _rec_inputs()

    def _L0_conv_setup():
        import jax, jax.numpy as jnp
        import numpy as np
        B, H, W, DIM, NH = (4, 32, 32, 192, 12)
        HD = DIM // NH

        def _get_rel_pos(size, rel_pos):
            idx = jnp.arange(size)[:, None] - jnp.arange(size)[None, :] + (size - 1)
            return rel_pos[idx]
        key = jax.random.key(seed)
        ks = jax.random.split(key, 7)
        s = 0.02
        return {'x': jax.random.normal(ks[0], (B, H, W, DIM), dtype=jnp.float32), 'qkv_w': jax.random.normal(ks[1], (3 * DIM, DIM), dtype=jnp.float32) * s, 'qkv_b': jax.random.normal(ks[2], (3 * DIM,), dtype=jnp.float32) * s, 'proj_w': jax.random.normal(ks[3], (DIM, DIM), dtype=jnp.float32) * s, 'proj_b': jax.random.normal(ks[4], (DIM,), dtype=jnp.float32) * s, 'rel_pos_h': jax.random.normal(ks[5], (2 * H - 1, HD), dtype=jnp.float32) * s, 'rel_pos_w': jax.random.normal(ks[6], (2 * W - 1, HD), dtype=jnp.float32) * s}
    _L0_conv_all = _L0_conv_setup()
    _L0_conv_in = {k: v for k, v in _L0_conv_all.items() if k in ('qkv_w', 'qkv_b', 'proj_w', 'proj_b', 'rel_pos_h', 'rel_pos_w')}
    del _L0_conv_all

    def _L0_ffn_setup():
        import jax, jax.numpy as jnp
        import numpy as np
        K = 2
        key = jax.random.key(seed)
        ks = jax.random.split(key, 5)
        B, T, D, E, H = (2, 512, 192, 8, 384)
        x = jax.random.normal(ks[0], (B, T, D), dtype=jnp.float32)
        gate_w = jax.random.normal(ks[1], (E, D), dtype=jnp.float32) * (1.0 / np.sqrt(D))
        gate_bank = jax.random.normal(ks[2], (E, D, H), dtype=jnp.float32) * (1.0 / np.sqrt(D))
        up_bank = jax.random.normal(ks[3], (E, D, H), dtype=jnp.float32) * (1.0 / np.sqrt(D))
        down_bank = jax.random.normal(ks[4], (E, H, D), dtype=jnp.float32) * (1.0 / np.sqrt(H))
        return {'x': x, 'gate_w': gate_w, 'gate_bank': gate_bank, 'up_bank': up_bank, 'down_bank': down_bank}
    _L0_ffn_all = _L0_ffn_setup()
    _L0_ffn_in = {k: v for k, v in _L0_ffn_all.items() if k in ('gate_w', 'gate_bank', 'up_bank', 'down_bank')}
    del _L0_ffn_all

    def _L1_conv_setup():
        import jax, jax.numpy as jnp
        import numpy as np
        B, Hs, Ws, DIM = (8, 32, 32, 192)
        NH, HD = (12, 16)

        def get_rel_pos(size, rel_pos):
            coords = jnp.arange(size)[:, None] - jnp.arange(size)[None, :] + (size - 1)
            return rel_pos[coords]
        key = jax.random.key(seed)
        ks = jax.random.split(key, 7)
        inv = 1.0 / np.sqrt(DIM)
        return {'x': jax.random.normal(ks[0], (B, Hs, Ws, DIM), jnp.float32), 'qkv_w': jax.random.normal(ks[1], (3 * DIM, DIM), jnp.float32) * inv, 'qkv_b': jax.random.normal(ks[2], (3 * DIM,), jnp.float32) * 0.02, 'proj_w': jax.random.normal(ks[3], (DIM, DIM), jnp.float32) * inv, 'proj_b': jax.random.normal(ks[4], (DIM,), jnp.float32) * 0.02, 'rel_pos_h': jax.random.normal(ks[5], (2 * Hs - 1, HD), jnp.float32) * 0.02, 'rel_pos_w': jax.random.normal(ks[6], (2 * Ws - 1, HD), jnp.float32) * 0.02}
    _L1_conv_all = _L1_conv_setup()
    _L1_conv_in = {k: v for k, v in _L1_conv_all.items() if k in ('qkv_w', 'qkv_b', 'proj_w', 'proj_b', 'rel_pos_h', 'rel_pos_w')}
    del _L1_conv_all

    def _L1_ffn_setup():
        import jax, jax.numpy as jnp
        import numpy as np
        E = 192
        H = 12
        D = E // H
        HID = 768
        NEXP = 4
        TOPK = 2
        EPS = 1e-05

        def _ln(x, g, b):
            m = jnp.mean(x, axis=-1, keepdims=True)
            v = jnp.mean(jnp.square(x - m), axis=-1, keepdims=True)
            return (x - m) * jax.lax.rsqrt(v + EPS) * g + b
        key = jax.random.key(seed)
        ks = jax.random.split(key, 10)
        s = 0.02
        return {'x': jax.random.normal(ks[0], (8, 256, E), jnp.float32), 'ln1_g': jnp.ones((E,), jnp.float32), 'ln1_b': jnp.zeros((E,), jnp.float32), 'in_w': jax.random.normal(ks[1], (3 * E, E), jnp.float32) * s, 'in_b': jnp.zeros((3 * E,), jnp.float32), 'out_w': jax.random.normal(ks[2], (E, E), jnp.float32) * s, 'out_b': jnp.zeros((E,), jnp.float32), 'mlp_w1': jax.random.normal(ks[3], (E, HID), jnp.float32) * s, 'mlp_b1': jnp.zeros((HID,), jnp.float32), 'mlp_w2': jax.random.normal(ks[4], (HID, E), jnp.float32) * s, 'mlp_b2': jnp.zeros((E,), jnp.float32), 'ln2_g': jnp.ones((E,), jnp.float32), 'ln2_b': jnp.zeros((E,), jnp.float32), 'gate_w': jax.random.normal(ks[5], (NEXP, E), jnp.float32) * s, 'gate_b': jnp.zeros((NEXP,), jnp.float32), 'exp_w1': jax.random.normal(ks[6], (NEXP, E, HID), jnp.float32) * s, 'exp_b1': jnp.zeros((NEXP, HID), jnp.float32), 'exp_w2': jax.random.normal(ks[7], (NEXP, HID, E), jnp.float32) * s, 'exp_b2': jnp.zeros((NEXP, E), jnp.float32)}
    _L1_ffn_all = _L1_ffn_setup()
    _L1_ffn_in = {k: v for k, v in _L1_ffn_all.items() if k in ('ln1_g', 'ln1_b', 'in_w', 'in_b', 'out_w', 'out_b', 'mlp_w1', 'mlp_b1', 'mlp_w2', 'mlp_b2', 'ln2_g', 'ln2_b', 'gate_w', 'gate_b', 'exp_w1', 'exp_b1', 'exp_w2', 'exp_b2')}
    del _L1_ffn_all
    return {'x': x, 'L0_conv_qkv_w': _L0_conv_in['qkv_w'], 'L0_conv_qkv_b': _L0_conv_in['qkv_b'], 'L0_conv_proj_w': _L0_conv_in['proj_w'], 'L0_conv_proj_b': _L0_conv_in['proj_b'], 'L0_conv_rel_pos_h': _L0_conv_in['rel_pos_h'], 'L0_conv_rel_pos_w': _L0_conv_in['rel_pos_w'], 'L0_ffn_gate_w': _L0_ffn_in['gate_w'], 'L0_ffn_gate_bank': _L0_ffn_in['gate_bank'], 'L0_ffn_up_bank': _L0_ffn_in['up_bank'], 'L0_ffn_down_bank': _L0_ffn_in['down_bank'], 'L1_conv_qkv_w': _L1_conv_in['qkv_w'], 'L1_conv_qkv_b': _L1_conv_in['qkv_b'], 'L1_conv_proj_w': _L1_conv_in['proj_w'], 'L1_conv_proj_b': _L1_conv_in['proj_b'], 'L1_conv_rel_pos_h': _L1_conv_in['rel_pos_h'], 'L1_conv_rel_pos_w': _L1_conv_in['rel_pos_w'], 'L1_ffn_ln1_g': _L1_ffn_in['ln1_g'], 'L1_ffn_ln1_b': _L1_ffn_in['ln1_b'], 'L1_ffn_in_w': _L1_ffn_in['in_w'], 'L1_ffn_in_b': _L1_ffn_in['in_b'], 'L1_ffn_out_w': _L1_ffn_in['out_w'], 'L1_ffn_out_b': _L1_ffn_in['out_b'], 'L1_ffn_mlp_w1': _L1_ffn_in['mlp_w1'], 'L1_ffn_mlp_b1': _L1_ffn_in['mlp_b1'], 'L1_ffn_mlp_w2': _L1_ffn_in['mlp_w2'], 'L1_ffn_mlp_b2': _L1_ffn_in['mlp_b2'], 'L1_ffn_ln2_g': _L1_ffn_in['ln2_g'], 'L1_ffn_ln2_b': _L1_ffn_in['ln2_b'], 'L1_ffn_gate_w': _L1_ffn_in['gate_w'], 'L1_ffn_gate_b': _L1_ffn_in['gate_b'], 'L1_ffn_exp_w1': _L1_ffn_in['exp_w1'], 'L1_ffn_exp_b1': _L1_ffn_in['exp_b1'], 'L1_ffn_exp_w2': _L1_ffn_in['exp_w2'], 'L1_ffn_exp_b2': _L1_ffn_in['exp_b2']}

def reference(x, L0_conv_qkv_w, L0_conv_qkv_b, L0_conv_proj_w, L0_conv_proj_b, L0_conv_rel_pos_h, L0_conv_rel_pos_w, L0_ffn_gate_w, L0_ffn_gate_bank, L0_ffn_up_bank, L0_ffn_down_bank, L1_conv_qkv_w, L1_conv_qkv_b, L1_conv_proj_w, L1_conv_proj_b, L1_conv_rel_pos_h, L1_conv_rel_pos_w, L1_ffn_ln1_g, L1_ffn_ln1_b, L1_ffn_in_w, L1_ffn_in_b, L1_ffn_out_w, L1_ffn_out_b, L1_ffn_mlp_w1, L1_ffn_mlp_b1, L1_ffn_mlp_w2, L1_ffn_mlp_b2, L1_ffn_ln2_g, L1_ffn_ln2_b, L1_ffn_gate_w, L1_ffn_gate_b, L1_ffn_exp_w1, L1_ffn_exp_b1, L1_ffn_exp_w2, L1_ffn_exp_b2):
    import jax
    import jax.numpy as jnp

    def _L0_conv_ref(x, qkv_w, qkv_b, proj_w, proj_b, rel_pos_h, rel_pos_w):
        import jax, jax.numpy as jnp
        import numpy as np
        B, H, W, DIM, NH = (4, 32, 32, 192, 12)
        HD = DIM // NH

        def _get_rel_pos(size, rel_pos):
            idx = jnp.arange(size)[:, None] - jnp.arange(size)[None, :] + (size - 1)
            return rel_pos[idx]
        b, h, w, c = x.shape
        hw = h * w
        hd = c // NH
        scale = hd ** (-0.5)
        qkv = x @ qkv_w.T + qkv_b
        qkv = qkv.reshape(b, hw, 3, NH, hd).transpose(2, 0, 3, 1, 4)
        q, k, v = (qkv[0], qkv[1], qkv[2])
        Rh = _get_rel_pos(h, rel_pos_h)
        Rw = _get_rel_pos(w, rel_pos_w)
        r_q = q.reshape(b, NH, h, w, hd)
        rel_h = jnp.einsum('bnhwc,hkc->bnhwk', r_q, Rh)
        rel_w = jnp.einsum('bnhwc,wkc->bnhwk', r_q, Rw)
        bias = (rel_h[..., :, None] + rel_w[..., None, :]).reshape(b, NH, hw, hw)
        attn = jnp.einsum('bnqd,bnkd->bnqk', q, k) * scale + bias
        attn = jax.nn.softmax(attn, axis=-1)
        out = jnp.einsum('bnqk,bnkd->bnqd', attn, v)
        out = out.reshape(b, NH, h, w, hd).transpose(0, 2, 3, 1, 4).reshape(b, h, w, c)
        return out @ proj_w.T + proj_b

    def _L0_ffn_ref(x, gate_w, gate_bank, up_bank, down_bank):
        import jax, jax.numpy as jnp
        import numpy as np
        K = 2
        logits = jnp.einsum('btd,ed->bte', x, gate_w)
        probs = jax.nn.softmax(logits, axis=-1)
        selected_probs, selected_idx = jax.lax.top_k(probs, K)
        selected_probs = selected_probs / (jnp.sum(selected_probs, axis=-1, keepdims=True) + 1e-08)
        a = jnp.einsum('btd,edh->bteh', x, gate_bank)
        u = jnp.einsum('btd,edh->bteh', x, up_bank)
        h = jax.nn.silu(a) * u
        y_all = jnp.einsum('bteh,ehd->bted', h, down_bank)
        y_sel = jnp.take_along_axis(y_all, selected_idx[..., None], axis=2)
        y = jnp.sum(y_sel * selected_probs[..., None], axis=2)
        return y

    def _L1_conv_ref(x, qkv_w, qkv_b, proj_w, proj_b, rel_pos_h, rel_pos_w):
        import jax, jax.numpy as jnp
        import numpy as np
        B, Hs, Ws, DIM = (8, 32, 32, 192)
        NH, HD = (12, 16)

        def get_rel_pos(size, rel_pos):
            coords = jnp.arange(size)[:, None] - jnp.arange(size)[None, :] + (size - 1)
            return rel_pos[coords]
        Bb, H, W, C = x.shape
        L = H * W
        scale = HD ** (-0.5)
        qkv = x @ qkv_w.T + qkv_b
        qkv = qkv.reshape(Bb, L, 3, NH, HD).transpose(2, 0, 3, 1, 4)
        q, k, v = (qkv[0], qkv[1], qkv[2])
        rel_h = get_rel_pos(H, rel_pos_h)
        rel_w = get_rel_pos(W, rel_pos_w)
        q5 = q.reshape(Bb, NH, H, W, HD)
        rel_h_attn = jnp.einsum('bnhwc,hkc->bnhwk', q5, rel_h)
        rel_w_attn = jnp.einsum('bnhwc,wkc->bnhwk', q5, rel_w)
        bias = rel_h_attn[..., :, None] + rel_w_attn[..., None, :]
        bias = bias.reshape(Bb, NH, L, L)
        scores = jnp.einsum('bnqd,bnkd->bnqk', q, k) * scale + bias
        attn = jax.nn.softmax(scores, axis=-1)
        out = jnp.einsum('bnqk,bnkd->bnqd', attn, v)
        out = out.reshape(Bb, NH, H, W, HD).transpose(0, 2, 3, 1, 4).reshape(Bb, H, W, C)
        return out @ proj_w.T + proj_b

    def _L1_ffn_ref(x, ln1_g, ln1_b, in_w, in_b, out_w, out_b, mlp_w1, mlp_b1, mlp_w2, mlp_b2, ln2_g, ln2_b, gate_w, gate_b, exp_w1, exp_b1, exp_w2, exp_b2):
        import jax, jax.numpy as jnp
        import numpy as np
        E = 192
        H = 12
        D = E // H
        HID = 768
        NEXP = 4
        TOPK = 2
        EPS = 1e-05

        def _ln(x, g, b):
            m = jnp.mean(x, axis=-1, keepdims=True)
            v = jnp.mean(jnp.square(x - m), axis=-1, keepdims=True)
            return (x - m) * jax.lax.rsqrt(v + EPS) * g + b
        B, N, _ = x.shape
        h = _ln(x, ln1_g, ln1_b)
        qkv = h @ in_w.T + in_b
        q, k, v = jnp.split(qkv, 3, axis=-1)
        q = q.reshape(B, N, H, D)
        k = k.reshape(B, N, H, D)
        v = v.reshape(B, N, H, D)
        scores = jnp.einsum('bqhd,bkhd->bhqk', q, k) / jnp.sqrt(jnp.float32(D))
        attn = jax.nn.softmax(scores, axis=-1)
        ctx = jnp.einsum('bhqk,bkhd->bqhd', attn, v).reshape(B, N, E)
        x = x + ctx @ out_w.T + out_b
        x = x + jax.nn.gelu(x @ mlp_w1 + mlp_b1, approximate=False) @ mlp_w2 + mlp_b2
        xm = _ln(x, ln2_g, ln2_b)
        logits = xm @ gate_w.T + gate_b
        topv, topi = jax.lax.top_k(logits, TOPK)
        gates = jax.nn.softmax(topv, axis=-1)
        onehot = jax.nn.one_hot(topi, NEXP, dtype=x.dtype)
        comb = jnp.einsum('bnk,bnke->bne', gates, onehot)
        moe_out = jnp.zeros_like(x)
        for e in range(NEXP):
            he = jax.nn.gelu(xm @ exp_w1[e] + exp_b1[e], approximate=False)
            oe = he @ exp_w2[e] + exp_b2[e]
            moe_out = moe_out + comb[..., e:e + 1] * oe
        return x + moe_out

    def _gn(v, G=32, eps=1e-05):
        B_, H_, W_, C_ = v.shape
        g = v.reshape(B_, H_, W_, G, C_ // G)
        m = jnp.mean(g, axis=(1, 2, 4), keepdims=True)
        s = jnp.var(g, axis=(1, 2, 4), keepdims=True)
        return ((g - m) / jnp.sqrt(s + eps)).reshape(v.shape)

    def _ln_c(v, eps=1e-06):
        m = jnp.mean(v, axis=-1, keepdims=True)
        s = jnp.var(v, axis=-1, keepdims=True)
        return (v - m) / jnp.sqrt(s + eps)

    def _ln_t(v, eps=1e-05):
        m = jnp.mean(v, axis=-1, keepdims=True)
        s = jnp.var(v, axis=-1, keepdims=True)
        return (v - m) / jnp.sqrt(s + eps)

    def _to_tokens(v):
        B_, H_, W_, C_ = v.shape
        return v.reshape(B_, H_ * W_, C_)

    def _from_tokens(t, like):
        return t.reshape(like.shape)
    x = x + _L0_conv_ref(_ln_c(x), L0_conv_qkv_w, L0_conv_qkv_b, L0_conv_proj_w, L0_conv_proj_b, L0_conv_rel_pos_h, L0_conv_rel_pos_w)
    t = _to_tokens(x)
    t = t + _L0_ffn_ref(_ln_t(t), L0_ffn_gate_w, L0_ffn_gate_bank, L0_ffn_up_bank, L0_ffn_down_bank)
    x = _from_tokens(t, x)
    x = x + _L1_conv_ref(_ln_c(x), L1_conv_qkv_w, L1_conv_qkv_b, L1_conv_proj_w, L1_conv_proj_b, L1_conv_rel_pos_h, L1_conv_rel_pos_w)
    t = _to_tokens(x)
    t = t + _L1_ffn_ref(_ln_t(t), L1_ffn_ln1_g, L1_ffn_ln1_b, L1_ffn_in_w, L1_ffn_in_b, L1_ffn_out_w, L1_ffn_out_b, L1_ffn_mlp_w1, L1_ffn_mlp_b1, L1_ffn_mlp_w2, L1_ffn_mlp_b2, L1_ffn_ln2_g, L1_ffn_ln2_b, L1_ffn_gate_w, L1_ffn_gate_b, L1_ffn_exp_w1, L1_ffn_exp_b1, L1_ffn_exp_w2, L1_ffn_exp_b2)
    x = _from_tokens(t, x)
    return x

_drawn_inputs = setup_inputs


def setup_inputs(seed=0):
    import zlib

    import numpy as np

    out = dict(_drawn_inputs(seed))
    spreads = {'L1_ffn_ln1_g': (1.0, 0.6),
     'L1_ffn_ln1_b': (0.0, 0.8),
     'L1_ffn_in_b': (0.0, 0.531),
     'L1_ffn_out_b': (0.0, 0.328),
     'L1_ffn_mlp_b1': (0.0, 0.501),
     'L1_ffn_mlp_b2': (0.0, 0.369),
     'L1_ffn_ln2_g': (1.0, 0.6),
     'L1_ffn_ln2_b': (0.0, 2.0),
     'L1_ffn_gate_b': (0.0, 0.493),
     'L1_ffn_exp_b1': (0.0, 0.769),
     'L1_ffn_exp_b2': (0.0, 0.458)}
    factors = {'L0_conv_qkv_w': 4.45,
     'L0_conv_qkv_b': 3.628,
     'L0_conv_rel_pos_h': 8.0,
     'L0_conv_rel_pos_w': 8.0,
     'L1_conv_qkv_b': 3.091,
     'L1_conv_proj_b': 3.175,
     'L1_conv_rel_pos_h': 8.0,
     'L1_conv_rel_pos_w': 8.0,
     'L1_ffn_in_w': 8.0,
     'L1_ffn_out_w': 4.131}
    for name, (base, spread) in spreads.items():
        noise = np.random.default_rng([zlib.crc32(name.encode()), seed]).standard_normal(out[name].shape)
        drawn = base * np.exp(spread * noise) if base else spread * noise
        out[name] = jnp.asarray(drawn.astype(out[name].dtype))
    for name, factor in factors.items():
        out[name] = (out[name] * factor).astype(out[name].dtype)
    return out
```

```python
from contextlib import ExitStack

import numpy as np

import concourse.bass as bass
from concourse import mybir

F32 = mybir.dt.float32
F16 = mybir.dt.float16
U32 = mybir.dt.uint32
ALU = mybir.AluOpType
ACT = mybir.ActivationFunctionType
AX = mybir.AxisListType

B, SIDE, C, NH, HD = 4, 32, 192, 12, 16
L = SIDE * SIDE
T = B * L
P = 128
TILES = T // P
CHUNK = 512
C0, C1 = P, C - P
GROUPS = 3
GH = NH // GROUPS
GW = GH * HD
KT = L // P
PAIRS = B * NH // 2
RING = 3

R_REL = 0
R_QK = 64
R_MAX = 96
R_LOW = 97
R_END = R_LOW + HD


def ts(i, n):
    return bass.ts(i, n)


class Pool:

    def __init__(self, nc, name):
        self.nc, self.name, self.stack, self.sems = nc, name, ExitStack(), []

    def __enter__(self):
        return self

    def __exit__(self, *what):
        if what[0] is None:
            nc, sems = self.nc, self.sems
            with nc.Block() as block:
                @block.sync
                def _(sp):
                    for s in sems:
                        sp.sem_clear(s)
        self.stack.close()

    def sb(self, name, width, dt=F32, parts=P):
        return self.stack.enter_context(self.nc.sbuf_tensor(f"{self.name}_{name}", [parts, width], dt))

    def ps(self, name, width=CHUNK):
        return self.stack.enter_context(self.nc.psum_tensor(f"{self.name}_{name}", [P, width], F32))

    def sem(self, name):
        s = self.stack.enter_context(self.nc.semaphore(f"{self.name}_{name}"))
        self.sems.append(s)
        return s


def linker(engine, sem):
    count = [0]

    def link(ins):
        count[0] += 1
        ins.then_inc(sem, 1)
        engine.wait_ge(sem, count[0])

    return link


def layer_norm(nc, name, src, eps, store=None, turned_to=None, gain=None, shift=None, ident=None, parts=None):
    with Pool(nc, name) as m:
        st = m.sb("stats", TILES * 6)
        mean, mdiff, vsum, var, std, rstd = (m.sb(n, TILES) for n in ("mean", "mdiff", "vsum", "var", "std", "rstd"))
        s_stats, s_chain, s_std = m.sem("stats"), m.sem("chain"), m.sem("std")
        s_ready = m.sem("ready")
        s_norm, s_turned, s_evac = m.sem("norm"), m.sem("turned"), m.sem("evac")
        s_stored = m.sem("stored")
        s_hi, s_lo, s_f32 = m.sem("hi"), m.sem("lo"), m.sem("f32")
        if turned_to is not None:
            nrm = [m.sb(f"nrm{u}", 4 * C) for u in range(2)]
            t0 = [m.ps(f"t0{u}") for u in range(2)]
            t1 = [m.ps(f"t1{u}") for u in range(2)]
        with nc.Block() as block:
            @block.vector
            def _(dve):
                with dve.Fori(0, TILES // 8) as it:
                    for j in range(8):
                        t = it * 8 + j
                        dve.bn_stats(st[:, ts(t, 6)], src[:, ts(t, C)]).then_inc(s_stats, 1)
                dve.wait_ge(s_stats, TILES)
                half = st[:, :].rearrange("p (t s) -> p s t", s=6)
                link = linker(dve, s_chain)
                link(dve.tensor_tensor(mean[:, :], half[:, 1, :], half[:, 4, :], ALU.add))
                link(dve.tensor_tensor(mdiff[:, :], half[:, 1, :], half[:, 4, :], ALU.subtract))
                link(dve.tensor_tensor(vsum[:, :], half[:, 2, :], half[:, 5, :], ALU.add))
                link(dve.tensor_tensor(mdiff[:, :], mdiff[:, :], mdiff[:, :], ALU.mult))
                link(dve.tensor_scalar(vsum[:, :], vsum[:, :], 1.0 / C, eps, ALU.mult, ALU.add))
                link(dve.scalar_tensor_tensor(out=var[:, :], in0=mdiff[:, :], scalar=0.25, in1=vsum[:, :],
                                              op0=ALU.mult, op1=ALU.add))
                link(dve.tensor_scalar(mean[:, :], mean[:, :], 0.5, None, ALU.mult))
                dve.wait_ge(s_std, 1)
                link(dve.reciprocal(rstd[:, :], std[:, :]))
                link(dve.tensor_tensor(std[:, :], rstd[:, :], rstd[:, :], ALU.mult))
                link(dve.tensor_tensor(std[:, :], std[:, :], var[:, :], ALU.mult))
                link(dve.tensor_scalar(std[:, :], std[:, :], -0.5, 1.5, ALU.mult, ALU.add))
                link(dve.tensor_tensor(rstd[:, :], rstd[:, :], std[:, :], ALU.mult))
                if store is not None:
                    with dve.Fori(0, TILES // 8) as it:
                        for j in range(8):
                            t = it * 8 + j
                            dve.tensor_scalar(store[:, ts(t, C)], src[:, ts(t, C)], mean[:, ts(t, 1)],
                                              rstd[:, ts(t, 1)], ALU.subtract, ALU.mult).then_inc(s_stored, 1)
                    dve.wait_ge(s_stored, TILES)
                else:
                    dve.sem_inc(s_turned, 2)
                    with dve.Fori(0, TILES // 8) as it:
                        for u in range(2):
                            dve.wait_ge(s_turned, it * 2 + (u + 1))
                            for j in range(4):
                                t = it * 8 + (4 * u + j)
                                dve.tensor_scalar(nrm[u][:, j * C:(j + 1) * C], src[:, ts(t, C)],
                                                  mean[:, ts(t, 1)], rstd[:, ts(t, 1)],
                                                  ALU.subtract, ALU.mult).then_inc(s_norm, 1)
                    if parts is not None:
                        xa_hi, xa_lo, xb = parts
                        with dve.Fori(0, TILES // 8) as it:
                            for u in range(2):
                                dve.wait_ge(s_evac, it * 4 + (2 * u + 6))
                                cols = ts(it * 2 + u, CHUNK)
                                dve.tensor_tensor(xa_lo[:, cols], turned_to[0][:, cols], xa_hi[:, cols],
                                                  ALU.subtract).then_inc(s_lo, 1)
                                dve.tensor_tensor(xb[C1:P, cols], turned_to[1][0:C1, cols], xb[0:C1, cols],
                                                  ALU.subtract).then_inc(s_lo, 1)
                        dve.wait_ge(s_lo, TILES // 2)

            @block.scalar
            def _(act):
                act.wait_ge(s_chain, 6)
                act.activation(std[:, :], var[:, :], ACT.Sqrt).then_inc(s_std, 1)
                if turned_to is None:
                    return
                with act.Fori(0, TILES // 8) as it:
                    for u in range(2):
                        act.wait_ge(s_turned, it * 2 + (u + 3))
                        cols = ts(it * 2 + u, CHUNK)
                        for k, (tile, n) in enumerate(((t0[u], C0), (t1[u], C1))):
                            scale = 1.0 if gain is None else gain[0:n, k:k + 1]
                            bias = 0.0 if shift is None else shift[0:n, k:k + 1]
                            act.activation(turned_to[k][0:n, cols], tile[0:n, :], ACT.Identity,
                                           bias=bias, scale=scale).then_inc(s_f32, 1)
                            if parts is not None:
                                act.activation(parts[2 * k][0:n, cols], tile[0:n, :], ACT.Identity,
                                               bias=bias, scale=scale).then_inc(s_hi, 1)
                        act.wait_ge(s_f32, it * 4 + (2 * u + 2))
                        if parts is not None:
                            act.wait_ge(s_hi, it * 4 + (2 * u + 2))
                        act.sem_inc(s_evac, 2)

            @block.tensor
            def _(pe):
                if turned_to is None:
                    return
                pe.sem_inc(s_evac, 4)
                with pe.Fori(0, TILES // 8) as it:
                    for u in range(2):
                        pe.wait_ge(s_norm, it * 8 + (4 * u + 4))
                        pe.wait_ge(s_evac, it * 4 + (2 * u + 2))
                        for j in range(4):
                            pe.transpose(t0[u][:, j * P:(j + 1) * P], nrm[u][:, j * C:j * C + C0], ident)
                            ins = pe.transpose(t1[u][0:C1, j * P:(j + 1) * P],
                                               nrm[u][:, j * C + C0:(j + 1) * C], ident)
                        ins.then_inc(s_turned, 1)


def qkv(nc, name, xt, vt, w, scratch):
    rel = "rel_h" in w
    with Pool(nc, name) as m:
        wqk = [m.sb("wqk0", 2 * C), m.sb("wqk1", 2 * C, parts=C1)]
        wv = [m.sb("wv0", C), m.sb("wv1", C, parts=C1)]
        bqk, bv, scale = m.sb("bqk", GROUPS), m.sb("bv", C), m.sb("scale", 1)
        qt = m.sb("qt", GROUPS * T)
        hi = [m.sb(f"hi{u}", L, F16) for u in range(2)]
        lo = [m.sb(f"lo{u}", L, F16) for u in range(2)]
        qp = [m.ps(f"qp{u}") for u in range(2)]
        vp = [m.ps(f"vp{u}") for u in range(2)]
        rp = [m.ps(f"rp{u}") for u in range(2)]
        s_w, s_tab, s_init, s_tabs = m.sem("w"), m.sem("tab"), m.sem("init"), m.sem("tabs")
        s_qk, s_qt, s_hi, s_lo = m.sem("qk"), m.sem("qt"), m.sem("hi"), m.sem("lo")
        s_st = [m.sem(f"st{u}") for u in range(2)]
        s_v, s_vt = m.sem("v"), m.sem("vt")
        s_rel, s_rhi, s_rlo = m.sem("rel"), m.sem("rhi"), m.sem("rlo")
        s_rst = [m.sem(f"rst{u}") for u in range(2)]
        if rel:
            raw = [m.sb(f"raw{k}", 2 * SIDE - 1, parts=GW) for k in range(2)]
            tab = [m.sb(f"tab{k}", (2 * SIDE - 1) * GH) for k in range(2)]
            own = m.sb("own", GH, parts=GW)
            rhi = [m.sb(f"rhi{k}", T, F16) for k in range(2)]
            rlo = [m.sb(f"rlo{k}", T, F16) for k in range(2)]
        vt4 = vt[:, :].rearrange("p (a k f) -> p a k f", a=PAIRS, k=KT)
        with nc.Block() as block:
            @block.sync
            def _(sp):
                sp.dma_start(wqk[0][:, :], w["wqk"][0:C0, :]).then_inc(s_w, 16)
                sp.dma_start(wqk[1][:, :], w["wqk"][C0:C, :]).then_inc(s_w, 16)
                sp.dma_start(bqk[:, :], w["bqk"]).then_inc(s_w, 16)
                sp.dma_start(wv[0][:, :], w["wv"][0:C0, :]).then_inc(s_w, 16)
                sp.dma_start(wv[1][:, :], w["wv"][C0:C, :]).then_inc(s_w, 16)
                sp.dma_start(bv[:, :], w["bv"].broadcast_to([P, C])).then_inc(s_w, 16)
                if rel:
                    for k, key in enumerate(("rel_h", "rel_w")):
                        for h in range(GH):
                            sp.dma_start(raw[k][h * HD:(h + 1) * HD, :], w[key]).then_inc(s_tab, 16)
                    sp.dma_start(own[:, :], w["own"]).then_inc(s_tab, 16)
                with sp.Fori(0, 2) as it:
                    for g2 in range(6):
                        u = g2 % 2
                        n = it * 12 + 2 * g2
                        sp.wait_ge(s_hi, n + 2)
                        sp.wait_ge(s_lo, n + 2)
                        row = (it * 6 + g2) * GH
                        for s in range(2):
                            for part, buf in enumerate((hi[u], lo[u])):
                                sp.dma_start(scratch["qk"][s, bass.ds(row, GH), part, :, :],
                                             buf[GW * s:GW * (s + 1), :]).then_inc(s_st[u], 16)
                if rel:
                    for g in range(GROUPS):
                        for k in range(2):
                            sp.wait_ge(s_rlo, g * 16 + (8 * k + 8 + 2))
                            for b in range(B):
                                for part, buf in enumerate((rhi[k], rlo[k])):
                                    rows = scratch["rel"][bass.ds(g * GH + b * NH, GH), part, 1 - k, :, :]
                                    sp.dma_start(rows.rearrange("h r n -> r h n"),
                                                 buf[:, b * L:(b + 1) * L]).then_inc(s_rst[k], 16)
                for u in range(2):
                    sp.wait_ge(s_st[u], 64 * 7)
                    if rel:
                        sp.wait_ge(s_rst[u], 128 * (GROUPS + 1))

            @block.gpsimd
            def _(pool):
                pool.memset(scale[0:GW, :], float(HD) ** -0.5).then_inc(s_init, 1)
                pool.memset(scale[GW:P, :], 1.0).then_inc(s_init, 1)
                with pool.Fori(0, 2) as it:
                    for g2 in range(6):
                        u = g2 % 2
                        pool.wait_ge(s_st[u], it * 192 + (g2 // 2 + 1) * 64)
                        for half in range(2):
                            n = it * 12 + (2 * g2 + half)
                            pool.wait_ge(s_hi, n + 1)
                            cols = bass.ds((it * 2 + g2 // 3) * L + ((g2 % 3) * T + half * CHUNK), CHUNK)
                            pool.tensor_tensor(lo[u][:, half * CHUNK:(half + 1) * CHUNK], qt[:, cols],
                                               hi[u][:, half * CHUNK:(half + 1) * CHUNK],
                                               ALU.subtract).then_inc(s_lo, 1)

            @block.tensor
            def _(pe):
                pe.wait_ge(s_w, 6 * 16)
                pe.sem_inc(s_qt, 2)
                with pe.Fori(0, 2) as it:
                    for g2 in range(6):
                        g = g2 % 3
                        for half in range(2):
                            n = it * 12 + (2 * g2 + half)
                            cols = bass.ds((it * 2 + g2 // 3) * L + half * CHUNK, CHUNK)
                            pe.wait_ge(s_qt, n + 1)
                            pe.matmul(qp[half][:, :], wqk[0][:, g * P:(g + 1) * P], xt[0][:, cols],
                                      start=True, stop=False)
                            pe.matmul(qp[half][:, :], wqk[1][:, g * P:(g + 1) * P], xt[1][0:C1, cols],
                                      start=False, stop=True).then_inc(s_qk, 1)
                for t in range(TILES):
                    if t >= 2:
                        pe.wait_ge(s_vt, t - 1)
                    pe.matmul(vp[t % 2][:, 0:C], xt[0][:, t * P:(t + 1) * P], wv[0][:, :], start=True, stop=False)
                    pe.matmul(vp[t % 2][:, 0:C], xt[1][0:C1, t * P:(t + 1) * P], wv[1][:, :],
                              start=False, stop=True).then_inc(s_v, 1)
                if not rel:
                    return
                pe.wait_ge(s_tabs, 4)
                pe.wait_ge(s_qt, 24 + 2)
                pe.sem_inc(s_rlo, 2)
                with pe.Fori(0, GROUPS) as g:
                    for k in range(2):
                        for qq in range(8):
                            pe.wait_ge(s_rlo, g * 16 + (8 * k + qq + 1))
                            for j in range(4):
                                r = 4 * qq + j
                                table = tab[k][:, (SIDE - 1 - r) * GH:(2 * SIDE - 1 - r) * GH]
                                q = qt[:, ts(g, T)]
                                if k == 0:
                                    q = q.rearrange("p (b r c) -> p r b c", b=B, r=SIDE)[:, r, :, :]
                                    out = rp[qq % 2][:, :].rearrange("p (b j c) -> p j b c", b=B, j=4)[:, j, :, :]
                                else:
                                    q = q.rearrange("p (n c) -> p c n", c=SIDE)[:, r, :]
                                    out = rp[qq % 2][:, j * P:(j + 1) * P]
                                ins = pe.matmul(out, table, q, start=True, stop=True)
                            ins.then_inc(s_rel, 1)

            @block.vector
            def _(dve):
                if rel:
                    dve.wait_ge(s_tab, 9 * 16)
                    for k in range(2):
                        dims = [GW, 2 * SIDE - 1, GH]
                        dve.memset(tab[k][GW:P, :], 0.0).then_inc(s_tabs, 1)
                        dve.tensor_tensor(tab[k][0:GW, :].rearrange("p (i h) -> p i h", h=GH),
                                          raw[k][:, :].unsqueeze(2).broadcast_to(dims),
                                          own[:, :].unsqueeze(1).broadcast_to(dims), ALU.mult).then_inc(s_tabs, 1)
                dve.wait_ge(s_w, 6 * 16)
                dve.wait_ge(s_init, 2)
                with dve.Fori(0, 2) as it:
                    for g2 in range(6):
                        for half in range(2):
                            n = it * 12 + (2 * g2 + half)
                            dve.wait_ge(s_qk, n + 1)
                            cols = bass.ds((it * 2 + g2 // 3) * L + ((g2 % 3) * T + half * CHUNK), CHUNK)
                            dve.tensor_scalar(qt[:, cols], qp[half][:, :], bqk[:, g2 % 3:g2 % 3 + 1],
                                              scale[:, 0:1], ALU.add, ALU.mult).then_inc(s_qt, 1)
                for t in range(TILES):
                    dve.wait_ge(s_v, t + 1)
                    b, kt = t // KT, t % KT
                    dve.tensor_tensor(vt4[:, NH // 2 * b:NH // 2 * (b + 1), kt, :],
                                      vp[t % 2][:, 0:C].rearrange("p (g f) -> p g f", f=2 * HD),
                                      bv[:, :].rearrange("p (g f) -> p g f", f=2 * HD),
                                      ALU.add).then_inc(s_vt, 1)
                dve.wait_ge(s_vt, TILES)
                if not rel:
                    return
                with dve.Fori(0, GROUPS) as g:
                    for k in range(2):
                        for qq in range(8):
                            n = g * 16 + (8 * k + qq)
                            dve.wait_ge(s_rhi, n + 1)
                            src, out, high = rel_views(rp[qq % 2], rlo[k], rhi[k], k, qq)
                            dve.tensor_tensor(out, src, high, ALU.subtract).then_inc(s_rlo, 1)

            @block.scalar
            def _(act):
                for u in range(2):
                    act.sem_inc(s_st[u], 64)
                with act.Fori(0, 2) as it:
                    for g2 in range(6):
                        u = g2 % 2
                        act.wait_ge(s_st[u], it * 192 + (g2 // 2 + 1) * 64)
                        act.wait_ge(s_lo, it * 12 + 2 * g2) if g2 else None
                        for half in range(2):
                            n = it * 12 + (2 * g2 + half)
                            act.wait_ge(s_qt, n + 3)
                            cols = bass.ds((it * 2 + g2 // 3) * L + ((g2 % 3) * T + half * CHUNK), CHUNK)
                            act.activation(hi[u][:, half * CHUNK:(half + 1) * CHUNK], qt[:, cols],
                                           ACT.Identity).then_inc(s_hi, 1)
                if not rel:
                    return
                for k in range(2):
                    act.sem_inc(s_rst[k], 128)
                with act.Fori(0, GROUPS) as g:
                    for k in range(2):
                        act.wait_ge(s_rst[k], g * 128 + 128)
                        for qq in range(8):
                            n = g * 16 + (8 * k + qq)
                            act.wait_ge(s_rel, n + 1)
                            src, out, _ = rel_views(rp[qq % 2], rhi[k], rhi[k], k, qq)
                            act.activation(out, src, ACT.Identity).then_inc(s_rhi, 1)


def rel_views(bank, part, high, k, qq):
    if k == 0:
        src = bank[:, :].rearrange("p (b x) -> p b x", b=B)
        where = [t[:, :].rearrange("p (b x) -> p b x", b=B)[:, :, qq * P:(qq + 1) * P] for t in (part, high)]
    else:
        src = bank[:, :].rearrange("p (j n) -> p j n", j=4)
        where = [t[:, :].rearrange("p (n c) -> p c n", c=SIDE)[:, 4 * qq:4 * qq + 4, :] for t in (part, high)]
    return src, where[0], where[1]


def attention(nc, name, vt, rel, scratch, hot, ident16):
    with Pool(nc, name) as m:
        qa = [m.sb(f"qa{u}", 2 * L, F16) for u in range(RING)]
        ka = [m.sb(f"ka{u}", 2 * L, F16) for u in range(RING)]
        vs = [m.sb(f"vs{u}", 2 * KT * 32) for u in range(RING)]
        osb = [m.sb(f"o{u}", CHUNK) for u in range(RING)]
        pr = [[m.sb(f"p{h}{k}", L) for k in range(2)] for h in range(2)]
        mx = m.sb("mx", 2 * KT * 2)
        m32, m16 = m.sb("m32", 2 * KT), m.sb("m16", 2 * KT, F16)
        if rel:
            qb = [m.sb(f"qb{u}", 2 * L, F16) for u in range(RING)]
            kb = m.sb("kb", L, F16)
        sps = [m.ps(f"s{h}", L) for h in range(2)]
        mps = [m.ps(f"m{k}") for k in range(2)]
        ops, rps = m.ps("o"), m.ps("r")
        s_const, s_ones = m.sem("const"), m.sem("ones")
        s_ld = [m.sem(f"ld{u}") for u in range(RING)]
        s_vs, s_mm, s_mx = m.sem("vs"), m.sem("maxprod"), m.sem("maxima")
        s_chain = m.sem("chain")
        s_m16, s_row, s_qm = m.sem("m16"), m.sem("maxrow"), m.sem("qamax")
        s_s, s_e, s_pv = m.sem("scores"), m.sem("exp"), m.sem("pv")
        s_o = m.sem("out")
        s_st = [m.sem(f"st{u}") for u in range(RING)]
        LOADS = 6 + (2 if rel else 0)
        MAXES = 2 * 2 * KT
        ONES = 2 * RING + (RING + 1 if rel else 2 * RING)

        def pairs(buf, a, z):
            return buf[a:z, :].rearrange("p (h n) -> p h n", h=2)

        def load(sp, pair, u):
            heads = bass.ds(pair * 2, 2)
            for s, part, buf, row in ((0, 0, qa, R_QK), (0, 0, qa, R_QK + HD), (0, 1, qa, R_LOW),
                                      (1, 0, ka, R_QK), (1, 1, ka, R_QK + HD), (1, 0, ka, R_LOW)):
                sp.dma_start(pairs(buf[u], row, row + HD),
                             scratch["qk"][s, heads, part, :, :].rearrange("h r n -> r h n")).then_inc(s_ld[u], 16)
            if rel:
                for part, buf in enumerate((qa, qb)):
                    sp.dma_start(pairs(buf[u], R_REL, R_QK),
                                 scratch["rel"][heads, part].rearrange("h k r n -> (k r) h n")).then_inc(s_ld[u], 16)

        def max_product(pe, pair, u, n):
            h, qi, c = n // 16, n // 2 % 8, n % 2
            qcol = slice(h * L + qi * P, h * L + (qi + 1) * P)
            kcol = slice(h * L + c * CHUNK, h * L + (c + 1) * CHUNK)
            if not (isinstance(pair, int) and pair == 0 and n < 2):
                pe.wait_ge(s_mx, pair * MAXES + (n - 1))
            pe.matmul(mps[n % 2][:, :], qa[u][0:R_MAX, qcol], ka[u][0:R_MAX, kcol],
                      start=True, stop=True).then_inc(s_mm, 1)

        def max_row(pe, pair, h):
            pe.wait_ge(s_m16, pair * 2 + (h + 1))
            if not (isinstance(pair, int) and pair == 0 and h == 0):
                pe.wait_ge(s_qm, pair * 2 + h)
            for j in range(KT):
                half = j // 4
                ins = pe.matmul(rps[32 * half:32 * half + 1, (j % 4) * P:(j % 4 + 1) * P],
                                m16[:, h * KT + j:h * KT + j + 1], ident16, start=True, stop=True)
            ins.then_inc(s_row, 1)

        def score(pe, pair, u, h, kt, first=False):
            if kt == 0:
                pe.wait_ge(s_qm, pair * 2 + (h + 1))
            if not first:
                pe.wait_ge(s_e, pair * 16 + (2 * kt + h - 1))
            kcol = slice(h * L + kt * P, h * L + (kt + 1) * P)
            for c in range(2):
                qcol = slice(h * L + c * CHUNK, h * L + (c + 1) * CHUNK)
                ins = pe.matmul(sps[h][:, c * CHUNK:(c + 1) * CHUNK], ka[u][0:R_END, kcol], qa[u][0:R_END, qcol],
                                start=True, stop=not rel)
            if rel:
                for c in range(2):
                    qcol = slice(h * L + c * CHUNK, h * L + (c + 1) * CHUNK)
                    ins = pe.matmul(sps[h][:, c * CHUNK:(c + 1) * CHUNK], kb[:, kt * P:(kt + 1) * P],
                                    qb[u][:, qcol], start=False, stop=True)
            ins.then_inc(s_s, 1)

        def weigh(pe, pair, u, kt):
            pe.wait_ge(s_e, pair * 16 + (2 * kt + 2))
            if kt == 0:
                pe.wait_ge(s_vs, pair * 2 + 2)
                pe.wait_ge(s_o, pair + 1)
            for h in range(2):
                for c in range(2):
                    row = 32 * (2 * h + c)
                    ins = pe.matmul(ops[row:row + 32, :], vs[u][:, (h * KT + kt) * 32:(h * KT + kt + 1) * 32],
                                    pr[h][kt % 2][:, c * CHUNK:(c + 1) * CHUNK], start=kt == 0, stop=kt == KT - 1)
            ins.then_inc(s_pv, 1)

        PLAN = [(2, 0, 0)] + 6 * [(1, 2, 2)] + [(0, 0, 0)]
        ROW0, ROW1 = 5, 7
        assert sum(map(sum, PLAN)) == MAXES

        def pe_pair(pe, turn, pair, u, last):
            n, v = 0, (u + 1) % RING

            def maxima(count):
                nonlocal n
                for _ in range(0 if last else count):
                    max_product(pe, pair + 1, v, n)
                    n += 1

            if not last:
                pe.wait_ge(s_ld[v], (turn + (2 if v == 0 else 1)) * (16 * LOADS))
            for kt in range(KT):
                if kt:
                    score(pe, pair, u, 0, kt)
                maxima(PLAN[kt][0])
                if kt:
                    score(pe, pair, u, 1, kt)
                maxima(PLAN[kt][1])
                if kt:
                    weigh(pe, pair, u, kt - 1)
                maxima(PLAN[kt][2])
                if not last and kt == ROW0:
                    max_row(pe, pair + 1, 0)
                if not last and kt == ROW1:
                    score(pe, pair + 1, v, 0, 0)
                    max_row(pe, pair + 1, 1)
            weigh(pe, pair, u, KT - 1)
            if not last:
                score(pe, pair + 1, v, 1, 0)

        def dve_max(dve, pair, n):
            dve.wait_ge(s_mm, pair * MAXES + (n + 1))
            dve.tensor_reduce(mx[:, n:n + 1], mps[n % 2][:, :], AX.X, ALU.max).then_inc(s_mx, 1)

        def dve_m16(dve, pair, h):
            dve.wait_ge(s_mx, pair * MAXES + (16 * h + 16))
            dve.tensor_reduce(m32[:, h * KT:(h + 1) * KT],
                              mx[:, 16 * h:16 * h + 16].rearrange("p (q c) -> p q c", c=2),
                              AX.X, ALU.max).then_inc(s_chain, 1)
            dve.wait_ge(s_chain, pair * 2 + (h + 1))
            dve.tensor_scalar(m16[:, h * KT:(h + 1) * KT], m32[:, h * KT:(h + 1) * KT], -1.0, None,
                              ALU.mult).then_inc(s_m16, 1)

        def dve_row(dve, pair, u, h):
            dve.wait_ge(s_row, pair * 2 + (h + 1))
            for half in range(2):
                ins = dve.tensor_copy(qa[u][R_MAX:R_MAX + 1, h * L + half * CHUNK:h * L + (half + 1) * CHUNK],
                                      rps[32 * half:32 * half + 1, :])
            ins.then_inc(s_qm, 1)

        def dve_pair(dve, turn, pair, u, last):
            if not last:
                n, v = 0, (u + 1) % RING
                for kt in range(KT):
                    for _ in range(sum(PLAN[kt])):
                        dve_max(dve, pair + 1, n)
                        n += 1
                        if n % 16 == 0:
                            dve_m16(dve, pair + 1, n // 16 - 1)
                    if kt == ROW0:
                        dve_row(dve, pair + 1, v, 0)
                dve_row(dve, pair + 1, v, 1)
            dve.wait_ge(s_pv, pair * KT + KT)
            dve.wait_ge(s_st[u], (turn + 1) * 16)
            dve.tensor_copy(osb[u][:, :], ops[:, :]).then_inc(s_o, 1)

        def stage_values(pool, pair, u):
            src = vt[:, ts(pair, KT * 2 * HD)].rearrange("p (k f) -> p k f", k=KT)
            for h in range(2):
                dst = vs[u][:, h * KT * 32:(h + 1) * KT * 32].rearrange("p (k f) -> p k f", k=KT)
                pool.tensor_copy(dst[:, :, 0:HD], src[:, :, h * HD:(h + 1) * HD]).then_inc(s_vs, 1)

        LAST = PAIRS // RING - 1
        with nc.Block() as block:
            @block.sync
            def _(sp):
                if rel:
                    for u in range(RING):
                        for h in range(2):
                            sp.dma_start(ka[u][R_REL:R_QK, h * L:(h + 1) * L], hot).then_inc(s_const, 16)
                    sp.dma_start(kb[R_REL:R_QK, :], hot).then_inc(s_const, 16)
                for u in range(RING):
                    load(sp, u, u)
                with sp.Fori(1, PAIRS // RING) as it:
                    for u in range(RING):
                        sp.wait_ge(s_s, it * (16 * RING) + 16 * (u + 1 - RING))
                        load(sp, it * RING + u, u)

            @block.gpsimd
            def _(pool):
                for u in range(RING):
                    stage_values(pool, u, u)
                with pool.Fori(1, PAIRS // RING) as it:
                    for u in range(RING):
                        pool.wait_ge(s_pv, it * (KT * RING) + KT * (u + 1 - RING))
                        stage_values(pool, it * RING + u, u)

            @block.tensor
            def _(pe):
                if rel:
                    pe.wait_ge(s_const, (2 * RING + 1) * 16)
                pe.wait_ge(s_ones, ONES)
                pe.wait_ge(s_ld[0], 16 * LOADS)
                for n in range(MAXES):
                    max_product(pe, 0, 0, n)
                    if n == 20:
                        max_row(pe, 0, 0)
                score(pe, 0, 0, 0, 0, first=True)
                max_row(pe, 0, 1)
                score(pe, 0, 0, 1, 0, first=True)
                with pe.Fori(0, LAST) as it:
                    for u in range(RING):
                        pe_pair(pe, it, it * RING + u, u, False)
                for u in range(RING):
                    pe_pair(pe, LAST, LAST * RING + u, u, u == RING - 1)

            @block.vector
            def _(dve):
                for u in range(RING):
                    ones = vs[u][:, :].rearrange("p (k f) -> p k f", f=32)
                    dve.memset(ones[:, :, HD:32], 1.0).then_inc(s_ones, 1)
                    dve.memset(ka[u][R_MAX:R_MAX + 1, :], 1.0).then_inc(s_ones, 1)
                    if rel:
                        dve.memset(qb[u][R_QK:P, :], 0.0).then_inc(s_ones, 1)
                    else:
                        for buf in (qa, ka):
                            dve.memset(buf[u][R_REL:R_QK, :], 0.0).then_inc(s_ones, 1)
                if rel:
                    dve.memset(kb[R_QK:P, :], 0.0).then_inc(s_ones, 1)
                for u in range(RING):
                    dve.sem_inc(s_st[u], 16)
                dve.sem_inc(s_o, 1)
                for n in range(MAXES):
                    dve_max(dve, 0, n)
                    if n == 15:
                        dve_m16(dve, 0, 0)
                    if n == 20:
                        dve_row(dve, 0, 0, 0)
                dve_m16(dve, 0, 1)
                dve_row(dve, 0, 0, 1)
                with dve.Fori(0, LAST) as it:
                    for u in range(RING):
                        dve_pair(dve, it, it * RING + u, u, False)
                for u in range(RING):
                    dve_pair(dve, LAST, LAST * RING + u, u, u == RING - 1)

            @block.scalar
            def _(act):
                def store(pair, u):
                    act.wait_ge(s_o, pair + 2)
                    act.dma_start(scratch["o"][bass.ds(pair, 1)].rearrange("a p n -> (a p) n"),
                                  osb[u][:, :]).then_inc(s_st[u], 16)

                def exps(pair, u, kts):
                    for kt in kts:
                        for h in range(2):
                            act.wait_ge(s_s, pair * 16 + (2 * kt + h + 1))
                            if kt >= 2:
                                act.wait_ge(s_pv, pair * KT + (kt - 1))
                            act.activation(pr[h][kt % 2][:, :], sps[h][:, :], ACT.Exp).then_inc(s_e, 1)

                exps(0, 0, range(KT))
                exps(1, 1, range(2))
                store(0, 0)
                exps(1, 1, range(2, KT))
                exps(2, 2, range(2))
                store(1, 1)
                exps(2, 2, range(2, KT))
                with act.Fori(1, PAIRS // RING) as it:
                    for u in range(RING):
                        pair = it * RING + u
                        exps(pair, u, range(2))
                        store(pair - 1, (u - 1) % RING)
                        exps(pair, u, range(2, KT))
                store(PAIRS - 1, RING - 1)
                for u in range(RING):
                    act.wait_ge(s_st[u], 16 * (PAIRS // RING + 1))


def project(nc, name, res, w, b, scratch):
    with Pool(nc, name) as m:
        z = m.sb("z", CHUNK)
        rz = m.sb("rz", CHUNK)
        pw = [m.sb("pw0", C), m.sb("pw1", C, parts=C1)]
        bias = m.sb("bias", C)
        num = [[m.sb(f"num{k}{u}", CHUNK, parts=(C0, C1)[k]) for k in range(2)] for u in range(2)]
        inv = [[m.sb(f"inv{k}{u}", CHUNK, parts=(C0, C1)[k]) for k in range(2)] for u in range(2)]
        yp = [m.ps(f"y{u}") for u in range(2)]
        s_w, s_z, s_rz, s_rzst = m.sem("w"), m.sem("z"), m.sem("rz"), m.sem("rzst")
        s_ld = [m.sem(f"ld{u}") for u in range(2)]
        s_at, s_y, s_add, s_bias, s_used = m.sem("at"), m.sem("y"), m.sem("add"), m.sem("bias"), m.sem("used")
        zrows = scratch["o"].rearrange("a (s r) n -> (a s) r n", r=32)[:, HD, :]
        heads = scratch["o"].rearrange("a (h c r) n -> (a h) c r n", h=2, c=2)
        zheads = scratch["rz"].rearrange("(h c) n -> h c n", c=2)
        with nc.Block() as block:
            @block.sync
            def _(sp):
                sp.dma_start(z[0:2 * B * NH, :], zrows).then_inc(s_z, 16)
                sp.dma_start(pw[0][:, :], w[0:C0, :]).then_inc(s_w, 16)
                sp.dma_start(pw[1][:, :], w[C0:C, :]).then_inc(s_w, 16)
                sp.dma_start(bias[:, :], b.broadcast_to([P, C])).then_inc(s_w, 16)
                sp.wait_ge(s_rz, 1)
                sp.dma_start(scratch["rz"], rz[0:2 * B * NH, :]).then_inc(s_rzst, 16)
                sp.wait_ge(s_rzst, 16)
                sp.sem_inc(s_used, 8)
                with sp.Fori(0, B) as bt:
                    for u in range(2):
                        sp.wait_ge(s_used, bt * 8 + (4 * u + 4))
                        for k, (h0, n) in enumerate(((0, 8), (8, 4))):
                            rows = bass.ds(bt * NH + h0, n)
                            sp.dma_start(num[u][k][:, :], heads[rows, u, 0:HD, :]).then_inc(s_ld[u], 16)
                            sp.dma_start(inv[u][k][:, :],
                                         zheads[rows, u, :].unsqueeze(1).broadcast_to([n, HD, CHUNK])
                                         ).then_inc(s_ld[u], 16)

            @block.vector
            def _(dve):
                dve.wait_ge(s_z, 16)
                dve.reciprocal(rz[0:2 * B * NH, :], z[0:2 * B * NH, :]).then_inc(s_rz, 1)
                dve.wait_ge(s_w, 3 * 16)
                dve.tensor_tensor(res[:, :].rearrange("p (t f) -> p t f", t=TILES),
                                  res[:, :].rearrange("p (t f) -> p t f", t=TILES),
                                  bias[:, :].unsqueeze(1).broadcast_to([P, TILES, C]), ALU.add).then_inc(s_bias, 1)
                dve.wait_ge(s_bias, 1)
                with dve.Fori(0, B) as bt:
                    for u in range(2):
                        dve.wait_ge(s_ld[u], bt * 64 + 64)
                        for k in range(2):
                            dve.tensor_tensor(num[u][k][:, :], num[u][k][:, :], inv[u][k][:, :],
                                              ALU.mult).then_inc(s_at, 1)
                        for t in range(4):
                            n = bt * 8 + (4 * u + t)
                            dve.wait_ge(s_y, n + 1)
                            dve.tensor_tensor(res[:, ts(n, C)], res[:, ts(n, C)], yp[t % 2][:, 0:C],
                                              ALU.add).then_inc(s_add, 1)

            @block.tensor
            def _(pe):
                pe.wait_ge(s_w, 3 * 16)
                pe.sem_inc(s_add, 2)
                with pe.Fori(0, B) as bt:
                    for u in range(2):
                        pe.wait_ge(s_at, bt * 4 + (2 * u + 2))
                        for t in range(4):
                            n = bt * 8 + (4 * u + t)
                            pe.wait_ge(s_add, n + 1)
                            for k in range(2):
                                ins = pe.matmul(yp[t % 2][:, 0:C], num[u][k][:, t * P:(t + 1) * P], pw[k][:, :],
                                                start=k == 0, stop=k == 1)
                            ins.then_inc(s_y, 1)

            @block.scalar
            def _(act):
                with act.Fori(0, TILES) as n:
                    act.wait_ge(s_y, n + 1)
                    act.sem_inc(s_used, 1)


def gates(nc, name, xt, gate_w, experts, comb, iota, gate_b=None, add_bias=None):
    E8 = 8
    with Pool(nc, name) as m:
        gw = [m.sb("gw0", experts), m.sb("gw1", experts, parts=C1)]
        lg, top, idxf, pick = (m.sb(n, TILES * E8) for n in ("logits", "top", "idxf", "pick"))
        idx = m.sb("idx", TILES * E8, U32)
        one, w0, w1 = (m.sb(n, TILES) for n in ("one", "w0", "w1"))
        gb, lp = m.sb("gb", experts), m.ps("lp")
        s_w, s_l, s_chain, s_exp, s_x = m.sem("w"), m.sem("l"), m.sem("chain"), m.sem("exp"), m.sem("x")
        s_acc, s_top = m.sem("acc"), m.sem("top")
        b2 = m.sb("b2", experts * C) if add_bias else None

        def cube(t):
            return t[:, :].rearrange("p (t e) -> p t e", e=E8)

        def wide(t):
            return t[:, :].unsqueeze(2).broadcast_to([P, TILES, E8])

        loads = 2 + (gate_b is not None) + (add_bias is not None)
        with nc.Block() as block:
            @block.sync
            def _(sp):
                sp.dma_start(gw[0][:, :], gate_w[0:C0, :]).then_inc(s_w, 16)
                sp.dma_start(gw[1][:, :], gate_w[C0:C, :]).then_inc(s_w, 16)
                if gate_b is not None:
                    sp.dma_start(gb[:, :], gate_b.broadcast_to([P, experts])).then_inc(s_w, 16)
                if add_bias is not None:
                    sp.dma_start(b2[:, :], add_bias[1].broadcast_to([P, experts * C])).then_inc(s_w, 16)

            @block.tensor
            def _(pe):
                pe.wait_ge(s_w, loads * 16)
                for t in range(TILES):
                    for k, n in enumerate((C0, C1)):
                        ins = pe.matmul(lp[:, t * E8:t * E8 + experts], xt[k][0:n, t * P:(t + 1) * P], gw[k][:, :],
                                        start=k == 0, stop=k == 1)
                ins.then_inc(s_l, 1)

            @block.vector
            def _(dve):
                link = linker(dve, s_chain)
                dve.wait_ge(s_w, loads * 16)
                dve.wait_ge(s_l, 1)
                psum = lp[:, 0:TILES * E8].rearrange("p (t e) -> p t e", e=E8)[:, :, 0:experts]
                if gate_b is None:
                    link(dve.tensor_copy(cube(lg), psum))
                    link(dve.tensor_reduce(one[:, :], cube(lg), AX.X, ALU.max))
                    link(dve.tensor_tensor(cube(lg), cube(lg), wide(one), ALU.subtract))
                    dve.sem_inc(s_x, 1)
                    dve.wait_ge(s_exp, 1)
                    link(dve.tensor_reduce(one[:, :], cube(lg), AX.X, ALU.add))
                    link(dve.reciprocal(one[:, :], one[:, :]))
                    link(dve.tensor_tensor(cube(lg), cube(lg), wide(one), ALU.mult))
                else:
                    link(dve.memset(lg[:, :], -3.0e38))
                    link(dve.tensor_tensor(cube(lg)[:, :, 0:experts], psum,
                                           gb[:, :].unsqueeze(1).broadcast_to([P, TILES, experts]), ALU.add))
                for t in range(TILES):
                    cols = slice(t * E8, (t + 1) * E8)
                    dve.max(out=top[:, cols], in_=lg[:, cols]).then_inc(s_top, 1)
                dve.wait_ge(s_top, TILES)
                for t in range(TILES):
                    cols = slice(t * E8, (t + 1) * E8)
                    dve.max_index(idx[:, cols], top[:, cols], lg[:, cols]).then_inc(s_top, 1)
                dve.wait_ge(s_top, 2 * TILES)
                first, second = cube(top)[:, :, 0], cube(top)[:, :, 1]
                if gate_b is None:
                    link(dve.tensor_tensor(one[:, :], first, second, ALU.add))
                    link(dve.tensor_scalar(one[:, :], one[:, :], 1e-8, None, ALU.add))
                    link(dve.reciprocal(one[:, :], one[:, :]))
                    link(dve.tensor_tensor(w0[:, :], first, one[:, :], ALU.mult))
                    link(dve.tensor_tensor(w1[:, :], second, one[:, :], ALU.mult))
                else:
                    link(dve.tensor_tensor(w1[:, :], second, first, ALU.subtract))
                    dve.sem_inc(s_x, 1)
                    dve.wait_ge(s_exp, 1)
                    link(dve.tensor_scalar(one[:, :], w1[:, :], 1.0, None, ALU.add))
                    link(dve.reciprocal(w0[:, :], one[:, :]))
                    link(dve.tensor_tensor(w1[:, :], w1[:, :], w0[:, :], ALU.mult))
                link(dve.tensor_copy(idxf[:, :], idx[:, :]))
                experts_of = iota.unsqueeze(1).broadcast_to([P, TILES, E8])
                for k, wk in enumerate((w0, w1)):
                    dst = comb if k == 0 else pick
                    which = cube(idxf)[:, :, k:k + 1].broadcast_to([P, TILES, E8])
                    link(dve.tensor_tensor(cube(dst), experts_of, which, ALU.is_equal))
                    link(dve.tensor_tensor(cube(dst), cube(dst), wide(wk), ALU.mult))
                link(dve.tensor_tensor(comb[:, :], comb[:, :], pick[:, :], ALU.add))
                if add_bias is not None:
                    res = add_bias[0]
                    dve.sem_inc(s_acc, 8)
                    with dve.Fori(0, TILES // 8) as it:
                        for e in range(experts):
                            dve.wait_ge(s_acc, it * (8 * experts) + (8 * e + 8))
                            for j in range(8):
                                t = it * 8 + j
                                dve.scalar_tensor_tensor(out=res[:, ts(t, C)], in0=b2[:, e * C:(e + 1) * C],
                                                         scalar=comb[:, bass.ds(t * E8 + e, 1)],
                                                         in1=res[:, ts(t, C)],
                                                         op0=ALU.mult, op1=ALU.add).then_inc(s_acc, 1)
                    dve.wait_ge(s_acc, TILES * experts + 8)

            @block.scalar
            def _(act):
                act.wait_ge(s_x, 1)
                src = lg if gate_b is None else w1
                act.activation(src[:, :], src[:, :], ACT.Exp).then_inc(s_exp, 1)


W_SCALE = 64.0


def feed_forward(nc, name, parts, res, blocks, mt, w_up, w_down, gate_bank=None, b_up=None, comb=None,
                 b_down=None):
    gated = gate_bank is not None
    per_turn = 1 if blocks % 2 == 0 else 2
    turns = T // CHUNK // per_turn
    ring = 2 if gated else 4
    mats = (gate_bank, w_up) if gated else (w_up,)
    nm = len(mats)
    bw = mt * P
    hid = blocks * bw
    xa_hi, xa_lo, xb = parts
    assert per_turn * blocks * mt % ring == 0
    with Pool(nc, name) as m:
        ah = [m.sb(f"ah{i}", hid, F16) for i in range(nm)]
        al = [m.sb(f"al{i}", hid, F16) for i in range(nm)]
        bh = [m.sb(f"bh{i}", hid, F16) for i in range(nm)]
        bl = [m.sb(f"bl{i}", hid, F16, parts=C1) for i in range(nm)]
        raw_a = [[m.sb(f"ra{i}{r}", bw) for i in range(nm)] for r in range(2)]
        raw_b = [[m.sb(f"rb{i}{r}", bw) for i in range(nm)] for r in range(2)]
        down = m.sb("down", blocks * mt * C)
        bu = m.sb("bu", blocks * mt) if b_up is not None else None
        bd = m.sb("bd", C) if b_down is not None else None
        h = [m.sb(f"h{u}", mt * CHUNK) for u in range(2)]
        s_buf = [m.sb(f"s{u}", CHUNK) for u in range(2)] if gated else None
        ups = [[m.ps(f"u{i}{k}") for i in range(nm)] for k in range(ring)]
        yps = [[m.ps(f"y{u}{k}") for k in range(2)] for u in range(2)]
        s_raw = [m.sem(f"raw{r}") for r in range(2)]
        s_wh, s_wl, s_b, s_wd = m.sem("wh"), m.sem("wl"), m.sem("b"), m.sem("wd")
        s_up, s_s, s_h = m.sem("up"), m.sem("s"), m.sem("h")
        s_down, s_y, s_bias = m.sem("down"), m.sem("y"), m.sem("bias")
        n_b = (b_up is not None) + (b_down is not None)

        def unit(it, c, blk, k):
            return it * (per_turn * blocks * mt) + ((c * blocks + blk) * mt + k)

        def block_no(it, c, blk):
            return it * (per_turn * blocks) + (c * blocks + blk)

        def cut(blk):
            return slice(blk * bw, (blk + 1) * bw)

        with nc.Block() as block:
            @block.sync
            def _(sp):
                if b_up is not None:
                    sp.dma_start(bu[:, :], b_up).then_inc(s_b, 16)
                if b_down is not None:
                    sp.dma_start(bd[:, :], b_down.broadcast_to([P, C])).then_inc(s_b, 16)
                for blk in range(blocks):
                    r = blk % 2
                    if blk >= 2:
                        sp.wait_ge(s_wl, 2 * nm * (blk - 1))
                    for i, src in enumerate(mats):
                        sp.dma_start(raw_a[r][i][:, :], src[0:C0, cut(blk)]).then_inc(s_raw[r], 16)
                        for half in range(2):
                            sp.dma_start(raw_b[r][i][C1 * half:C1 * (half + 1), :],
                                         src[C0:C, cut(blk)]).then_inc(s_raw[r], 16)
                    sp.dma_start(down[:, blk * mt * C:(blk + 1) * mt * C].rearrange("p (k n) -> p k n", n=C),
                                 w_down[cut(blk), :].rearrange("(k p) n -> p k n", p=P)).then_inc(s_wd, 16)

            def run(engine, turn_of):
                turn_of(0, True)
                with engine.Fori(1, turns) as it:
                    turn_of(it, False)

            @block.tensor
            def _(pe):
                def rise(it, c, blk, first):
                    cols = ts(it * per_turn + c, CHUNK)
                    if first and c == 0:
                        pe.wait_ge(s_wl, 2 * nm * (blk + 1))
                    for k in range(mt):
                        pe.wait_ge(s_h, unit(it, c, blk, k) + 1)
                        n = (c * blocks + blk) * mt + k
                        w = slice((blk * mt + k) * P, (blk * mt + k + 1) * P)
                        for i in range(nm):
                            bank = ups[n % ring][i][:, :]
                            pe.matmul(bank, ah[i][:, w], xa_hi[:, cols], start=True, stop=False)
                            pe.matmul(bank, al[i][:, w], xa_hi[:, cols], start=False, stop=False)
                            pe.matmul(bank, ah[i][:, w], xa_lo[:, cols], start=False, stop=False)
                            pe.matmul(bank, bh[i][:, w], xb[:, cols], start=False, stop=False)
                            ins = pe.matmul(bank, bl[i][:, w], xb[0:C1, cols], start=False, stop=True)
                        ins.then_inc(s_up, 1)

                def fall(it, c, blk, first):
                    q = c * blocks + blk
                    if first and c == 0:
                        pe.wait_ge(s_wd, 16 * (blk + 1))
                    pe.wait_ge(s_h, unit(it, c, blk, mt - 1) + (1 + ring))
                    pe.wait_ge(s_y, block_no(it, c, blk) + 1)
                    for t in range(4):
                        for k in range(mt):
                            ins = pe.matmul(yps[q % 2][t // 2][:, (t % 2) * C:(t % 2 + 1) * C],
                                            h[q % 2][:, k * CHUNK + t * P:k * CHUNK + (t + 1) * P],
                                            down[:, (blk * mt + k) * C:(blk * mt + k + 1) * C],
                                            start=k == 0, stop=k == mt - 1)
                    ins.then_inc(s_down, 1)

                def one_turn(it, first):
                    last = None
                    for c in range(per_turn):
                        for blk in range(blocks):
                            rise(it, c, blk, first)
                            if last is not None:
                                fall(it, *last, first)
                            last = (c, blk)
                    fall(it, *last, first)

                pe.sem_inc(s_h, ring)
                pe.sem_inc(s_y, 2)
                run(pe, one_turn)

            @block.scalar
            def _(act):
                def split_high(blk):
                    act.wait_ge(s_raw[blk % 2], 16 * 3 * nm * (blk // 2 + 1))
                    for i in range(nm):
                        for raw, high in ((raw_a, ah), (raw_b, bh)):
                            act.activation(high[i][:, cut(blk)], raw[blk % 2][i][:, :], ACT.Identity,
                                           scale=W_SCALE).then_inc(s_wh, 1)

                def one_turn(it, first):
                    for c in range(per_turn):
                        for blk in range(blocks):
                            if first and c == 0 and blk + 1 < blocks:
                                split_high(blk + 1)
                            q = c * blocks + blk
                            if not gated:
                                act.wait_ge(s_down, block_no(it, c, blk) + 1)
                            for k in range(mt):
                                n = unit(it, c, blk, k)
                                i = q * mt + k
                                act.wait_ge(s_up, n + 1)
                                if gated:
                                    act.wait_ge(s_h, n + 1)
                                    act.activation(s_buf[i % 2][:, :], ups[i % ring][0][:, :],
                                                   ACT.Silu, scale=1.0 / W_SCALE).then_inc(s_s, 1)
                                else:
                                    act.activation(h[q % 2][:, k * CHUNK:(k + 1) * CHUNK], ups[i % ring][0][:, :],
                                                   ACT.Gelu, bias=bu[:, blk * mt + k:blk * mt + k + 1],
                                                   scale=1.0 / W_SCALE).then_inc(s_h, 1)

                split_high(0)
                if n_b:
                    act.wait_ge(s_b, n_b * 16)
                if not gated:
                    act.sem_inc(s_down, 2)
                run(act, one_turn)

            @block.vector
            def _(dve):
                def split_low(blk):
                    dve.wait_ge(s_wh, 2 * nm * (blk + 1))
                    for i in range(nm):
                        for raw, high, low, n in ((raw_a, ah, al, P), (raw_b, bh, bl, C1)):
                            dve.scalar_tensor_tensor(out=low[i][0:n, cut(blk)], in0=raw[blk % 2][i][0:n, :],
                                                     scalar=W_SCALE, in1=high[i][0:n, cut(blk)],
                                                     op0=ALU.mult, op1=ALU.subtract).then_inc(s_wl, 1)

                def collect(it, c, blk):
                    q = c * blocks + blk
                    dve.wait_ge(s_down, block_no(it, c, blk) + 3)
                    dve.wait_ge(s_y, block_no(it, c, blk) + 2)
                    for t in range(4):
                        tile = (it * per_turn + c) * 4 + t
                        y = yps[q % 2][t // 2][:, (t % 2) * C:(t % 2 + 1) * C]
                        dst = res[:, ts(tile, C)]
                        if comb is None:
                            ins = dve.tensor_tensor(dst, y, dst, ALU.add)
                        else:
                            ins = dve.scalar_tensor_tensor(out=dst, in0=y, scalar=comb[:, bass.ds(tile * 8 + blk, 1)],
                                                           in1=dst, op0=ALU.mult, op1=ALU.add)
                    ins.then_inc(s_y, 1)

                def one_turn(it, first):
                    last = None
                    for c in range(per_turn):
                        for blk in range(blocks):
                            if first and c == 0 and blk + 1 < blocks:
                                split_low(blk + 1)
                            q = c * blocks + blk
                            if gated:
                                dve.wait_ge(s_down, block_no(it, c, blk) + 1)
                                for k in range(mt):
                                    n = unit(it, c, blk, k)
                                    i = q * mt + k
                                    dve.wait_ge(s_s, n + 1)
                                    dve.scalar_tensor_tensor(out=h[q % 2][:, k * CHUNK:(k + 1) * CHUNK],
                                                             in0=ups[i % ring][1][:, :], scalar=1.0 / W_SCALE,
                                                             in1=s_buf[i % 2][:, :],
                                                             op0=ALU.mult, op1=ALU.mult).then_inc(s_h, 1)
                            if last is not None:
                                collect(it, *last)
                            last = (c, blk)
                    collect(it, *last)

                split_low(0)
                if bd is not None:
                    dve.wait_ge(s_b, n_b * 16)
                    dve.tensor_tensor(res[:, :].rearrange("p (t f) -> p t f", t=TILES),
                                      res[:, :].rearrange("p (t f) -> p t f", t=TILES),
                                      bd[:, :].unsqueeze(1).broadcast_to([P, TILES, C]), ALU.add).then_inc(s_bias, 1)
                    dve.wait_ge(s_bias, 1)
                if gated:
                    dve.sem_inc(s_down, 2)
                run(dve, one_turn)
                dve.wait_ge(s_y, T // CHUNK * blocks + 2)


def turn(nc, name, src, parts, ident):
    xa_hi, xa_lo, xb = parts
    with Pool(nc, name) as m:
        t0 = [m.ps(f"t0{u}") for u in range(2)]
        t1 = [m.ps(f"t1{u}") for u in range(2)]
        s_t, s_hi, s_lo = m.sem("turned"), m.sem("hi"), m.sem("lo")
        with nc.Block() as block:
            @block.tensor
            def _(pe):
                for n in range(TILES // 4):
                    if n >= 2:
                        pe.wait_ge(s_lo, 2 * n - 2)
                    for j in range(4):
                        t = 4 * n + j
                        pe.transpose(t0[n % 2][:, j * P:(j + 1) * P], src[:, t * C:t * C + C0], ident)
                        ins = pe.transpose(t1[n % 2][0:C1, j * P:(j + 1) * P], src[:, t * C + C0:(t + 1) * C], ident)
                    ins.then_inc(s_t, 1)

            @block.scalar
            def _(act):
                for n in range(TILES // 4):
                    act.wait_ge(s_t, n + 1)
                    cols = slice(n * CHUNK, (n + 1) * CHUNK)
                    act.activation(xa_hi[:, cols], t0[n % 2][:, :], ACT.Identity).then_inc(s_hi, 1)
                    act.activation(xb[0:C1, cols], t1[n % 2][0:C1, :], ACT.Identity).then_inc(s_hi, 1)

            @block.vector
            def _(dve):
                for n in range(TILES // 4):
                    cols = slice(n * CHUNK, (n + 1) * CHUNK)
                    dve.wait_ge(s_hi, 2 * n + 2)
                    dve.tensor_tensor(xa_lo[:, cols], t0[n % 2][:, :], xa_hi[:, cols], ALU.subtract).then_inc(s_lo, 1)
                    dve.tensor_tensor(xb[C1:P, cols], t1[n % 2][0:C1, :], xb[0:C1, cols],
                                      ALU.subtract).then_inc(s_lo, 1)


def build(nc, a, out, stop=99):
    with ExitStack() as ctx:
        def sb(name, width, dt=F32, parts=P):
            return ctx.enter_context(nc.sbuf_tensor(name, [parts, width], dt))

        x = sb("x", TILES * C)
        y = sb("y", TILES * C)
        vt = sb("vt", TILES * C)
        xt = [sb("xt0", T), sb("xt1", T, parts=C1)]
        ident, ident16 = sb("ident", P), sb("ident16", P, F16)
        iota, cols = sb("iota", 8), sb("cols", 8)
        comb = sb("comb", TILES * 8)
        scratch = {
            "qk": nc.dram_tensor("qk_parts", [2, B * NH, 2, HD, L], F16, kind="Internal").ap(),
            "rel": nc.dram_tensor("rel_parts", [B * NH, 2, 2, SIDE, L], F16, kind="Internal").ap(),
            "o": nc.dram_tensor("o_sums", [B * NH // 2, P, CHUNK], F32, kind="Internal").ap(),
            "rz": nc.dram_tensor("rz_rows", [2 * B * NH, CHUNK], F32, kind="Internal").ap(),
        }

        with Pool(nc, "start") as m:
            s_in = m.sem("in")
            with nc.Block() as block:
                @block.sync
                def _(sp):
                    sp.dma_start(x[:, :].rearrange("p (t f) -> p t f", t=TILES),
                                 a["x"].rearrange("(t p) f -> p t f", p=P)).then_inc(s_in, 16)
                    sp.dma_start(ident[:, :], a["ident"]).then_inc(s_in, 16)
                    sp.dma_start(ident16[:, :], a["ident16"]).then_inc(s_in, 16)
                    sp.dma_start(iota[:, :], a["iota"].broadcast_to([P, 8])).then_inc(s_in, 16)
                    for k, key in enumerate(("ln1_g", "ln1_b", "ln2_g", "ln2_b")):
                        sp.dma_start(cols[:, 2 * k:2 * k + 1], a[key][0:C0, :]).then_inc(s_in, 16)
                        sp.dma_start(cols[0:C1, 2 * k + 1:2 * k + 2], a[key][C0:C, :]).then_inc(s_in, 16)
                    sp.wait_ge(s_in, 12 * 16)

        idn = ident[:, :]
        vt16 = vt[:, :].bitcast(F16)
        parts = [vt16[:, T * k:T * (k + 1)] for k in range(3)]
        stages = []

        def conv(l):
            w = {k: a[f"{l}_{k}"] for k in ("wqk", "bqk", "wv", "bv", "rel_h", "rel_w")}
            w["own"] = a["own"]
            stages.append(lambda: layer_norm(nc, l + "ln", x, 1e-6, turned_to=xt, ident=idn))
            stages.append(lambda: qkv(nc, l + "qkv", xt, vt, w, scratch))
            stages.append(lambda: attention(nc, l + "att", vt, True, scratch, a["hot"], ident16[:, :]))
            stages.append(lambda: project(nc, l + "proj", x, a[f"{l}_wo"], a[f"{l}_bo"], scratch))

        conv("c0")
        stages.append(lambda: layer_norm(nc, "f0ln", x, 1e-5, turned_to=xt, ident=idn, parts=parts))
        stages.append(lambda: gates(nc, "f0gate", xt, a["f0_gate"], 8, comb, iota[:, :]))
        stages.append(lambda: feed_forward(nc, "f0", parts, x, 8, 3, a["f0_up"], a["f0_down"], gate_bank=a["f0_bank"], comb=comb))
        conv("c1")
        stages.append(lambda: layer_norm(nc, "u", x, 1e-5, store=y))
        stages.append(lambda: layer_norm(nc, "h", y, 1e-5, turned_to=xt, gain=cols[:, 0:2], shift=cols[:, 2:4], ident=idn))
        w1 = {k: a[f"f1_{k}"] for k in ("wqk", "bqk", "wv", "bv")}
        stages.append(lambda: qkv(nc, "f1qkv", xt, vt, w1, scratch))
        stages.append(lambda: attention(nc, "f1att", vt, False, scratch, None, ident16[:, :]))
        stages.append(lambda: project(nc, "f1proj", y, a["f1_wo"], a["f1_bo"], scratch))
        stages.append(lambda: turn(nc, "f1turn", y, parts, idn))
        stages.append(lambda: feed_forward(nc, "mlp", parts, y, 1, 6, a["mlp_w1"], a["mlp_w2"], b_up=a["mlp_b1"], b_down=a["mlp_b2"]))
        stages.append(lambda: layer_norm(nc, "xm", y, 1e-5, turned_to=xt, gain=cols[:, 4:6], shift=cols[:, 6:8], ident=idn, parts=parts))
        stages.append(lambda: gates(nc, "f1gate", xt, a["f1_gate"], 4, comb, iota[:, :], gate_b=a["f1_gate_b"],
                                    add_bias=(y, a["exp_b2"])))
        stages.append(lambda: feed_forward(nc, "moe", parts, y, 4, 6, a["exp_w1"], a["exp_w2"], b_up=a["exp_b1"], comb=comb))
        for s in stages[:stop]:
            s()

        with Pool(nc, "end") as m:
            s_sum, s_out = m.sem("sum"), m.sem("out")
            with nc.Block() as block:
                @block.vector
                def _(dve):
                    dve.tensor_tensor(x[:, :], x[:, :], y[:, :] if stop > len(stages) else x[:, :], ALU.add).then_inc(s_sum, 1)

                @block.sync
                def _(sp):
                    sp.wait_ge(s_sum, 1)
                    sp.dma_start(out.rearrange("(t p) f -> p t f", p=P),
                                 x[:, :].rearrange("p (t f) -> p t f", t=TILES)).then_inc(s_out, 16)
                    sp.wait_ge(s_out, 16)


def _attn(inputs, l, qkv_w, qkv_b, proj_w, proj_b):
    w, bias = np.asarray(inputs[qkv_w]), np.asarray(inputs[qkv_b])
    q, k, v = w[0:C], w[C:2 * C], w[2 * C:]
    bq, bk = bias[0:C], bias[C:2 * C]
    groups = [slice(GW * g, GW * (g + 1)) for g in range(GROUPS)]
    return {
        f"{l}_wqk": np.concatenate([np.concatenate([q[s], k[s]]) for s in groups]).T,
        f"{l}_bqk": np.stack([np.concatenate([bq[s], bk[s]]) for s in groups], axis=1),
        f"{l}_wv": v.T,
        f"{l}_bv": bias[2 * C:][None],
        f"{l}_wo": np.asarray(inputs[proj_w]).T,
        f"{l}_bo": np.asarray(inputs[proj_b])[None],
    }


def host_arrays(inputs):
    i = {k: np.asarray(v) for k, v in inputs.items()}
    a = {"x": i["x"].reshape(T, C)}
    for l, n in (("c0", "L0_conv"), ("c1", "L1_conv")):
        a.update(_attn(i, l, f"{n}_qkv_w", f"{n}_qkv_b", f"{n}_proj_w", f"{n}_proj_b"))
        a[f"{l}_rel_h"] = i[f"{n}_rel_pos_h"][::-1].T
        a[f"{l}_rel_w"] = i[f"{n}_rel_pos_w"][::-1].T
    a.update(_attn(i, "f1", "L1_ffn_in_w", "L1_ffn_in_b", "L1_ffn_out_w", "L1_ffn_out_b"))
    wide = lambda w: w.transpose(1, 0, 2).reshape(C, -1)
    a["f0_gate"] = i["L0_ffn_gate_w"].T
    a["f0_bank"], a["f0_up"] = wide(i["L0_ffn_gate_bank"]), wide(i["L0_ffn_up_bank"])
    a["f0_down"] = i["L0_ffn_down_bank"].reshape(-1, C)
    for k in ("ln1_g", "ln1_b", "ln2_g", "ln2_b"):
        a[k] = i[f"L1_ffn_{k}"][:, None]
    a["mlp_w1"], a["mlp_w2"] = i["L1_ffn_mlp_w1"], i["L1_ffn_mlp_w2"]
    a["mlp_b1"] = i["L1_ffn_mlp_b1"].reshape(-1, P).T
    a["mlp_b2"] = i["L1_ffn_mlp_b2"][None]
    a["f1_gate"] = i["L1_ffn_gate_w"].T
    a["f1_gate_b"] = i["L1_ffn_gate_b"][None]
    a["exp_w1"] = wide(i["L1_ffn_exp_w1"])
    a["exp_b1"] = i["L1_ffn_exp_b1"].reshape(-1, P).T
    a["exp_w2"] = i["L1_ffn_exp_w2"].reshape(-1, C)
    a["exp_b2"] = i["L1_ffn_exp_b2"].reshape(1, -1)
    a["ident"] = np.eye(P, dtype=np.float32)
    a["ident16"] = np.eye(P, dtype=np.float16)
    a["iota"] = np.arange(8, dtype=np.float32)[None]
    a["own"] = (np.arange(GW)[:, None] // HD == np.arange(GH)[None]).astype(np.float32) * np.float32(HD ** 0.5)
    token = np.arange(L)
    a["hot"] = np.concatenate([token[None] % SIDE == np.arange(SIDE)[:, None],
                               token[None] // SIDE == np.arange(SIDE)[:, None]]).astype(np.float16)
    return {k: np.ascontiguousarray(v) for k, v in a.items()}


def kernel(**inputs):
    import concourse.bacc as bacc
    from concourse.bass_utils import run_bass_kernel_spmd

    nc = bacc.Bacc("TRN2", target_bir_lowering=False, num_devices=1)
    arrays = host_arrays(inputs)
    aps = {k: nc.dram_tensor(f"in_{k}", v.shape, mybir.dt.from_np(v.dtype), kind="ExternalInput").ap()
           for k, v in arrays.items()}
    out = nc.dram_tensor("out_x", (T, C), F32, kind="ExternalOutput").ap()
    build(nc, aps, out)
    r = run_bass_kernel_spmd(nc, [{f"in_{k}": v for k, v in arrays.items()}], core_ids=[0])
    return r.results[0]["out_x"].reshape(B, SIDE, SIDE, C)
```

```python
from contextlib import ExitStack

import numpy as np

import concourse.bass as bass
from concourse import mybir

F32 = mybir.dt.float32
F16 = mybir.dt.float16
U32 = mybir.dt.uint32
ALU = mybir.AluOpType
ACT = mybir.ActivationFunctionType
AX = mybir.AxisListType

B, SIDE, C, NH, HD = 4, 32, 192, 12, 16
L = SIDE * SIDE
T = B * L
P = 128
TILES = T // P
CHUNK = 512
C0, C1 = P, C - P
GROUPS = 3
GH = NH // GROUPS
GW = GH * HD
KT = L // P
QSIDE = SIDE // 2
Q = QSIDE * QSIDE
PAIRS = B * NH // 2
RING = 3

R_REL = 0
R_QK = 64
R_MAX = 96
R_LOW = 97
R_END = R_LOW + HD
QUARTERS = 4


def ts(i, n):
    return bass.ts(i, n)


class Pool:

    def __init__(self, nc, name):
        self.nc, self.name, self.stack, self.sems = nc, name, ExitStack(), []

    def __enter__(self):
        return self

    def __exit__(self, *what):
        if what[0] is None:
            nc, sems = self.nc, self.sems
            with nc.Block() as block:
                @block.sync
                def _(sp):
                    for s in sems:
                        sp.sem_clear(s)
        self.stack.close()

    def sb(self, name, width, dt=F32, parts=P):
        return self.stack.enter_context(self.nc.sbuf_tensor(f"{self.name}_{name}", [parts, width], dt))

    def ps(self, name, width=CHUNK):
        return self.stack.enter_context(self.nc.psum_tensor(f"{self.name}_{name}", [P, width], F32))

    def sem(self, name):
        s = self.stack.enter_context(self.nc.semaphore(f"{self.name}_{name}"))
        self.sems.append(s)
        return s


def linker(engine, sem):
    count = [0]

    def link(ins):
        count[0] += 1
        ins.then_inc(sem, 1)
        engine.wait_ge(sem, count[0])

    return link


def layer_norm(nc, name, src, eps, store=None, turned_to=None, gain=None, shift=None, ident=None, parts=None):
    with Pool(nc, name) as m:
        st = m.sb("stats", TILES * 6)
        mean, mdiff, vsum, var, std, rstd = (m.sb(n, TILES) for n in ("mean", "mdiff", "vsum", "var", "std", "rstd"))
        s_stats, s_chain, s_std = m.sem("stats"), m.sem("chain"), m.sem("std")
        s_ready = m.sem("ready")
        s_norm, s_turned, s_evac = m.sem("norm"), m.sem("turned"), m.sem("evac")
        s_stored = m.sem("stored")
        s_hi, s_lo, s_f32 = m.sem("hi"), m.sem("lo"), m.sem("f32")
        if turned_to is not None:
            nrm = [m.sb(f"nrm{u}", 4 * C) for u in range(2)]
            t0 = [m.ps(f"t0{u}") for u in range(2)]
            t1 = [m.ps(f"t1{u}") for u in range(2)]
        with nc.Block() as block:
            @block.vector
            def _(dve):
                with dve.Fori(0, TILES // 8) as it:
                    for j in range(8):
                        t = it * 8 + j
                        dve.bn_stats(st[:, ts(t, 6)], src[:, ts(t, C)]).then_inc(s_stats, 1)
                dve.wait_ge(s_stats, TILES)
                half = st[:, :].rearrange("p (t s) -> p s t", s=6)
                link = linker(dve, s_chain)
                link(dve.tensor_tensor(mean[:, :], half[:, 1, :], half[:, 4, :], ALU.add))
                link(dve.tensor_tensor(mdiff[:, :], half[:, 1, :], half[:, 4, :], ALU.subtract))
                link(dve.tensor_tensor(vsum[:, :], half[:, 2, :], half[:, 5, :], ALU.add))
                link(dve.tensor_tensor(mdiff[:, :], mdiff[:, :], mdiff[:, :], ALU.mult))
                link(dve.tensor_scalar(vsum[:, :], vsum[:, :], 1.0 / C, eps, ALU.mult, ALU.add))
                link(dve.scalar_tensor_tensor(out=var[:, :], in0=mdiff[:, :], scalar=0.25, in1=vsum[:, :],
                                              op0=ALU.mult, op1=ALU.add))
                link(dve.tensor_scalar(mean[:, :], mean[:, :], 0.5, None, ALU.mult))
                dve.wait_ge(s_std, 1)
                link(dve.reciprocal(rstd[:, :], std[:, :]))
                link(dve.tensor_tensor(std[:, :], rstd[:, :], rstd[:, :], ALU.mult))
                link(dve.tensor_tensor(std[:, :], std[:, :], var[:, :], ALU.mult))
                link(dve.tensor_scalar(std[:, :], std[:, :], -0.5, 1.5, ALU.mult, ALU.add))
                link(dve.tensor_tensor(rstd[:, :], rstd[:, :], std[:, :], ALU.mult))
                if store is not None:
                    with dve.Fori(0, TILES // 8) as it:
                        for j in range(8):
                            t = it * 8 + j
                            dve.tensor_scalar(store[:, ts(t, C)], src[:, ts(t, C)], mean[:, ts(t, 1)],
                                              rstd[:, ts(t, 1)], ALU.subtract, ALU.mult).then_inc(s_stored, 1)
                    dve.wait_ge(s_stored, TILES)
                else:
                    dve.sem_inc(s_turned, 2)
                    with dve.Fori(0, TILES // 8) as it:
                        for u in range(2):
                            dve.wait_ge(s_turned, it * 2 + (u + 1))
                            for j in range(4):
                                t = it * 8 + (4 * u + j)
                                dve.tensor_scalar(nrm[u][:, j * C:(j + 1) * C], src[:, ts(t, C)],
                                                  mean[:, ts(t, 1)], rstd[:, ts(t, 1)],
                                                  ALU.subtract, ALU.mult).then_inc(s_norm, 1)
                    if parts is not None:
                        xa_hi, xa_lo, xb = parts
                        with dve.Fori(0, TILES // 8) as it:
                            for u in range(2):
                                dve.wait_ge(s_evac, it * 4 + (2 * u + 6))
                                cols = ts(it * 2 + u, CHUNK)
                                dve.tensor_tensor(xa_lo[:, cols], turned_to[0][:, cols], xa_hi[:, cols],
                                                  ALU.subtract).then_inc(s_lo, 1)
                                dve.tensor_tensor(xb[C1:P, cols], turned_to[1][0:C1, cols], xb[0:C1, cols],
                                                  ALU.subtract).then_inc(s_lo, 1)
                        dve.wait_ge(s_lo, TILES // 2)

            @block.scalar
            def _(act):
                act.wait_ge(s_chain, 6)
                act.activation(std[:, :], var[:, :], ACT.Sqrt).then_inc(s_std, 1)
                if turned_to is None:
                    return
                with act.Fori(0, TILES // 8) as it:
                    for u in range(2):
                        act.wait_ge(s_turned, it * 2 + (u + 3))
                        cols = ts(it * 2 + u, CHUNK)
                        for k, (tile, n) in enumerate(((t0[u], C0), (t1[u], C1))):
                            scale = 1.0 if gain is None else gain[0:n, k:k + 1]
                            bias = 0.0 if shift is None else shift[0:n, k:k + 1]
                            act.activation(turned_to[k][0:n, cols], tile[0:n, :], ACT.Identity,
                                           bias=bias, scale=scale).then_inc(s_f32, 1)
                            if parts is not None:
                                act.activation(parts[2 * k][0:n, cols], tile[0:n, :], ACT.Identity,
                                               bias=bias, scale=scale).then_inc(s_hi, 1)
                        act.wait_ge(s_f32, it * 4 + (2 * u + 2))
                        if parts is not None:
                            act.wait_ge(s_hi, it * 4 + (2 * u + 2))
                        act.sem_inc(s_evac, 2)

            @block.tensor
            def _(pe):
                if turned_to is None:
                    return
                pe.sem_inc(s_evac, 4)
                with pe.Fori(0, TILES // 8) as it:
                    for u in range(2):
                        pe.wait_ge(s_norm, it * 8 + (4 * u + 4))
                        pe.wait_ge(s_evac, it * 4 + (2 * u + 2))
                        for j in range(4):
                            pe.transpose(t0[u][:, j * P:(j + 1) * P], nrm[u][:, j * C:j * C + C0], ident)
                            ins = pe.transpose(t1[u][0:C1, j * P:(j + 1) * P],
                                               nrm[u][:, j * C + C0:(j + 1) * C], ident)
                        ins.then_inc(s_turned, 1)


def qkv(nc, name, xt, vt, w, scratch):
    rel = "rel_h" in w
    with Pool(nc, name) as m:
        wqk = [m.sb("wqk0", 2 * C), m.sb("wqk1", 2 * C, parts=C1)]
        wv = [m.sb("wv0", C), m.sb("wv1", C, parts=C1)]
        bqk, bv, scale = m.sb("bqk", GROUPS), m.sb("bv", C), m.sb("scale", 1)
        qt = m.sb("qt", GROUPS * T)
        hi = [m.sb(f"hi{u}", L, F16) for u in range(2)]
        lo = [m.sb(f"lo{u}", L, F16) for u in range(2)]
        qp = [m.ps(f"qp{u}") for u in range(2)]
        vp = [m.ps(f"vp{u}") for u in range(2)]
        rp = [m.ps(f"rp{u}") for u in range(2)]
        s_w, s_tab, s_init, s_tabs = m.sem("w"), m.sem("tab"), m.sem("init"), m.sem("tabs")
        s_qk, s_qt, s_hi, s_lo = m.sem("qk"), m.sem("qt"), m.sem("hi"), m.sem("lo")
        s_st = [m.sem(f"st{u}") for u in range(2)]
        s_v, s_vt = m.sem("v"), m.sem("vt")
        s_rel, s_rhi, s_rlo = m.sem("rel"), m.sem("rhi"), m.sem("rlo")
        s_rst = [m.sem(f"rst{u}") for u in range(2)]
        if rel:
            raw = [m.sb(f"raw{k}", 2 * SIDE - 1, parts=GW) for k in range(2)]
            tab = [m.sb(f"tab{k}", (2 * SIDE - 1) * GH) for k in range(2)]
            own = m.sb("own", GH, parts=GW)
            rhi = [m.sb(f"rhi{k}", T, F16) for k in range(2)]
            rlo = [m.sb(f"rlo{k}", T, F16) for k in range(2)]
        vt4 = vt[:, :].rearrange("p (a k f) -> p a k f", a=PAIRS, k=KT)
        with nc.Block() as block:
            @block.sync
            def _(sp):
                sp.dma_start(wqk[0][:, :], w["wqk"][0:C0, :]).then_inc(s_w, 16)
                sp.dma_start(wqk[1][:, :], w["wqk"][C0:C, :]).then_inc(s_w, 16)
                sp.dma_start(bqk[:, :], w["bqk"]).then_inc(s_w, 16)
                sp.dma_start(wv[0][:, :], w["wv"][0:C0, :]).then_inc(s_w, 16)
                sp.dma_start(wv[1][:, :], w["wv"][C0:C, :]).then_inc(s_w, 16)
                sp.dma_start(bv[:, :], w["bv"].broadcast_to([P, C])).then_inc(s_w, 16)
                if rel:
                    for k, key in enumerate(("rel_h", "rel_w")):
                        for h in range(GH):
                            sp.dma_start(raw[k][h * HD:(h + 1) * HD, :], w[key]).then_inc(s_tab, 16)
                    sp.dma_start(own[:, :], w["own"]).then_inc(s_tab, 16)
                with sp.Fori(0, 2) as it:
                    for g2 in range(6):
                        u = g2 % 2
                        n = it * 12 + 2 * g2
                        sp.wait_ge(s_hi, n + 2)
                        sp.wait_ge(s_lo, n + 2)
                        row = (it * 6 + g2) * GH
                        for s in range(2):
                            for part, buf in enumerate((hi[u], lo[u])):
                                sp.dma_start(scratch["qk"][s, bass.ds(row, GH), part, :, :],
                                             buf[GW * s:GW * (s + 1), :]).then_inc(s_st[u], 16)
                if rel:
                    for g in range(GROUPS):
                        for k in range(2):
                            sp.wait_ge(s_rlo, g * 16 + (8 * k + 8 + 2))
                            for b in range(B):
                                for part, buf in enumerate((rhi[k], rlo[k])):
                                    for half in range(2):
                                        rows = scratch["rel"][g * GH + b * NH:(g + 1) * GH + b * NH, k, half, part]
                                        sp.dma_start(rows.rearrange("h r n -> r h n"),
                                                     buf[C1 * half:C1 * (half + 1), b * L:(b + 1) * L]
                                                     ).then_inc(s_rst[k], 16)
                for u in range(2):
                    sp.wait_ge(s_st[u], 64 * 7)
                    if rel:
                        sp.wait_ge(s_rst[u], 256 * (GROUPS + 1))

            @block.gpsimd
            def _(pool):
                pool.memset(scale[0:GW, :], float(HD) ** -0.5).then_inc(s_init, 1)
                pool.memset(scale[GW:P, :], 1.0).then_inc(s_init, 1)
                with pool.Fori(0, 2) as it:
                    for g2 in range(6):
                        u = g2 % 2
                        pool.wait_ge(s_st[u], it * 192 + (g2 // 2 + 1) * 64)
                        for half in range(2):
                            n = it * 12 + (2 * g2 + half)
                            pool.wait_ge(s_hi, n + 1)
                            cols = bass.ds((it * 2 + g2 // 3) * L + ((g2 % 3) * T + half * CHUNK), CHUNK)
                            pool.tensor_tensor(lo[u][:, half * CHUNK:(half + 1) * CHUNK], qt[:, cols],
                                               hi[u][:, half * CHUNK:(half + 1) * CHUNK],
                                               ALU.subtract).then_inc(s_lo, 1)

            @block.tensor
            def _(pe):
                pe.wait_ge(s_w, 6 * 16)
                pe.sem_inc(s_qt, 2)
                with pe.Fori(0, 2) as it:
                    for g2 in range(6):
                        g = g2 % 3
                        for half in range(2):
                            n = it * 12 + (2 * g2 + half)
                            cols = bass.ds((it * 2 + g2 // 3) * L + half * CHUNK, CHUNK)
                            pe.wait_ge(s_qt, n + 1)
                            pe.matmul(qp[half][:, :], wqk[0][:, g * P:(g + 1) * P], xt[0][:, cols],
                                      start=True, stop=False)
                            pe.matmul(qp[half][:, :], wqk[1][:, g * P:(g + 1) * P], xt[1][0:C1, cols],
                                      start=False, stop=True).then_inc(s_qk, 1)
                for t in range(TILES):
                    if t >= 2:
                        pe.wait_ge(s_vt, t - 1)
                    pe.matmul(vp[t % 2][:, 0:C], xt[0][:, t * P:(t + 1) * P], wv[0][:, :], start=True, stop=False)
                    pe.matmul(vp[t % 2][:, 0:C], xt[1][0:C1, t * P:(t + 1) * P], wv[1][:, :],
                              start=False, stop=True).then_inc(s_v, 1)
                if not rel:
                    return
                pe.wait_ge(s_tabs, 4)
                pe.wait_ge(s_qt, 24 + 2)
                pe.sem_inc(s_rlo, 2)
                with pe.Fori(0, GROUPS) as g:
                    for k in range(2):
                        for qq in range(8):
                            pe.wait_ge(s_rlo, g * 16 + (8 * k + qq + 1))
                            for j in range(4):
                                r = 4 * qq + j
                                table = tab[k][:, (SIDE - 1 - r) * GH:(2 * SIDE - 1 - r) * GH]
                                q = qt[:, ts(g, T)]
                                if k == 0:
                                    q = q.rearrange("p (b u s y x) -> p u y b s x", b=B, u=2, s=2, y=QSIDE)[
                                        :, r // QSIDE, r % QSIDE]
                                    out = rp[qq % 2][:, :].rearrange("p (b s j x) -> p j b s x", b=B, s=2, j=4)[:, j]
                                else:
                                    q = q.rearrange("p (n s y x) -> p s x n y", s=2, y=QSIDE, x=QSIDE)[
                                        :, r // QSIDE, r % QSIDE]
                                    out = rp[qq % 2][:, j * P:(j + 1) * P].rearrange("p (n y) -> p n y", y=QSIDE)
                                ins = pe.matmul(out, table, q, start=True, stop=True)
                            ins.then_inc(s_rel, 1)

            @block.vector
            def _(dve):
                if rel:
                    dve.wait_ge(s_tab, 9 * 16)
                    for k in range(2):
                        dims = [GW, 2 * SIDE - 1, GH]
                        dve.memset(tab[k][GW:P, :], 0.0).then_inc(s_tabs, 1)
                        dve.tensor_tensor(tab[k][0:GW, :].rearrange("p (i h) -> p i h", h=GH),
                                          raw[k][:, :].unsqueeze(2).broadcast_to(dims),
                                          own[:, :].unsqueeze(1).broadcast_to(dims), ALU.mult).then_inc(s_tabs, 1)
                dve.wait_ge(s_w, 6 * 16)
                dve.wait_ge(s_init, 2)
                with dve.Fori(0, 2) as it:
                    for g2 in range(6):
                        for half in range(2):
                            n = it * 12 + (2 * g2 + half)
                            dve.wait_ge(s_qk, n + 1)
                            cols = bass.ds((it * 2 + g2 // 3) * L + ((g2 % 3) * T + half * CHUNK), CHUNK)
                            dve.tensor_scalar(qt[:, cols], qp[half][:, :], bqk[:, g2 % 3:g2 % 3 + 1],
                                              scale[:, 0:1], ALU.add, ALU.mult).then_inc(s_qt, 1)
                for t in range(TILES):
                    dve.wait_ge(s_v, t + 1)
                    b, kt = t // KT, t % KT
                    dve.tensor_tensor(vt4[:, NH // 2 * b:NH // 2 * (b + 1), kt, :],
                                      vp[t % 2][:, 0:C].rearrange("p (g f) -> p g f", f=2 * HD),
                                      bv[:, :].rearrange("p (g f) -> p g f", f=2 * HD),
                                      ALU.add).then_inc(s_vt, 1)
                dve.wait_ge(s_vt, TILES)
                if not rel:
                    return
                with dve.Fori(0, GROUPS) as g:
                    for k in range(2):
                        for qq in range(8):
                            n = g * 16 + (8 * k + qq)
                            dve.wait_ge(s_rhi, n + 1)
                            src, out, high = rel_views(rp[qq % 2], rlo[k], rhi[k], k, qq)
                            dve.tensor_tensor(out, src, high, ALU.subtract).then_inc(s_rlo, 1)

            @block.scalar
            def _(act):
                for u in range(2):
                    act.sem_inc(s_st[u], 64)
                with act.Fori(0, 2) as it:
                    for g2 in range(6):
                        u = g2 % 2
                        act.wait_ge(s_st[u], it * 192 + (g2 // 2 + 1) * 64)
                        act.wait_ge(s_lo, it * 12 + 2 * g2) if g2 else None
                        for half in range(2):
                            n = it * 12 + (2 * g2 + half)
                            act.wait_ge(s_qt, n + 3)
                            cols = bass.ds((it * 2 + g2 // 3) * L + ((g2 % 3) * T + half * CHUNK), CHUNK)
                            act.activation(hi[u][:, half * CHUNK:(half + 1) * CHUNK], qt[:, cols],
                                           ACT.Identity).then_inc(s_hi, 1)
                if not rel:
                    return
                for k in range(2):
                    act.sem_inc(s_rst[k], 256)
                with act.Fori(0, GROUPS) as g:
                    for k in range(2):
                        act.wait_ge(s_rst[k], g * 256 + 256)
                        for qq in range(8):
                            n = g * 16 + (8 * k + qq)
                            act.wait_ge(s_rel, n + 1)
                            src, out, _ = rel_views(rp[qq % 2], rhi[k], rhi[k], k, qq)
                            act.activation(out, src, ACT.Identity).then_inc(s_rhi, 1)


def rel_views(bank, part, high, k, qq):
    half, first = qq // 4, qq % 4 * 4
    if k == 0:
        src = bank[:, :].rearrange("p (b s m) -> p b s m", b=B, s=2)
        where = [t[:, :].rearrange("p (b u s m) -> p u b s m", b=B, u=2, s=2)[
            :, half, :, :, first * QSIDE:(first + 4) * QSIDE] for t in (part, high)]
    else:
        src = bank[:, :].rearrange("p (j n y) -> p j n y", j=4, y=QSIDE)
        where = [t[:, :].rearrange("p (n s y x) -> p s x n y", s=2, y=QSIDE, x=QSIDE)[
            :, half, first:first + 4, :, :] for t in (part, high)]
    return src, where[0], where[1]


def attention(nc, name, vt, rel, scratch, hot, ident16, room=None):
    with Pool(nc, name) as m:
        versions = QUARTERS if rel else 1
        qa = room or [m.sb(f"qa{u}", 2 * L, F16) for u in range(RING)]
        ka = [m.sb(f"ka{u}", 2 * L, F16) for u in range(RING)]
        vs = [m.sb(f"vs{u}", 2 * KT * 32) for u in range(RING)]
        osb = [m.sb(f"o{u}", CHUNK) for u in range(RING)]
        pr = [[m.sb(f"p{h}{k}", L) for k in range(2)] for h in range(2)]
        mx = m.sb("mx", 2 * KT * 2)
        m32, m16 = m.sb("m32", 2 * KT), m.sb("m16", 2 * KT, F16)
        sps = [m.ps(f"s{h}", L) for h in range(2)]
        mps = [m.ps(f"m{k}") for k in range(3)]
        ops = m.ps("o")
        s_const, s_ones = m.sem("const"), m.sem("ones")
        s_ld = [m.sem(f"ld{u}") for u in range(RING)]
        s_vs, s_mm, s_mx = m.sem("vs"), m.sem("maxprod"), m.sem("maxima")
        s_chain = m.sem("chain")
        s_m16, s_row, s_qm = m.sem("m16"), m.sem("maxrow"), m.sem("qamax")
        s_s, s_e, s_pv = m.sem("scores"), m.sem("exp"), m.sem("pv")
        s_o, s_qv = m.sem("out"), [m.sem(f"qaversions{h}") for h in range(2)]
        s_st = [m.sem(f"st{u}") for u in range(RING)]
        LOADS = 3 + (2 * 7 if rel else 3)
        MAXES = 2 * 2 * KT
        ONES = 2 * RING + (0 if rel else 2 * RING)

        def queries(h, version, first, count):
            at = (h * versions + version) * L + first
            return slice(at, at + count)

        def load(sp, pair, u):
            heads = bass.ds(pair * 2, 2)
            for part, row in ((0, R_QK), (1, R_QK + HD), (0, R_LOW)):
                sp.dma_start(ka[u][row:row + HD, :].rearrange("p (h n) -> p h n", h=2),
                             scratch["qk"][1, heads, part, :, :].rearrange("h r n -> r h n")).then_inc(s_ld[u], 16)
            if not rel:
                for part, row in ((0, R_QK), (0, R_QK + HD), (1, R_LOW)):
                    sp.dma_start(qa[u][row:row + HD, :].rearrange("p (h n) -> p h n", h=2),
                                 scratch["qk"][0, heads, part, :, :].rearrange("h r n -> r h n")
                                 ).then_inc(s_ld[u], 16)
                return
            for h in range(2):
                head = bass.ds(pair * 2 + h, 1)
                to = qa[u][:, h * versions * L:(h + 1) * versions * L]
                for part, row in ((0, R_QK), (0, R_QK + HD), (1, R_LOW)):
                    src = scratch["qk"][0, head, part, :, :].rearrange("a r n -> (a r) n").unsqueeze(1)
                    sp.dma_start(to[row:row + HD, :].rearrange("p (v n) -> p v n", v=versions),
                                 src.broadcast_to([HD, versions, L])).then_inc(s_ld[u], 16)
                for k in range(2):
                    for half in range(2):
                        row = R_REL + 2 * QSIDE * k
                        src = scratch["rel"][head, k, half].rearrange("a p r n -> (a p r) n").unsqueeze(1)
                        dst = to[row:row + 2 * QSIDE, :].rearrange("p (u s n) -> p u s n", u=2, s=2)
                        dst = dst[:, half, :, :] if k == 0 else dst[:, :, half, :]
                        sp.dma_start(dst, src.broadcast_to([2 * QSIDE, 2, L])).then_inc(s_ld[u], 16)

        def spread_rows(sp, pair, u):
            for h in range(2 if rel else 0):
                sp.wait_ge(s_qm, pair * 4 + (2 * h + 2))
                at = qa[u][R_MAX:R_MAX + 1, h * versions * L:(h + 1) * versions * L]
                sp.dma_start(at[:, L:].rearrange("p (v n) -> p v n", n=L),
                             at[:, 0:L].unsqueeze(1).broadcast_to([1, versions - 1, L])).then_inc(s_qv[h], 16)

        EARLY = 6
        counts = [(2, 0, 0, 0)] + (KT - 2) * [(1, 1, 2, 0)] + [(1, 1, 2, 2)]
        ROW0 = 4
        items, PLAN = [(1, n) for n in range(EARLY, MAXES)] + [(2, n) for n in range(EARLY)], []
        for kt in range(KT):
            PLAN.append([[items.pop(0) for _ in range(c)] for c in counts[kt]])
            if kt == ROW0:
                PLAN[kt][2].append((1, "row", 0))
            if kt == KT - 1:
                PLAN[kt][2].append((1, "row", 1))
        assert not items
        USES = [item for steps in PLAN for step in steps for item in step]
        START = ([(0, n) for n in range(22)] + [(0, "row", 0)] + [(0, n) for n in range(22, MAXES)]
                 + [(i[0] - 1,) + i[1:] for i in USES[-EARLY - 1:]])

        def free(item, pair):
            if item[1] == "row":
                return s_qm, (pair + item[0]) * 4 + (2 * item[2] + 2)
            return s_mx, (pair + item[0]) * MAXES + (item[1] + 1)

        def use_bank(pe, pair, pos, item, u, skip=()):
            started = pair is None
            g = pos if started else len(START) + len(USES) * u + pos
            before = pos - 3
            if started:
                if before >= 0:
                    pe.wait_ge(*free(START[before], 0))
            else:
                while before >= 0 and USES[before][0] in skip:
                    before -= 3
                pe.wait_ge(*free(USES[before], pair if before >= 0 else pair - 1))
            bank, q = mps[g % 3], 0 if started else pair
            v = (u + item[0]) % RING
            if item[1] == "row":
                h = item[2]
                pe.wait_ge(s_m16, (q + item[0]) * 2 + (h + 1))
                for j in range(KT):
                    half = j // 4
                    ins = pe.matmul(bank[32 * half:32 * half + 1, (j % 4) * P:(j % 4 + 1) * P],
                                    m16[:, h * KT + j:h * KT + j + 1], ident16, start=True, stop=True)
                ins.then_inc(s_row, 1)
            else:
                n = item[1]
                h, qi, c = n // 16, n // 2 % 8, n % 2
                width = CHUNK // 2 if rel else CHUNK
                for i in range(CHUNK // width):
                    k0 = c * CHUNK + i * width
                    ins = pe.matmul(bank[:, i * width:(i + 1) * width],
                                    qa[v][0:R_MAX, queries(h, k0 // Q if rel else 0, qi * P, P)],
                                    ka[v][0:R_MAX, h * L + k0:h * L + k0 + width], start=True, stop=True)
                ins.then_inc(s_mm, 1)

        def score(pe, pair, u, h, kt, first=False):
            if kt == 0:
                pe.wait_ge(s_qm, pair * 4 + (2 * h + 2))
            if not first:
                pe.wait_ge(s_e, pair * 16 + (2 * kt + h - 1))
            version = kt * P // Q if rel else 0
            if rel and kt == Q // P:
                pe.wait_ge(s_qv[h], pair * 16 + 16)
            kcol = slice(h * L + kt * P, h * L + (kt + 1) * P)
            for c in range(2):
                ins = pe.matmul(sps[h][:, c * CHUNK:(c + 1) * CHUNK], ka[u][0:R_END, kcol],
                                qa[u][0:R_END, queries(h, version, c * CHUNK, CHUNK)], start=True, stop=True)
            ins.then_inc(s_s, 1)

        def weigh(pe, pair, u, kt):
            pe.wait_ge(s_e, pair * 16 + (2 * kt + 2))
            if kt == 0:
                pe.wait_ge(s_vs, pair * 2 + 2)
                pe.wait_ge(s_o, pair + 1)
            for h in range(2):
                for c in range(2):
                    row = 32 * (2 * h + c)
                    ins = pe.matmul(ops[row:row + 32, :], vs[u][:, (h * KT + kt) * 32:(h * KT + kt + 1) * 32],
                                    pr[h][kt % 2][:, c * CHUNK:(c + 1) * CHUNK], start=kt == 0, stop=kt == KT - 1)
            ins.then_inc(s_pv, 1)

        def pe_pair(pe, turn, pair, u, skip=()):
            pos = 0

            def maxima(steps):
                nonlocal pos
                for item in steps:
                    if item[0] not in skip:
                        if item == USES[len(USES) - EARLY - 1]:
                            pe.wait_ge(s_ld[(u + 2) % RING], (turn + (u + 2) // RING + 1) * (16 * LOADS))
                        use_bank(pe, pair, pos, item, u, skip)
                    pos += 1

            for kt in range(KT):
                if kt:
                    score(pe, pair, u, 0, kt)
                maxima(PLAN[kt][0])
                if kt:
                    score(pe, pair, u, 1, kt)
                maxima(PLAN[kt][1])
                if kt:
                    weigh(pe, pair, u, kt - 1)
                if kt == KT - 1 and 1 not in skip:
                    score(pe, pair + 1, (u + 1) % RING, 0, 0)
                maxima(PLAN[kt][2])
            weigh(pe, pair, u, KT - 1)
            if 1 not in skip:
                score(pe, pair + 1, (u + 1) % RING, 1, 0)
            maxima(PLAN[KT - 1][3])

        def bank_of(u, item):
            return mps[(len(START) + len(USES) * u + USES.index(item)) % 3]

        def dve_max(dve, pair, n, bank):
            dve.wait_ge(s_mm, pair * MAXES + (n + 1))
            dve.tensor_reduce(mx[:, n:n + 1], bank[:, :], AX.X, ALU.max).then_inc(s_mx, 1)
            if n % 16 < 15:
                return
            h = n // 16
            dve.wait_ge(s_mx, pair * MAXES + (n + 1))
            dve.tensor_reduce(m32[:, h * KT:(h + 1) * KT],
                              mx[:, 16 * h:16 * h + 16].rearrange("p (q c) -> p q c", c=2),
                              AX.X, ALU.max).then_inc(s_chain, 1)
            dve.wait_ge(s_chain, pair * 2 + (h + 1))
            dve.tensor_scalar(m16[:, h * KT:(h + 1) * KT], m32[:, h * KT:(h + 1) * KT], -1.0, None,
                              ALU.mult).then_inc(s_m16, 1)

        def act_row(act, pair, u, h, bank):
            act.wait_ge(s_row, pair * 2 + (h + 1))
            for half in range(2):
                act.activation(qa[u][R_MAX:R_MAX + 1, queries(h, 0, half * CHUNK, CHUNK)],
                               bank[32 * half:32 * half + 1, :], ACT.Copy).then_inc(s_qm, 1)

        def dve_pair(dve, pair, u, skip=()):
            for item in USES:
                if item[0] not in skip and item[1] != "row":
                    dve_max(dve, pair + item[0], item[1], bank_of(u, item))

        def stage_values(pool, pair, u):
            src = vt[:, ts(pair, KT * 2 * HD)].rearrange("p (k f) -> p k f", k=KT)
            for h in range(2):
                dst = vs[u][:, h * KT * 32:(h + 1) * KT * 32].rearrange("p (k f) -> p k f", k=KT)
                pool.tensor_copy(dst[:, :, 0:HD], src[:, :, h * HD:(h + 1) * HD]).then_inc(s_vs, 1)

        LAST = PAIRS // RING - 1
        LATE = [()] * (RING - 2) + [(2,), (1, 2)]
        with nc.Block() as block:
            @block.sync
            def _(sp):
                if rel:
                    for u in range(RING):
                        for h in range(2):
                            sp.dma_start(ka[u][R_REL:R_QK, h * L:(h + 1) * L], hot).then_inc(s_const, 16)
                for u in range(RING):
                    load(sp, u, u)
                for u in range(RING - 1):
                    spread_rows(sp, u, u)
                with sp.Fori(1, PAIRS // RING) as it:
                    for u in range(RING):
                        sp.wait_ge(s_s, it * (16 * RING) + 16 * (u + 1 - RING))
                        load(sp, it * RING + u, u)
                        spread_rows(sp, it * RING + (u - 1), (u - 1) % RING)
                spread_rows(sp, PAIRS - 1, RING - 1)

            @block.gpsimd
            def _(pool):
                for u in range(RING):
                    stage_values(pool, u, u)
                with pool.Fori(1, PAIRS // RING) as it:
                    for u in range(RING):
                        pool.wait_ge(s_pv, it * (KT * RING) + KT * (u + 1 - RING))
                        stage_values(pool, it * RING + u, u)

            @block.tensor
            def _(pe):
                if rel:
                    pe.wait_ge(s_const, 2 * RING * 16)
                pe.wait_ge(s_ones, ONES)
                pe.wait_ge(s_ld[0], 16 * LOADS)
                for pos, item in enumerate(START):
                    if item == (1, 0):
                        pe.wait_ge(s_ld[1], 16 * LOADS)
                    use_bank(pe, None, pos, item, 0)
                score(pe, 0, 0, 0, 0, first=True)
                score(pe, 0, 0, 1, 0, first=True)
                with pe.Fori(0, LAST) as it:
                    for u in range(RING):
                        pe_pair(pe, it, it * RING + u, u)
                for u in range(RING):
                    pe_pair(pe, LAST, LAST * RING + u, u, LATE[u])

            @block.vector
            def _(dve):
                for u in range(RING):
                    ones = vs[u][:, :].rearrange("p (k f) -> p k f", f=32)
                    dve.memset(ones[:, :, HD:32], 1.0).then_inc(s_ones, 1)
                    dve.memset(ka[u][R_MAX:R_MAX + 1, :], 1.0).then_inc(s_ones, 1)
                    if not rel:
                        for buf in (qa, ka):
                            dve.memset(buf[u][R_REL:R_QK, :], 0.0).then_inc(s_ones, 1)
                for u in range(RING):
                    dve.sem_inc(s_st[u], 16)
                dve.sem_inc(s_o, 1)
                for pos, item in enumerate(START):
                    if item[1] != "row":
                        dve_max(dve, item[0], item[1], mps[pos % 3])
                with dve.Fori(0, LAST) as it:
                    for u in range(RING):
                        dve_pair(dve, it * RING + u, u)
                for u in range(RING):
                    dve_pair(dve, LAST * RING + u, u, LATE[u])

            @block.scalar
            def _(act):
                def exp(pair, kt, h):
                    act.wait_ge(s_s, pair * 16 + (2 * kt + h + 1))
                    if kt >= 2:
                        act.wait_ge(s_pv, pair * KT + (kt - 1))
                    act.activation(pr[h][kt % 2][:, :], sps[h][:, :], ACT.Exp).then_inc(s_e, 1)

                def sums(turn, pair, u):
                    act.wait_ge(s_pv, pair * KT + KT)
                    act.wait_ge(s_st[u], (turn + 1) * 16)
                    act.activation(osb[u][:, :], ops[:, :], ACT.Copy).then_inc(s_o, 1)

                def store(pair, u):
                    act.wait_ge(s_o, pair + 2)
                    act.dma_start(scratch["o"][bass.ds(pair, 1)].rearrange("a p n -> (a p) n"),
                                  osb[u][:, :]).then_inc(s_st[u], 16)

                def act_pair(turn, pair, u, first=False, last=False):
                    exp(pair, 0, 0)
                    if not first:
                        sums(turn - (u == 0), pair - 1, (u - 1) % RING)
                    for kt in range(KT):
                        if kt:
                            exp(pair, kt, 0)
                        exp(pair, kt, 1)
                        if kt == 1 and not first:
                            store(pair - 1, (u - 1) % RING)
                        if kt == ROW0 and not last:
                            act_row(act, pair + 1, (u + 1) % RING, 0, bank_of(u, (1, "row", 0)))
                    if not last:
                        act_row(act, pair + 1, (u + 1) % RING, 1, bank_of(u, (1, "row", 1)))

                for h in range(2):
                    act_row(act, 0, 0, h, mps[START.index((0, "row", h)) % 3])
                for u in range(RING):
                    act_pair(0, u, u, first=u == 0)
                with act.Fori(1, LAST) as it:
                    for u in range(RING):
                        act_pair(it, it * RING + u, u)
                for u in range(RING):
                    act_pair(LAST, LAST * RING + u, u, last=u == RING - 1)
                sums(LAST, PAIRS - 1, RING - 1)
                store(PAIRS - 1, RING - 1)
                for u in range(RING):
                    act.wait_ge(s_st[u], 16 * (PAIRS // RING + 1))


def project(nc, name, res, w, b, scratch):
    with Pool(nc, name) as m:
        z = m.sb("z", CHUNK)
        rz = m.sb("rz", CHUNK)
        pw = [m.sb("pw0", C), m.sb("pw1", C, parts=C1)]
        bias = m.sb("bias", C)
        num = [[m.sb(f"num{k}{u}", CHUNK, parts=(C0, C1)[k]) for k in range(2)] for u in range(2)]
        inv = [[m.sb(f"inv{k}{u}", CHUNK, parts=(C0, C1)[k]) for k in range(2)] for u in range(2)]
        yp = [m.ps(f"y{u}") for u in range(2)]
        s_w, s_z, s_rz, s_rzst = m.sem("w"), m.sem("z"), m.sem("rz"), m.sem("rzst")
        s_ld = [m.sem(f"ld{u}") for u in range(2)]
        s_at, s_y, s_add, s_bias, s_used = m.sem("at"), m.sem("y"), m.sem("add"), m.sem("bias"), m.sem("used")
        zrows = scratch["o"].rearrange("a (s r) n -> (a s) r n", r=32)[:, HD, :]
        heads = scratch["o"].rearrange("a (h c r) n -> (a h) c r n", h=2, c=2)
        zheads = scratch["rz"].rearrange("(h c) n -> h c n", c=2)
        with nc.Block() as block:
            @block.sync
            def _(sp):
                sp.dma_start(z[0:2 * B * NH, :], zrows).then_inc(s_z, 16)
                sp.dma_start(pw[0][:, :], w[0:C0, :]).then_inc(s_w, 16)
                sp.dma_start(pw[1][:, :], w[C0:C, :]).then_inc(s_w, 16)
                sp.dma_start(bias[:, :], b.broadcast_to([P, C])).then_inc(s_w, 16)
                sp.wait_ge(s_rz, 1)
                sp.dma_start(scratch["rz"], rz[0:2 * B * NH, :]).then_inc(s_rzst, 16)
                sp.wait_ge(s_rzst, 16)
                sp.sem_inc(s_used, 8)
                with sp.Fori(0, B) as bt:
                    for u in range(2):
                        sp.wait_ge(s_used, bt * 8 + (4 * u + 4))
                        for k, (h0, n) in enumerate(((0, 8), (8, 4))):
                            rows = bass.ds(bt * NH + h0, n)
                            sp.dma_start(num[u][k][:, :], heads[rows, u, 0:HD, :]).then_inc(s_ld[u], 16)
                            sp.dma_start(inv[u][k][:, :],
                                         zheads[rows, u, :].unsqueeze(1).broadcast_to([n, HD, CHUNK])
                                         ).then_inc(s_ld[u], 16)

            @block.vector
            def _(dve):
                dve.wait_ge(s_z, 16)
                dve.reciprocal(rz[0:2 * B * NH, :], z[0:2 * B * NH, :]).then_inc(s_rz, 1)
                dve.wait_ge(s_w, 3 * 16)
                dve.tensor_tensor(res[:, :].rearrange("p (t f) -> p t f", t=TILES),
                                  res[:, :].rearrange("p (t f) -> p t f", t=TILES),
                                  bias[:, :].unsqueeze(1).broadcast_to([P, TILES, C]), ALU.add).then_inc(s_bias, 1)
                dve.wait_ge(s_bias, 1)
                with dve.Fori(0, B) as bt:
                    for u in range(2):
                        dve.wait_ge(s_ld[u], bt * 64 + 64)
                        for k in range(2):
                            dve.tensor_tensor(num[u][k][:, :], num[u][k][:, :], inv[u][k][:, :],
                                              ALU.mult).then_inc(s_at, 1)
                        for t in range(4):
                            n = bt * 8 + (4 * u + t)
                            dve.wait_ge(s_y, n + 1)
                            dve.tensor_tensor(res[:, ts(n, C)], res[:, ts(n, C)], yp[t % 2][:, 0:C],
                                              ALU.add).then_inc(s_add, 1)

            @block.tensor
            def _(pe):
                pe.wait_ge(s_w, 3 * 16)
                pe.sem_inc(s_add, 2)
                with pe.Fori(0, B) as bt:
                    for u in range(2):
                        pe.wait_ge(s_at, bt * 4 + (2 * u + 2))
                        for t in range(4):
                            n = bt * 8 + (4 * u + t)
                            pe.wait_ge(s_add, n + 1)
                            for k in range(2):
                                ins = pe.matmul(yp[t % 2][:, 0:C], num[u][k][:, t * P:(t + 1) * P], pw[k][:, :],
                                                start=k == 0, stop=k == 1)
                            ins.then_inc(s_y, 1)

            @block.scalar
            def _(act):
                with act.Fori(0, TILES) as n:
                    act.wait_ge(s_y, n + 1)
                    act.sem_inc(s_used, 1)


def gates(nc, name, xt, gate_w, experts, comb, iota, gate_b=None, add_bias=None):
    E8 = 8
    with Pool(nc, name) as m:
        gw = [m.sb("gw0", experts), m.sb("gw1", experts, parts=C1)]
        lg, top, idxf, pick = (m.sb(n, TILES * E8) for n in ("logits", "top", "idxf", "pick"))
        idx = m.sb("idx", TILES * E8, U32)
        one, w0, w1 = (m.sb(n, TILES) for n in ("one", "w0", "w1"))
        gb, lp = m.sb("gb", experts), m.ps("lp")
        s_w, s_l, s_chain, s_exp, s_x = m.sem("w"), m.sem("l"), m.sem("chain"), m.sem("exp"), m.sem("x")
        s_acc, s_top = m.sem("acc"), m.sem("top")
        b2 = m.sb("b2", experts * C) if add_bias else None

        def cube(t):
            return t[:, :].rearrange("p (t e) -> p t e", e=E8)

        def wide(t):
            return t[:, :].unsqueeze(2).broadcast_to([P, TILES, E8])

        loads = 2 + (gate_b is not None) + (add_bias is not None)
        with nc.Block() as block:
            @block.sync
            def _(sp):
                sp.dma_start(gw[0][:, :], gate_w[0:C0, :]).then_inc(s_w, 16)
                sp.dma_start(gw[1][:, :], gate_w[C0:C, :]).then_inc(s_w, 16)
                if gate_b is not None:
                    sp.dma_start(gb[:, :], gate_b.broadcast_to([P, experts])).then_inc(s_w, 16)
                if add_bias is not None:
                    sp.dma_start(b2[:, :], add_bias[1].broadcast_to([P, experts * C])).then_inc(s_w, 16)

            @block.tensor
            def _(pe):
                pe.wait_ge(s_w, loads * 16)
                for t in range(TILES):
                    for k, n in enumerate((C0, C1)):
                        ins = pe.matmul(lp[:, t * E8:t * E8 + experts], xt[k][0:n, t * P:(t + 1) * P], gw[k][:, :],
                                        start=k == 0, stop=k == 1)
                ins.then_inc(s_l, 1)

            @block.vector
            def _(dve):
                link = linker(dve, s_chain)
                dve.wait_ge(s_w, loads * 16)
                dve.wait_ge(s_l, 1)
                psum = lp[:, 0:TILES * E8].rearrange("p (t e) -> p t e", e=E8)[:, :, 0:experts]
                if gate_b is None:
                    link(dve.tensor_copy(cube(lg), psum))
                    link(dve.tensor_reduce(one[:, :], cube(lg), AX.X, ALU.max))
                    link(dve.tensor_tensor(cube(lg), cube(lg), wide(one), ALU.subtract))
                    dve.sem_inc(s_x, 1)
                    dve.wait_ge(s_exp, 1)
                    link(dve.tensor_reduce(one[:, :], cube(lg), AX.X, ALU.add))
                    link(dve.reciprocal(one[:, :], one[:, :]))
                    link(dve.tensor_tensor(cube(lg), cube(lg), wide(one), ALU.mult))
                else:
                    link(dve.memset(lg[:, :], -3.0e38))
                    link(dve.tensor_tensor(cube(lg)[:, :, 0:experts], psum,
                                           gb[:, :].unsqueeze(1).broadcast_to([P, TILES, experts]), ALU.add))
                for t in range(TILES):
                    cols = slice(t * E8, (t + 1) * E8)
                    dve.max(out=top[:, cols], in_=lg[:, cols]).then_inc(s_top, 1)
                dve.wait_ge(s_top, TILES)
                for t in range(TILES):
                    cols = slice(t * E8, (t + 1) * E8)
                    dve.max_index(idx[:, cols], top[:, cols], lg[:, cols]).then_inc(s_top, 1)
                dve.wait_ge(s_top, 2 * TILES)
                first, second = cube(top)[:, :, 0], cube(top)[:, :, 1]
                if gate_b is None:
                    link(dve.tensor_tensor(one[:, :], first, second, ALU.add))
                    link(dve.tensor_scalar(one[:, :], one[:, :], 1e-8, None, ALU.add))
                    link(dve.reciprocal(one[:, :], one[:, :]))
                    link(dve.tensor_tensor(w0[:, :], first, one[:, :], ALU.mult))
                    link(dve.tensor_tensor(w1[:, :], second, one[:, :], ALU.mult))
                else:
                    link(dve.tensor_tensor(w1[:, :], second, first, ALU.subtract))
                    dve.sem_inc(s_x, 1)
                    dve.wait_ge(s_exp, 1)
                    link(dve.tensor_scalar(one[:, :], w1[:, :], 1.0, None, ALU.add))
                    link(dve.reciprocal(w0[:, :], one[:, :]))
                    link(dve.tensor_tensor(w1[:, :], w1[:, :], w0[:, :], ALU.mult))
                link(dve.tensor_copy(idxf[:, :], idx[:, :]))
                experts_of = iota.unsqueeze(1).broadcast_to([P, TILES, E8])
                for k, wk in enumerate((w0, w1)):
                    dst = comb if k == 0 else pick
                    which = cube(idxf)[:, :, k:k + 1].broadcast_to([P, TILES, E8])
                    link(dve.tensor_tensor(cube(dst), experts_of, which, ALU.is_equal))
                    link(dve.tensor_tensor(cube(dst), cube(dst), wide(wk), ALU.mult))
                link(dve.tensor_tensor(comb[:, :], comb[:, :], pick[:, :], ALU.add))
                if add_bias is not None:
                    res = add_bias[0]
                    dve.sem_inc(s_acc, 8)
                    with dve.Fori(0, TILES // 8) as it:
                        for e in range(experts):
                            dve.wait_ge(s_acc, it * (8 * experts) + (8 * e + 8))
                            for j in range(8):
                                t = it * 8 + j
                                dve.scalar_tensor_tensor(out=res[:, ts(t, C)], in0=b2[:, e * C:(e + 1) * C],
                                                         scalar=comb[:, bass.ds(t * E8 + e, 1)],
                                                         in1=res[:, ts(t, C)],
                                                         op0=ALU.mult, op1=ALU.add).then_inc(s_acc, 1)
                    dve.wait_ge(s_acc, TILES * experts + 8)

            @block.scalar
            def _(act):
                act.wait_ge(s_x, 1)
                src = lg if gate_b is None else w1
                act.activation(src[:, :], src[:, :], ACT.Exp).then_inc(s_exp, 1)


W_SCALE = 64.0


def feed_forward(nc, name, parts, res, blocks, mt, w_up, w_down, gate_bank=None, b_up=None, comb=None,
                 b_down=None):
    gated = gate_bank is not None
    per_turn = 1 if blocks % 2 == 0 else 2
    turns = T // CHUNK // per_turn
    ring = 2 if gated else 4
    mats = (gate_bank, w_up) if gated else (w_up,)
    nm = len(mats)
    bw = mt * P
    hid = blocks * bw
    xa_hi, xa_lo, xb = parts
    assert per_turn * blocks * mt % ring == 0
    with Pool(nc, name) as m:
        ah = [m.sb(f"ah{i}", hid, F16) for i in range(nm)]
        al = [m.sb(f"al{i}", hid, F16) for i in range(nm)]
        bh = [m.sb(f"bh{i}", hid, F16) for i in range(nm)]
        bl = [m.sb(f"bl{i}", hid, F16, parts=C1) for i in range(nm)]
        raw_a = [[m.sb(f"ra{i}{r}", bw) for i in range(nm)] for r in range(2)]
        raw_b = [[m.sb(f"rb{i}{r}", bw) for i in range(nm)] for r in range(2)]
        down = m.sb("down", blocks * mt * C)
        bu = m.sb("bu", blocks * mt) if b_up is not None else None
        bd = m.sb("bd", C) if b_down is not None else None
        h = [m.sb(f"h{u}", mt * CHUNK) for u in range(2)]
        s_buf = [m.sb(f"s{u}", CHUNK) for u in range(2)] if gated else None
        ups = [[m.ps(f"u{i}{k}") for i in range(nm)] for k in range(ring)]
        yps = [[m.ps(f"y{u}{k}") for k in range(2)] for u in range(2)]
        s_raw = [m.sem(f"raw{r}") for r in range(2)]
        s_wh, s_wl, s_b, s_wd = m.sem("wh"), m.sem("wl"), m.sem("b"), m.sem("wd")
        s_up, s_s, s_h = m.sem("up"), m.sem("s"), m.sem("h")
        s_down, s_y, s_bias = m.sem("down"), m.sem("y"), m.sem("bias")
        n_b = (b_up is not None) + (b_down is not None)

        def unit(it, c, blk, k):
            return it * (per_turn * blocks * mt) + ((c * blocks + blk) * mt + k)

        def block_no(it, c, blk):
            return it * (per_turn * blocks) + (c * blocks + blk)

        def cut(blk):
            return slice(blk * bw, (blk + 1) * bw)

        with nc.Block() as block:
            @block.sync
            def _(sp):
                if b_up is not None:
                    sp.dma_start(bu[:, :], b_up).then_inc(s_b, 16)
                if b_down is not None:
                    sp.dma_start(bd[:, :], b_down.broadcast_to([P, C])).then_inc(s_b, 16)
                for blk in range(blocks):
                    r = blk % 2
                    if blk >= 2:
                        sp.wait_ge(s_wl, 2 * nm * (blk - 1))
                    for i, src in enumerate(mats):
                        sp.dma_start(raw_a[r][i][:, :], src[0:C0, cut(blk)]).then_inc(s_raw[r], 16)
                        for half in range(2):
                            sp.dma_start(raw_b[r][i][C1 * half:C1 * (half + 1), :],
                                         src[C0:C, cut(blk)]).then_inc(s_raw[r], 16)
                    sp.dma_start(down[:, blk * mt * C:(blk + 1) * mt * C].rearrange("p (k n) -> p k n", n=C),
                                 w_down[cut(blk), :].rearrange("(k p) n -> p k n", p=P)).then_inc(s_wd, 16)

            def run(engine, turn_of):
                turn_of(0, True)
                with engine.Fori(1, turns) as it:
                    turn_of(it, False)

            @block.tensor
            def _(pe):
                def rise(it, c, blk, first):
                    cols = ts(it * per_turn + c, CHUNK)
                    if first and c == 0:
                        pe.wait_ge(s_wl, 2 * nm * (blk + 1))
                    for k in range(mt):
                        pe.wait_ge(s_h, unit(it, c, blk, k) + 1)
                        n = (c * blocks + blk) * mt + k
                        w = slice((blk * mt + k) * P, (blk * mt + k + 1) * P)
                        for i in range(nm):
                            bank = ups[n % ring][i][:, :]
                            pe.matmul(bank, ah[i][:, w], xa_hi[:, cols], start=True, stop=False)
                            pe.matmul(bank, al[i][:, w], xa_hi[:, cols], start=False, stop=False)
                            pe.matmul(bank, ah[i][:, w], xa_lo[:, cols], start=False, stop=False)
                            pe.matmul(bank, bh[i][:, w], xb[:, cols], start=False, stop=False)
                            ins = pe.matmul(bank, bl[i][:, w], xb[0:C1, cols], start=False, stop=True)
                        ins.then_inc(s_up, 1)

                def fall(it, c, blk, first):
                    q = c * blocks + blk
                    if first and c == 0:
                        pe.wait_ge(s_wd, 16 * (blk + 1))
                    pe.wait_ge(s_h, unit(it, c, blk, mt - 1) + (1 + ring))
                    pe.wait_ge(s_y, block_no(it, c, blk) + 1)
                    for t in range(4):
                        for k in range(mt):
                            ins = pe.matmul(yps[q % 2][t // 2][:, (t % 2) * C:(t % 2 + 1) * C],
                                            h[q % 2][:, k * CHUNK + t * P:k * CHUNK + (t + 1) * P],
                                            down[:, (blk * mt + k) * C:(blk * mt + k + 1) * C],
                                            start=k == 0, stop=k == mt - 1)
                    ins.then_inc(s_down, 1)

                def one_turn(it, first):
                    last = None
                    for c in range(per_turn):
                        for blk in range(blocks):
                            rise(it, c, blk, first)
                            if last is not None:
                                fall(it, *last, first)
                            last = (c, blk)
                    fall(it, *last, first)

                pe.sem_inc(s_h, ring)
                pe.sem_inc(s_y, 2)
                run(pe, one_turn)

            @block.scalar
            def _(act):
                def split_high(blk):
                    act.wait_ge(s_raw[blk % 2], 16 * 3 * nm * (blk // 2 + 1))
                    for i in range(nm):
                        for raw, high in ((raw_a, ah), (raw_b, bh)):
                            act.activation(high[i][:, cut(blk)], raw[blk % 2][i][:, :], ACT.Identity,
                                           scale=W_SCALE).then_inc(s_wh, 1)

                def one_turn(it, first):
                    for c in range(per_turn):
                        for blk in range(blocks):
                            if first and c == 0 and blk + 1 < blocks:
                                split_high(blk + 1)
                            q = c * blocks + blk
                            if not gated:
                                act.wait_ge(s_down, block_no(it, c, blk) + 1)
                            for k in range(mt):
                                n = unit(it, c, blk, k)
                                i = q * mt + k
                                act.wait_ge(s_up, n + 1)
                                if gated:
                                    act.wait_ge(s_h, n + 1)
                                    act.activation(s_buf[i % 2][:, :], ups[i % ring][0][:, :],
                                                   ACT.Silu, scale=1.0 / W_SCALE).then_inc(s_s, 1)
                                else:
                                    act.activation(h[q % 2][:, k * CHUNK:(k + 1) * CHUNK], ups[i % ring][0][:, :],
                                                   ACT.Gelu, bias=bu[:, blk * mt + k:blk * mt + k + 1],
                                                   scale=1.0 / W_SCALE).then_inc(s_h, 1)

                split_high(0)
                if n_b:
                    act.wait_ge(s_b, n_b * 16)
                if not gated:
                    act.sem_inc(s_down, 2)
                run(act, one_turn)

            @block.vector
            def _(dve):
                def split_low(blk):
                    dve.wait_ge(s_wh, 2 * nm * (blk + 1))
                    for i in range(nm):
                        for raw, high, low, n in ((raw_a, ah, al, P), (raw_b, bh, bl, C1)):
                            dve.scalar_tensor_tensor(out=low[i][0:n, cut(blk)], in0=raw[blk % 2][i][0:n, :],
                                                     scalar=W_SCALE, in1=high[i][0:n, cut(blk)],
                                                     op0=ALU.mult, op1=ALU.subtract).then_inc(s_wl, 1)

                def collect(it, c, blk):
                    q = c * blocks + blk
                    dve.wait_ge(s_down, block_no(it, c, blk) + 3)
                    dve.wait_ge(s_y, block_no(it, c, blk) + 2)
                    for t in range(4):
                        tile = (it * per_turn + c) * 4 + t
                        y = yps[q % 2][t // 2][:, (t % 2) * C:(t % 2 + 1) * C]
                        dst = res[:, ts(tile, C)]
                        if comb is None:
                            ins = dve.tensor_tensor(dst, y, dst, ALU.add)
                        else:
                            ins = dve.scalar_tensor_tensor(out=dst, in0=y, scalar=comb[:, bass.ds(tile * 8 + blk, 1)],
                                                           in1=dst, op0=ALU.mult, op1=ALU.add)
                    ins.then_inc(s_y, 1)

                def one_turn(it, first):
                    last = None
                    for c in range(per_turn):
                        for blk in range(blocks):
                            if first and c == 0 and blk + 1 < blocks:
                                split_low(blk + 1)
                            q = c * blocks + blk
                            if gated:
                                dve.wait_ge(s_down, block_no(it, c, blk) + 1)
                                for k in range(mt):
                                    n = unit(it, c, blk, k)
                                    i = q * mt + k
                                    dve.wait_ge(s_s, n + 1)
                                    dve.scalar_tensor_tensor(out=h[q % 2][:, k * CHUNK:(k + 1) * CHUNK],
                                                             in0=ups[i % ring][1][:, :], scalar=1.0 / W_SCALE,
                                                             in1=s_buf[i % 2][:, :],
                                                             op0=ALU.mult, op1=ALU.mult).then_inc(s_h, 1)
                            if last is not None:
                                collect(it, *last)
                            last = (c, blk)
                    collect(it, *last)

                split_low(0)
                if bd is not None:
                    dve.wait_ge(s_b, n_b * 16)
                    dve.tensor_tensor(res[:, :].rearrange("p (t f) -> p t f", t=TILES),
                                      res[:, :].rearrange("p (t f) -> p t f", t=TILES),
                                      bd[:, :].unsqueeze(1).broadcast_to([P, TILES, C]), ALU.add).then_inc(s_bias, 1)
                    dve.wait_ge(s_bias, 1)
                if gated:
                    dve.sem_inc(s_down, 2)
                run(dve, one_turn)
                dve.wait_ge(s_y, T // CHUNK * blocks + 2)


def turn(nc, name, src, parts, ident):
    xa_hi, xa_lo, xb = parts
    with Pool(nc, name) as m:
        t0 = [m.ps(f"t0{u}") for u in range(2)]
        t1 = [m.ps(f"t1{u}") for u in range(2)]
        s_t, s_hi, s_lo = m.sem("turned"), m.sem("hi"), m.sem("lo")
        with nc.Block() as block:
            @block.tensor
            def _(pe):
                for n in range(TILES // 4):
                    if n >= 2:
                        pe.wait_ge(s_lo, 2 * n - 2)
                    for j in range(4):
                        t = 4 * n + j
                        pe.transpose(t0[n % 2][:, j * P:(j + 1) * P], src[:, t * C:t * C + C0], ident)
                        ins = pe.transpose(t1[n % 2][0:C1, j * P:(j + 1) * P], src[:, t * C + C0:(t + 1) * C], ident)
                    ins.then_inc(s_t, 1)

            @block.scalar
            def _(act):
                for n in range(TILES // 4):
                    act.wait_ge(s_t, n + 1)
                    cols = slice(n * CHUNK, (n + 1) * CHUNK)
                    act.activation(xa_hi[:, cols], t0[n % 2][:, :], ACT.Identity).then_inc(s_hi, 1)
                    act.activation(xb[0:C1, cols], t1[n % 2][0:C1, :], ACT.Identity).then_inc(s_hi, 1)

            @block.vector
            def _(dve):
                for n in range(TILES // 4):
                    cols = slice(n * CHUNK, (n + 1) * CHUNK)
                    dve.wait_ge(s_hi, 2 * n + 2)
                    dve.tensor_tensor(xa_lo[:, cols], t0[n % 2][:, :], xa_hi[:, cols], ALU.subtract).then_inc(s_lo, 1)
                    dve.tensor_tensor(xb[C1:P, cols], t1[n % 2][0:C1, :], xb[0:C1, cols],
                                      ALU.subtract).then_inc(s_lo, 1)


def build(nc, a, out, stop=99):
    with ExitStack() as ctx:
        def sb(name, width, dt=F32, parts=P):
            return ctx.enter_context(nc.sbuf_tensor(name, [parts, width], dt))

        x = sb("x", TILES * C)
        y = sb("y", TILES * C)
        vt = sb("vt", TILES * C)
        xt = [sb("xt0", T), sb("xt1", T)]
        ident, ident16 = sb("ident", P), sb("ident16", P, F16)
        iota, cols = sb("iota", 8), sb("cols", 8)
        comb = sb("comb", TILES * 8)
        scratch = {
            "qk": nc.dram_tensor("qk_parts", [2, B * NH, 2, HD, L], F16, kind="Internal").ap(),
            "rel": nc.dram_tensor("rel_parts", [B * NH, 2, 2, 2, QSIDE, L], F16, kind="Internal").ap(),
            "o": nc.dram_tensor("o_sums", [B * NH // 2, P, CHUNK], F32, kind="Internal").ap(),
            "rz": nc.dram_tensor("rz_rows", [2 * B * NH, CHUNK], F32, kind="Internal").ap(),
        }

        with Pool(nc, "start") as m:
            s_in = m.sem("in")
            with nc.Block() as block:
                @block.sync
                def _(sp):
                    sp.dma_start(x[:, :].rearrange("p (t f) -> p t f", t=TILES),
                                 a["x"].rearrange("(t p) f -> p t f", p=P)).then_inc(s_in, 16)
                    sp.dma_start(ident[:, :], a["ident"]).then_inc(s_in, 16)
                    sp.dma_start(ident16[:, :], a["ident16"]).then_inc(s_in, 16)
                    sp.dma_start(iota[:, :], a["iota"].broadcast_to([P, 8])).then_inc(s_in, 16)
                    for k, key in enumerate(("ln1_g", "ln1_b", "ln2_g", "ln2_b")):
                        sp.dma_start(cols[:, 2 * k:2 * k + 1], a[key][0:C0, :]).then_inc(s_in, 16)
                        sp.dma_start(cols[0:C1, 2 * k + 1:2 * k + 2], a[key][C0:C, :]).then_inc(s_in, 16)
                    sp.wait_ge(s_in, 12 * 16)

        idn = ident[:, :]
        vt16 = vt[:, :].bitcast(F16)
        parts = [vt16[:, T * k:T * (k + 1)] for k in range(3)]
        room = [t[:, 0:T].bitcast(F16) for t in (xt[0], xt[1], y)]
        stages = []

        def conv(l):
            w = {k: a[f"{l}_{k}"] for k in ("wqk", "bqk", "wv", "bv", "rel_h", "rel_w")}
            w["own"] = a["own"]
            stages.append(lambda: layer_norm(nc, l + "ln", x, 1e-6, turned_to=xt, ident=idn))
            stages.append(lambda: qkv(nc, l + "qkv", xt, vt, w, scratch))
            stages.append(lambda: attention(nc, l + "att", vt, True, scratch, a["hot"], ident16[:, :], room))
            stages.append(lambda: project(nc, l + "proj", x, a[f"{l}_wo"], a[f"{l}_bo"], scratch))

        conv("c0")
        stages.append(lambda: layer_norm(nc, "f0ln", x, 1e-5, turned_to=xt, ident=idn, parts=parts))
        stages.append(lambda: gates(nc, "f0gate", xt, a["f0_gate"], 8, comb, iota[:, :]))
        stages.append(lambda: feed_forward(nc, "f0", parts, x, 8, 3, a["f0_up"], a["f0_down"], gate_bank=a["f0_bank"], comb=comb))
        conv("c1")
        stages.append(lambda: layer_norm(nc, "u", x, 1e-5, store=y))
        stages.append(lambda: layer_norm(nc, "h", y, 1e-5, turned_to=xt, gain=cols[:, 0:2], shift=cols[:, 2:4], ident=idn))
        w1 = {k: a[f"f1_{k}"] for k in ("wqk", "bqk", "wv", "bv")}
        stages.append(lambda: qkv(nc, "f1qkv", xt, vt, w1, scratch))
        stages.append(lambda: attention(nc, "f1att", vt, False, scratch, None, ident16[:, :]))
        stages.append(lambda: project(nc, "f1proj", y, a["f1_wo"], a["f1_bo"], scratch))
        stages.append(lambda: turn(nc, "f1turn", y, parts, idn))
        stages.append(lambda: feed_forward(nc, "mlp", parts, y, 1, 6, a["mlp_w1"], a["mlp_w2"], b_up=a["mlp_b1"], b_down=a["mlp_b2"]))
        stages.append(lambda: layer_norm(nc, "xm", y, 1e-5, turned_to=xt, gain=cols[:, 4:6], shift=cols[:, 6:8], ident=idn, parts=parts))
        stages.append(lambda: gates(nc, "f1gate", xt, a["f1_gate"], 4, comb, iota[:, :], gate_b=a["f1_gate_b"],
                                    add_bias=(y, a["exp_b2"])))
        stages.append(lambda: feed_forward(nc, "moe", parts, y, 4, 6, a["exp_w1"], a["exp_w2"], b_up=a["exp_b1"], comb=comb))
        for s in stages[:stop]:
            s()

        with Pool(nc, "end") as m:
            s_sum, s_out = m.sem("sum"), m.sem("out")
            with nc.Block() as block:
                @block.vector
                def _(dve):
                    dve.tensor_tensor(x[:, :], x[:, :], y[:, :] if stop > len(stages) else x[:, :], ALU.add).then_inc(s_sum, 1)

                @block.sync
                def _(sp):
                    sp.wait_ge(s_sum, 1)
                    sp.dma_start(out.rearrange("(t p) f -> p t f", p=P),
                                 x[:, :].rearrange("p (t f) -> p t f", t=TILES)).then_inc(s_out, 16)
                    sp.wait_ge(s_out, 16)


def _attn(inputs, l, qkv_w, qkv_b, proj_w, proj_b):
    w, bias = np.asarray(inputs[qkv_w]), np.asarray(inputs[qkv_b])
    q, k, v = w[0:C], w[C:2 * C], w[2 * C:]
    bq, bk = bias[0:C], bias[C:2 * C]
    groups = [slice(GW * g, GW * (g + 1)) for g in range(GROUPS)]
    return {
        f"{l}_wqk": np.concatenate([np.concatenate([q[s], k[s]]) for s in groups]).T,
        f"{l}_bqk": np.stack([np.concatenate([bq[s], bk[s]]) for s in groups], axis=1),
        f"{l}_wv": v.T,
        f"{l}_bv": bias[2 * C:][None],
        f"{l}_wo": np.asarray(inputs[proj_w]).T,
        f"{l}_bo": np.asarray(inputs[proj_b])[None],
    }


def host_arrays(inputs):
    i = {k: np.asarray(v) for k, v in inputs.items()}
    a = {"x": i["x"].reshape(B, 2, QSIDE, 2, QSIDE, C).transpose(0, 1, 3, 2, 4, 5).reshape(T, C)}
    for l, n in (("c0", "L0_conv"), ("c1", "L1_conv")):
        a.update(_attn(i, l, f"{n}_qkv_w", f"{n}_qkv_b", f"{n}_proj_w", f"{n}_proj_b"))
        a[f"{l}_rel_h"] = i[f"{n}_rel_pos_h"][::-1].T
        a[f"{l}_rel_w"] = i[f"{n}_rel_pos_w"][::-1].T
    a.update(_attn(i, "f1", "L1_ffn_in_w", "L1_ffn_in_b", "L1_ffn_out_w", "L1_ffn_out_b"))
    wide = lambda w: w.transpose(1, 0, 2).reshape(C, -1)
    a["f0_gate"] = i["L0_ffn_gate_w"].T
    a["f0_bank"], a["f0_up"] = wide(i["L0_ffn_gate_bank"]), wide(i["L0_ffn_up_bank"])
    a["f0_down"] = i["L0_ffn_down_bank"].reshape(-1, C)
    for k in ("ln1_g", "ln1_b", "ln2_g", "ln2_b"):
        a[k] = i[f"L1_ffn_{k}"][:, None]
    a["mlp_w1"], a["mlp_w2"] = i["L1_ffn_mlp_w1"], i["L1_ffn_mlp_w2"]
    a["mlp_b1"] = i["L1_ffn_mlp_b1"].reshape(-1, P).T
    a["mlp_b2"] = i["L1_ffn_mlp_b2"][None]
    a["f1_gate"] = i["L1_ffn_gate_w"].T
    a["f1_gate_b"] = i["L1_ffn_gate_b"][None]
    a["exp_w1"] = wide(i["L1_ffn_exp_w1"])
    a["exp_b1"] = i["L1_ffn_exp_b1"].reshape(-1, P).T
    a["exp_w2"] = i["L1_ffn_exp_w2"].reshape(-1, C)
    a["exp_b2"] = i["L1_ffn_exp_b2"].reshape(1, -1)
    a["ident"] = np.eye(P, dtype=np.float32)
    a["ident16"] = np.eye(P, dtype=np.float16)
    a["iota"] = np.arange(8, dtype=np.float32)[None]
    a["own"] = (np.arange(GW)[:, None] // HD == np.arange(GH)[None]).astype(np.float32) * np.float32(HD ** 0.5)
    token = np.arange(L)
    row, column = (np.equal.outer(np.arange(QSIDE), t) for t in (token % Q // QSIDE, token % QSIDE))
    a["hot"] = np.concatenate([row, row, column, column]).astype(np.float16)
    return {k: np.ascontiguousarray(v) for k, v in a.items()}


def kernel(**inputs):
    import concourse.bacc as bacc
    from concourse.bass_utils import run_bass_kernel_spmd

    nc = bacc.Bacc("TRN2", target_bir_lowering=False, num_devices=1)
    arrays = host_arrays(inputs)
    aps = {k: nc.dram_tensor(f"in_{k}", v.shape, mybir.dt.from_np(v.dtype), kind="ExternalInput").ap()
           for k, v in arrays.items()}
    out = nc.dram_tensor("out_x", (T, C), F32, kind="ExternalOutput").ap()
    build(nc, aps, out)
    r = run_bass_kernel_spmd(nc, [{f"in_{k}": v for k, v in arrays.items()}], core_ids=[0])
    quarters = r.results[0]["out_x"].reshape(B, 2, 2, QSIDE, QSIDE, C)
    return quarters.transpose(0, 1, 3, 2, 4, 5).reshape(B, SIDE, SIDE, C)
```

```python
from contextlib import ExitStack

import numpy as np

import concourse.bass as bass
from concourse import mybir

F32 = mybir.dt.float32
F16 = mybir.dt.float16
U32 = mybir.dt.uint32
ALU = mybir.AluOpType
ACT = mybir.ActivationFunctionType
AX = mybir.AxisListType

B, SIDE, C, NH, HD = 4, 32, 192, 12, 16
L = SIDE * SIDE
T = B * L
P = 128
TILES = T // P
CHUNK = 512
C0, C1 = P, C - P
GROUPS = 3
GH = NH // GROUPS
GW = GH * HD
KT = L // P
QSIDE = SIDE // 2
Q = QSIDE * QSIDE
PAIRS = B * NH // 2
EARLY_HEADS = (B - 1) * NH
RING = 3

R_REL = 0
R_QK = 64
R_MAX = 96
R_LOW = 97
R_END = R_LOW + HD
QUARTERS = 4


def ts(i, n):
    return bass.ts(i, n)


class Pool:

    def __init__(self, nc, name):
        self.nc, self.name, self.stack, self.sems = nc, name, ExitStack(), []

    def __enter__(self):
        return self

    def __exit__(self, *what):
        if what[0] is None:
            nc, sems = self.nc, self.sems
            with nc.Block() as block:
                @block.sync
                def _(sp):
                    for s in sems:
                        sp.sem_clear(s)
        self.stack.close()

    def sb(self, name, width, dt=F32, parts=P):
        return self.stack.enter_context(self.nc.sbuf_tensor(f"{self.name}_{name}", [parts, width], dt))

    def ps(self, name, width=CHUNK):
        return self.stack.enter_context(self.nc.psum_tensor(f"{self.name}_{name}", [P, width], F32))

    def sem(self, name):
        s = self.stack.enter_context(self.nc.semaphore(f"{self.name}_{name}"))
        self.sems.append(s)
        return s


def linker(engine, sem):
    count = [0]

    def link(ins):
        count[0] += 1
        ins.then_inc(sem, 1)
        engine.wait_ge(sem, count[0])

    return link


def layer_norm(nc, name, src, eps, stats, turned_to, ident, gain=None, shift=None, parts=None, inner=None):
    with Pool(nc, name) as m:
        mean, mdiff, vsum, var, std, rstd = (m.sb(n, TILES) for n in ("mean", "mdiff", "vsum", "var", "std", "rstd"))
        s_stats, s_chain, s_std = m.sem("stats"), m.sem("chain"), m.sem("std")
        s_norm, s_turned, s_evac = m.sem("norm"), m.sem("turned"), m.sem("evac")
        s_stored = m.sem("stored")
        s_hi, s_lo, s_f32 = m.sem("hi"), m.sem("lo"), m.sem("f32")
        nrm = [m.sb(f"nrm{u}", 4 * C) for u in range(2)]
        t0 = [m.ps(f"t0{u}") for u in range(2)]
        t1 = [m.ps(f"t1{u}") for u in range(2)]
        MOMENTS, VAR = 12, 6
        with nc.Block() as block:
            @block.vector
            def _(dve):
                half = stats[:, :].rearrange("p (t s) -> p s t", s=6)
                link = linker(dve, s_chain)

                def moments(turn):
                    link(dve.tensor_tensor(mean[:, :], half[:, 1, :], half[:, 4, :], ALU.add))
                    link(dve.tensor_tensor(mdiff[:, :], half[:, 1, :], half[:, 4, :], ALU.subtract))
                    link(dve.tensor_tensor(vsum[:, :], half[:, 2, :], half[:, 5, :], ALU.add))
                    link(dve.tensor_tensor(mdiff[:, :], mdiff[:, :], mdiff[:, :], ALU.mult))
                    link(dve.tensor_scalar(vsum[:, :], vsum[:, :], 1.0 / C, eps, ALU.mult, ALU.add))
                    link(dve.scalar_tensor_tensor(out=var[:, :], in0=mdiff[:, :], scalar=0.25, in1=vsum[:, :],
                                                  op0=ALU.mult, op1=ALU.add))
                    link(dve.tensor_scalar(mean[:, :], mean[:, :], 0.5, None, ALU.mult))
                    dve.wait_ge(s_std, turn + 1)
                    link(dve.reciprocal(rstd[:, :], std[:, :]))
                    link(dve.tensor_tensor(std[:, :], rstd[:, :], rstd[:, :], ALU.mult))
                    link(dve.tensor_tensor(std[:, :], std[:, :], var[:, :], ALU.mult))
                    link(dve.tensor_scalar(std[:, :], std[:, :], -0.5, 1.5, ALU.mult, ALU.add))
                    link(dve.tensor_tensor(rstd[:, :], rstd[:, :], std[:, :], ALU.mult))

                moments(0)
                if inner is not None:
                    with dve.Fori(0, TILES // 8) as it:
                        for j in range(8):
                            t = it * 8 + j
                            dve.tensor_scalar(src[:, ts(t, C)], inner[:, ts(t, C)], mean[:, ts(t, 1)],
                                              rstd[:, ts(t, 1)], ALU.subtract, ALU.mult).then_inc(s_stored, 1)
                    dve.wait_ge(s_stored, TILES)
                    with dve.Fori(0, TILES // 8) as it:
                        for j in range(8):
                            t = it * 8 + j
                            dve.bn_stats(stats[:, ts(t, 6)], src[:, ts(t, C)]).then_inc(s_stats, 1)
                    dve.wait_ge(s_stats, TILES)
                    moments(1)
                dve.sem_inc(s_turned, 2)
                with dve.Fori(0, TILES // 8) as it:
                    for u in range(2):
                        dve.wait_ge(s_turned, it * 2 + (u + 1))
                        for j in range(4):
                            t = it * 8 + (4 * u + j)
                            dve.tensor_scalar(nrm[u][:, j * C:(j + 1) * C], src[:, ts(t, C)],
                                              mean[:, ts(t, 1)], rstd[:, ts(t, 1)],
                                              ALU.subtract, ALU.mult).then_inc(s_norm, 1)
                if parts is not None:
                    xa_hi, xa_lo, xb = parts
                    with dve.Fori(0, TILES // 8) as it:
                        for u in range(2):
                            dve.wait_ge(s_evac, it * 4 + (2 * u + 6))
                            cols = ts(it * 2 + u, CHUNK)
                            dve.tensor_tensor(xa_lo[:, cols], turned_to[0][:, cols], xa_hi[:, cols],
                                              ALU.subtract).then_inc(s_lo, 1)
                            dve.tensor_tensor(xb[C1:P, cols], turned_to[1][0:C1, cols], xb[0:C1, cols],
                                              ALU.subtract).then_inc(s_lo, 1)
                    dve.wait_ge(s_lo, TILES // 2)

            @block.scalar
            def _(act):
                for turn in range(1 if inner is None else 2):
                    act.wait_ge(s_chain, MOMENTS * turn + VAR)
                    act.activation(std[:, :], var[:, :], ACT.Sqrt).then_inc(s_std, 1)
                with act.Fori(0, TILES // 8) as it:
                    for u in range(2):
                        act.wait_ge(s_turned, it * 2 + (u + 3))
                        cols = ts(it * 2 + u, CHUNK)
                        for k, (tile, n) in enumerate(((t0[u], C0), (t1[u], C1))):
                            scale = 1.0 if gain is None else gain[0:n, k:k + 1]
                            bias = 0.0 if shift is None else shift[0:n, k:k + 1]
                            act.activation(turned_to[k][0:n, cols], tile[0:n, :], ACT.Identity,
                                           bias=bias, scale=scale).then_inc(s_f32, 1)
                            if parts is not None:
                                act.activation(parts[2 * k][0:n, cols], tile[0:n, :], ACT.Identity,
                                               bias=bias, scale=scale).then_inc(s_hi, 1)
                        act.wait_ge(s_f32, it * 4 + (2 * u + 2))
                        if parts is not None:
                            act.wait_ge(s_hi, it * 4 + (2 * u + 2))
                        act.sem_inc(s_evac, 2)

            @block.tensor
            def _(pe):
                pe.sem_inc(s_evac, 4)
                with pe.Fori(0, TILES // 8) as it:
                    for u in range(2):
                        pe.wait_ge(s_norm, it * 8 + (4 * u + 4))
                        pe.wait_ge(s_evac, it * 4 + (2 * u + 2))
                        for j in range(4):
                            pe.transpose(t0[u][:, j * P:(j + 1) * P], nrm[u][:, j * C:j * C + C0], ident)
                            ins = pe.transpose(t1[u][0:C1, j * P:(j + 1) * P],
                                               nrm[u][:, j * C + C0:(j + 1) * C], ident)
                        ins.then_inc(s_turned, 1)


def qkv(nc, name, xt, vt, w, scratch):
    rel = "rel_h" in w
    with Pool(nc, name) as m:
        wqk = [m.sb("wqk0", 2 * C), m.sb("wqk1", 2 * C, parts=C1)]
        wv = [m.sb("wv0", C), m.sb("wv1", C, parts=C1)]
        bqk, bv, scale = m.sb("bqk", GROUPS), m.sb("bv", C), m.sb("scale", 1)
        qt = m.sb("qt", GROUPS * T)
        hi = [m.sb(f"hi{u}", L, F16) for u in range(2)]
        lo = [m.sb(f"lo{u}", L, F16) for u in range(2)]
        qp = [m.ps(f"qp{u}") for u in range(2)]
        vp = [m.ps(f"vp{u}") for u in range(2)]
        rp = [m.ps(f"rp{u}") for u in range(4)]
        s_w, s_wv, s_tab, s_init, s_tabs = m.sem("w"), m.sem("wv"), m.sem("tab"), m.sem("init"), m.sem("tabs")
        s_qk, s_qt, s_hi, s_lo = m.sem("qk"), m.sem("qt"), m.sem("hi"), m.sem("lo")
        s_st = [m.sem(f"st{u}") for u in range(2)]
        s_v, s_vt = m.sem("v"), m.sem("vt")
        s_rel, s_rhi, s_rlo = m.sem("rel"), m.sem("rhi"), m.sem("rlo")
        s_rst = [m.sem(f"rst{u}") for u in range(2)]
        if rel:
            raw = [m.sb(f"raw{k}", 2 * SIDE - 1, parts=GW) for k in range(2)]
            tab = [m.sb(f"tab{k}", (2 * SIDE - 1) * GH) for k in range(2)]
            own = m.sb("own", GH, parts=GW)
            rhi = [m.sb(f"rhi{k}", T, F16) for k in range(2)]
            rlo = [m.sb(f"rlo{k}", T, F16) for k in range(2)]
        vt4 = vt[:, :].rearrange("p (a k f) -> p a k f", a=PAIRS, k=KT)
        with nc.Block() as block:
            @block.sync
            def _(sp):
                sp.dma_start(wqk[0][:, :], w["wqk"][0:C0, :]).then_inc(s_w, 16)
                sp.dma_start(wqk[1][:, :], w["wqk"][C0:C, :]).then_inc(s_w, 16)
                sp.dma_start(bqk[:, :], w["bqk"]).then_inc(s_w, 16)
                sp.dma_start(wv[0][:, :], w["wv"][0:C0, :]).then_inc(s_wv, 16)
                sp.dma_start(wv[1][:, :], w["wv"][C0:C, :]).then_inc(s_wv, 16)
                sp.dma_start(bv[:, :], w["bv"].broadcast_to([P, C])).then_inc(s_wv, 16)
                if rel:
                    for k, key in enumerate(("rel_h", "rel_w")):
                        for h in range(GH):
                            sp.dma_start(raw[k][h * HD:(h + 1) * HD, :], w[key]).then_inc(s_tab, 16)
                    sp.dma_start(own[:, :], w["own"]).then_inc(s_tab, 16)
                with sp.Fori(0, 2) as it:
                    for g2 in range(6):
                        u = g2 % 2
                        n = it * 12 + 2 * g2
                        sp.wait_ge(s_hi, n + 2)
                        sp.wait_ge(s_lo, n + 2)
                        row = (it * 6 + g2) * GH
                        for s in range(2):
                            for part, buf in enumerate((hi[u], lo[u])):
                                sp.dma_start(scratch["qk"][s, bass.ds(row, GH), part, :, :],
                                             buf[GW * s:GW * (s + 1), :]).then_inc(s_st[u], 16)
                if rel:
                    for g in range(GROUPS):
                        for k in range(2):
                            sp.wait_ge(s_rlo, g * 16 + (8 * k + 8 + 4))
                            for b in range(B):
                                for part, buf in enumerate((rhi[k], rlo[k])):
                                    for half in range(2):
                                        rows = scratch["rel"][g * GH + b * NH:(g + 1) * GH + b * NH, k, half, part]
                                        sp.dma_start(rows.rearrange("h r n -> r h n"),
                                                     buf[C1 * half:C1 * (half + 1), b * L:(b + 1) * L]
                                                     ).then_inc(s_rst[k], 16)
                for u in range(2):
                    sp.wait_ge(s_st[u], 64 * 7)
                    if rel:
                        sp.wait_ge(s_rst[u], 256 * (GROUPS + 1))

            @block.gpsimd
            def _(pool):
                pool.memset(scale[0:GW, :], float(HD) ** -0.5).then_inc(s_init, 1)
                pool.memset(scale[GW:P, :], 1.0).then_inc(s_init, 1)
                with pool.Fori(0, 2) as it:
                    for g2 in range(6):
                        u = g2 % 2
                        pool.wait_ge(s_st[u], it * 192 + (g2 // 2 + 1) * 64)
                        for half in range(2):
                            n = it * 12 + (2 * g2 + half)
                            pool.wait_ge(s_hi, n + 1)
                            cols = bass.ds((it * 2 + g2 // 3) * L + ((g2 % 3) * T + half * CHUNK), CHUNK)
                            pool.tensor_tensor(lo[u][:, half * CHUNK:(half + 1) * CHUNK], qt[:, cols],
                                               hi[u][:, half * CHUNK:(half + 1) * CHUNK],
                                               ALU.subtract).then_inc(s_lo, 1)

            @block.tensor
            def _(pe):
                pe.wait_ge(s_w, 3 * 16)
                pe.sem_inc(s_qt, 2)
                with pe.Fori(0, 2) as it:
                    for g2 in range(6):
                        g = g2 % 3
                        for half in range(2):
                            n = it * 12 + (2 * g2 + half)
                            cols = bass.ds((it * 2 + g2 // 3) * L + half * CHUNK, CHUNK)
                            pe.wait_ge(s_qt, n + 1)
                            pe.matmul(qp[half][:, :], wqk[0][:, g * P:(g + 1) * P], xt[0][:, cols],
                                      start=True, stop=False)
                            pe.matmul(qp[half][:, :], wqk[1][:, g * P:(g + 1) * P], xt[1][0:C1, cols],
                                      start=False, stop=True).then_inc(s_qk, 1)
                if rel:
                    pe.wait_ge(s_tabs, 4)
                    pe.wait_ge(s_qt, 24 + 2)
                    pe.sem_inc(s_rlo, 4)
                    with pe.Fori(0, GROUPS) as g:
                        for k in range(2):
                            for qq in range(8):
                                pe.wait_ge(s_rlo, g * 16 + (8 * k + qq + 1))
                                for j in range(4):
                                    r = 4 * qq + j
                                    table = tab[k][:, (SIDE - 1 - r) * GH:(2 * SIDE - 1 - r) * GH]
                                    q = qt[:, ts(g, T)]
                                    if k == 0:
                                        q = q.rearrange("p (b u s y x) -> p u y b s x", b=B, u=2, s=2, y=QSIDE)[
                                            :, r // QSIDE, r % QSIDE]
                                        out = rp[qq % 4][:, :].rearrange("p (b s j x) -> p j b s x", b=B, s=2, j=4)[:, j]
                                    else:
                                        q = q.rearrange("p (n s y x) -> p s x n y", s=2, y=QSIDE, x=QSIDE)[
                                            :, r // QSIDE, r % QSIDE]
                                        out = rp[qq % 4][:, j * P:(j + 1) * P].rearrange("p (n y) -> p n y", y=QSIDE)
                                    ins = pe.matmul(out, table, q, start=True, stop=True)
                                ins.then_inc(s_rel, 1)
                pe.wait_ge(s_wv, 3 * 16)
                for t in range(TILES):
                    if t >= 2:
                        pe.wait_ge(s_vt, t - 1)
                    pe.matmul(vp[t % 2][:, 0:C], xt[0][:, t * P:(t + 1) * P], wv[0][:, :], start=True, stop=False)
                    pe.matmul(vp[t % 2][:, 0:C], xt[1][0:C1, t * P:(t + 1) * P], wv[1][:, :],
                              start=False, stop=True).then_inc(s_v, 1)

            @block.vector
            def _(dve):
                dve.wait_ge(s_w, 3 * 16)
                dve.wait_ge(s_init, 2)
                with dve.Fori(0, 2) as it:
                    for g2 in range(6):
                        for half in range(2):
                            n = it * 12 + (2 * g2 + half)
                            dve.wait_ge(s_qk, n + 1)
                            cols = bass.ds((it * 2 + g2 // 3) * L + ((g2 % 3) * T + half * CHUNK), CHUNK)
                            dve.tensor_scalar(qt[:, cols], qp[half][:, :], bqk[:, g2 % 3:g2 % 3 + 1],
                                              scale[:, 0:1], ALU.add, ALU.mult).then_inc(s_qt, 1)
                if rel:
                    dve.wait_ge(s_tab, 9 * 16)
                    for k in range(2):
                        dims = [GW, 2 * SIDE - 1, GH]
                        dve.memset(tab[k][GW:P, :], 0.0).then_inc(s_tabs, 1)
                        dve.tensor_tensor(tab[k][0:GW, :].rearrange("p (i h) -> p i h", h=GH),
                                          raw[k][:, :].unsqueeze(2).broadcast_to(dims),
                                          own[:, :].unsqueeze(1).broadcast_to(dims), ALU.mult).then_inc(s_tabs, 1)
                    with dve.Fori(0, GROUPS) as g:
                        for k in range(2):
                            for qq in range(8):
                                n = g * 16 + (8 * k + qq)
                                dve.wait_ge(s_rhi, n + 1)
                                src, out, high = rel_views(rp[qq % 4], rlo[k], rhi[k], k, qq)
                                dve.tensor_tensor(out, src, high, ALU.subtract).then_inc(s_rlo, 1)
                dve.wait_ge(s_wv, 3 * 16)
                for t in range(TILES):
                    dve.wait_ge(s_v, t + 1)
                    b, kt = t // KT, t % KT
                    dve.tensor_tensor(vt4[:, NH // 2 * b:NH // 2 * (b + 1), kt, :],
                                      vp[t % 2][:, 0:C].rearrange("p (g f) -> p g f", f=2 * HD),
                                      bv[:, :].rearrange("p (g f) -> p g f", f=2 * HD),
                                      ALU.add).then_inc(s_vt, 1)
                dve.wait_ge(s_vt, TILES)

            @block.scalar
            def _(act):
                for u in range(2):
                    act.sem_inc(s_st[u], 64)
                with act.Fori(0, 2) as it:
                    for g2 in range(6):
                        u = g2 % 2
                        act.wait_ge(s_st[u], it * 192 + (g2 // 2 + 1) * 64)
                        if g2:
                            act.wait_ge(s_lo, it * 12 + 2 * g2)
                        for half in range(2):
                            n = it * 12 + (2 * g2 + half)
                            act.wait_ge(s_qt, n + 3)
                            cols = bass.ds((it * 2 + g2 // 3) * L + ((g2 % 3) * T + half * CHUNK), CHUNK)
                            act.activation(hi[u][:, half * CHUNK:(half + 1) * CHUNK], qt[:, cols],
                                           ACT.Identity).then_inc(s_hi, 1)
                if not rel:
                    return
                for k in range(2):
                    act.sem_inc(s_rst[k], 256)
                with act.Fori(0, GROUPS) as g:
                    for k in range(2):
                        act.wait_ge(s_rst[k], g * 256 + 256)
                        for qq in range(8):
                            n = g * 16 + (8 * k + qq)
                            act.wait_ge(s_rel, n + 1)
                            src, out, _ = rel_views(rp[qq % 4], rhi[k], rhi[k], k, qq)
                            act.activation(out, src, ACT.Identity).then_inc(s_rhi, 1)


def rel_views(bank, part, high, k, qq):
    half, first = qq // 4, qq % 4 * 4
    if k == 0:
        src = bank[:, :].rearrange("p (b s m) -> p b s m", b=B, s=2)
        where = [t[:, :].rearrange("p (b u s m) -> p u b s m", b=B, u=2, s=2)[
            :, half, :, :, first * QSIDE:(first + 4) * QSIDE] for t in (part, high)]
    else:
        src = bank[:, :].rearrange("p (j n y) -> p j n y", j=4, y=QSIDE)
        where = [t[:, :].rearrange("p (n s y x) -> p s x n y", s=2, y=QSIDE, x=QSIDE)[
            :, half, first:first + 4, :, :] for t in (part, high)]
    return src, where[0], where[1]


def attention(nc, name, vt, rel, scratch, hot, ident16, room=None):
    with Pool(nc, name) as m:
        versions = QUARTERS if rel else 1
        qa = room or [m.sb(f"qa{u}", 2 * L, F16) for u in range(RING)]
        ka = [m.sb(f"ka{u}", 2 * L, F16) for u in range(RING)]
        vs = [m.sb(f"vs{u}", 2 * KT * 32) for u in range(RING)]
        osb = [m.sb(f"o{u}", CHUNK) for u in range(RING)]
        pr = [[m.sb(f"p{h}{k}", L) for k in range(2)] for h in range(2)]
        mx = m.sb("mx", 2 * KT * 2)
        m32, m16 = m.sb("m32", 2 * KT), m.sb("m16", 2 * KT, F16)
        z, rz = m.sb("z", CHUNK), m.sb("rz", CHUNK)
        s_z, s_rz, s_rzst = m.sem("z"), m.sem("rz"), m.sem("rzst")
        sps = [m.ps(f"s{h}", L) for h in range(2)]
        mps = [m.ps(f"m{k}") for k in range(3)]
        ops = m.ps("o")
        s_ones = m.sem("ones")
        s_ld = [m.sem(f"ld{u}") for u in range(RING)]
        s_vs, s_mm, s_mx = m.sem("vs"), m.sem("maxprod"), m.sem("maxima")
        s_chain = m.sem("chain")
        s_m16, s_row, s_qm = m.sem("m16"), m.sem("maxrow"), m.sem("qamax")
        s_s, s_e, s_pv = m.sem("scores"), m.sem("exp"), m.sem("pv")
        s_o, s_qv = m.sem("out"), [m.sem(f"qaversions{h}") for h in range(2)]
        s_st = [m.sem(f"st{u}") for u in range(RING)]
        LOADS = 3 + (2 * 7 if rel else 3)
        CONST = 2 * 16 if rel else 0
        MAXES = 2 * 2 * KT
        ONES = 2 * RING + (0 if rel else 2 * RING)

        def queries(h, version, first, count):
            at = (h * versions + version) * L + first
            return slice(at, at + count)

        def load(sp, pair, u):
            heads = bass.ds(pair * 2, 2)
            for part, row in ((0, R_QK), (1, R_QK + HD), (0, R_LOW)):
                sp.dma_start(ka[u][row:row + HD, :].rearrange("p (h n) -> p h n", h=2),
                             scratch["qk"][1, heads, part, :, :].rearrange("h r n -> r h n")).then_inc(s_ld[u], 16)
            if not rel:
                for part, row in ((0, R_QK), (0, R_QK + HD), (1, R_LOW)):
                    sp.dma_start(qa[u][row:row + HD, :].rearrange("p (h n) -> p h n", h=2),
                                 scratch["qk"][0, heads, part, :, :].rearrange("h r n -> r h n")
                                 ).then_inc(s_ld[u], 16)
                return
            for h in range(2):
                head = bass.ds(pair * 2 + h, 1)
                to = qa[u][:, h * versions * L:(h + 1) * versions * L]
                for part, row in ((0, R_QK), (0, R_QK + HD), (1, R_LOW)):
                    src = scratch["qk"][0, head, part, :, :].rearrange("a r n -> (a r) n").unsqueeze(1)
                    sp.dma_start(to[row:row + HD, :].rearrange("p (v n) -> p v n", v=versions),
                                 src.broadcast_to([HD, versions, L])).then_inc(s_ld[u], 16)
                for k in range(2):
                    for half in range(2):
                        row = R_REL + 2 * QSIDE * k
                        src = scratch["rel"][head, k, half].rearrange("a p r n -> (a p r) n").unsqueeze(1)
                        dst = to[row:row + 2 * QSIDE, :].rearrange("p (u s n) -> p u s n", u=2, s=2)
                        dst = dst[:, half, :, :] if k == 0 else dst[:, :, half, :]
                        sp.dma_start(dst, src.broadcast_to([2 * QSIDE, 2, L])).then_inc(s_ld[u], 16)

        def spread_rows(sp, pair, u):
            for h in range(2 if rel else 0):
                sp.wait_ge(s_qm, pair * 4 + (2 * h + 2))
                at = qa[u][R_MAX:R_MAX + 1, h * versions * L:(h + 1) * versions * L]
                sp.dma_start(at[:, L:].rearrange("p (v n) -> p v n", n=L),
                             at[:, 0:L].unsqueeze(1).broadcast_to([1, versions - 1, L])).then_inc(s_qv[h], 16)

        EARLY = 6
        counts = [(2, 0, 0, 0)] + (KT - 2) * [(1, 1, 2, 0)] + [(1, 1, 2, 2)]
        ROW0 = 4
        items, PLAN = [(1, n) for n in range(EARLY, MAXES)] + [(2, n) for n in range(EARLY)], []
        for kt in range(KT):
            PLAN.append([[items.pop(0) for _ in range(c)] for c in counts[kt]])
            if kt == ROW0:
                PLAN[kt][2].append((1, "row", 0))
            if kt == KT - 1:
                PLAN[kt][2].append((1, "row", 1))
        assert not items
        USES = [item for steps in PLAN for step in steps for item in step]
        START = ([(0, n) for n in range(22)] + [(0, "row", 0)] + [(0, n) for n in range(22, MAXES)]
                 + [(i[0] - 1,) + i[1:] for i in USES[-EARLY - 1:]])

        def free(item, pair):
            if item[1] == "row":
                return s_qm, (pair + item[0]) * 4 + (2 * item[2] + 2)
            return s_mx, (pair + item[0]) * MAXES + (item[1] + 1)

        def use_bank(pe, pair, pos, item, u, skip=()):
            started = pair is None
            g = pos if started else len(START) + len(USES) * u + pos
            before = pos - 3
            if started:
                if before >= 0:
                    pe.wait_ge(*free(START[before], 0))
            else:
                while before >= 0 and USES[before][0] in skip:
                    before -= 3
                pe.wait_ge(*free(USES[before], pair if before >= 0 else pair - 1))
            bank, q = mps[g % 3], 0 if started else pair
            v = (u + item[0]) % RING
            if item[1] == "row":
                h = item[2]
                pe.wait_ge(s_m16, (q + item[0]) * 2 + (h + 1))
                for j in range(KT):
                    half = j // 4
                    ins = pe.matmul(bank[32 * half:32 * half + 1, (j % 4) * P:(j % 4 + 1) * P],
                                    m16[:, h * KT + j:h * KT + j + 1], ident16, start=True, stop=True)
                ins.then_inc(s_row, 1)
            else:
                n = item[1]
                h, qi, c = n // 16, n // 2 % 8, n % 2
                width = CHUNK // 2 if rel else CHUNK
                for i in range(CHUNK // width):
                    k0 = c * CHUNK + i * width
                    ins = pe.matmul(bank[:, i * width:(i + 1) * width],
                                    qa[v][0:R_MAX, queries(h, k0 // Q if rel else 0, qi * P, P)],
                                    ka[v][0:R_MAX, h * L + k0:h * L + k0 + width], start=True, stop=True)
                ins.then_inc(s_mm, 1)

        def score(pe, pair, u, h, kt, first=False):
            if kt == 0:
                pe.wait_ge(s_qm, pair * 4 + (2 * h + 2))
            if not first:
                pe.wait_ge(s_e, pair * 16 + (2 * kt + h - 1))
            version = kt * P // Q if rel else 0
            if rel and kt == Q // P:
                pe.wait_ge(s_qv[h], pair * 16 + 16)
            kcol = slice(h * L + kt * P, h * L + (kt + 1) * P)
            for c in range(2):
                ins = pe.matmul(sps[h][:, c * CHUNK:(c + 1) * CHUNK], ka[u][0:R_END, kcol],
                                qa[u][0:R_END, queries(h, version, c * CHUNK, CHUNK)], start=True, stop=True)
            ins.then_inc(s_s, 1)

        def weigh(pe, pair, u, kt):
            pe.wait_ge(s_e, pair * 16 + (2 * kt + 2))
            if kt == 0:
                pe.wait_ge(s_vs, pair * 2 + 2)
                pe.wait_ge(s_o, pair + 1)
            for h in range(2):
                for c in range(2):
                    row = 32 * (2 * h + c)
                    ins = pe.matmul(ops[row:row + 32, :], vs[u][:, (h * KT + kt) * 32:(h * KT + kt + 1) * 32],
                                    pr[h][kt % 2][:, c * CHUNK:(c + 1) * CHUNK], start=kt == 0, stop=kt == KT - 1)
            ins.then_inc(s_pv, 1)

        def pe_pair(pe, turn, pair, u, skip=()):
            pos = 0

            def maxima(steps):
                nonlocal pos
                for item in steps:
                    if item[0] not in skip:
                        if item == USES[len(USES) - EARLY - 1]:
                            pe.wait_ge(s_ld[(u + 2) % RING], (turn + (u + 2) // RING + 1) * (16 * LOADS) + CONST)
                        use_bank(pe, pair, pos, item, u, skip)
                    pos += 1

            for kt in range(KT):
                if kt:
                    score(pe, pair, u, 0, kt)
                maxima(PLAN[kt][0])
                if kt:
                    score(pe, pair, u, 1, kt)
                maxima(PLAN[kt][1])
                if kt:
                    weigh(pe, pair, u, kt - 1)
                if kt == KT - 1 and 1 not in skip:
                    score(pe, pair + 1, (u + 1) % RING, 0, 0)
                maxima(PLAN[kt][2])
            weigh(pe, pair, u, KT - 1)
            if 1 not in skip:
                score(pe, pair + 1, (u + 1) % RING, 1, 0)
            maxima(PLAN[KT - 1][3])

        def bank_of(u, item):
            return mps[(len(START) + len(USES) * u + USES.index(item)) % 3]

        def dve_max(dve, pair, n, bank):
            dve.wait_ge(s_mm, pair * MAXES + (n + 1))
            dve.tensor_reduce(mx[:, n:n + 1], bank[:, :], AX.X, ALU.max).then_inc(s_mx, 1)
            if n % 16 < 15:
                return
            h = n // 16
            dve.wait_ge(s_mx, pair * MAXES + (n + 1))
            dve.tensor_reduce(m32[:, h * KT:(h + 1) * KT],
                              mx[:, 16 * h:16 * h + 16].rearrange("p (q c) -> p q c", c=2),
                              AX.X, ALU.max).then_inc(s_chain, 1)
            dve.wait_ge(s_chain, pair * 2 + (h + 1))
            dve.tensor_scalar(m16[:, h * KT:(h + 1) * KT], m32[:, h * KT:(h + 1) * KT], -1.0, None,
                              ALU.mult).then_inc(s_m16, 1)

        def act_row(act, pair, u, h, bank):
            act.wait_ge(s_row, pair * 2 + (h + 1))
            for half in range(2):
                act.activation(qa[u][R_MAX:R_MAX + 1, queries(h, 0, half * CHUNK, CHUNK)],
                               bank[32 * half:32 * half + 1, :], ACT.Copy).then_inc(s_qm, 1)

        def dve_pair(dve, pair, u, skip=()):
            for item in USES:
                if item[0] not in skip and item[1] != "row":
                    dve_max(dve, pair + item[0], item[1], bank_of(u, item))

        def stage_values(pool, pair, u):
            src = vt[:, ts(pair, KT * 2 * HD)].rearrange("p (k f) -> p k f", k=KT)
            for h in range(2):
                dst = vs[u][:, h * KT * 32:(h + 1) * KT * 32].rearrange("p (k f) -> p k f", k=KT)
                pool.tensor_copy(dst[:, :, 0:HD], src[:, :, h * HD:(h + 1) * HD]).then_inc(s_vs, 1)

        LAST = PAIRS // RING - 1
        LATE = [()] * (RING - 2) + [(2,), (1, 2)]
        with nc.Block() as block:
            @block.sync
            def _(sp):
                for u in range(RING):
                    for h in range(2 if rel else 0):
                        sp.dma_start(ka[u][R_REL:R_QK, h * L:(h + 1) * L], hot).then_inc(s_ld[u], 16)
                    load(sp, u, u)
                for u in range(RING - 1):
                    spread_rows(sp, u, u)
                with sp.Fori(1, PAIRS // RING) as it:
                    for u in range(RING):
                        sp.wait_ge(s_s, it * (16 * RING) + 16 * (u + 1 - RING))
                        load(sp, it * RING + u, u)
                        spread_rows(sp, it * RING + (u - 1), (u - 1) % RING)
                spread_rows(sp, PAIRS - 1, RING - 1)
                for u in range(RING):
                    sp.wait_ge(s_st[u], 16 * (EARLY_HEADS // 2 // RING + 1))
                sp.dma_start(z[0:2 * EARLY_HEADS, :], row_sums(scratch)[0:2 * EARLY_HEADS, :]).then_inc(s_z, 16)
                sp.wait_ge(s_rz, 1)
                sp.dma_start(scratch["rz"][0:2 * EARLY_HEADS, :], rz[0:2 * EARLY_HEADS, :]).then_inc(s_rzst, 16)
                sp.wait_ge(s_rzst, 16)

            @block.gpsimd
            def _(pool):
                for u in range(RING):
                    stage_values(pool, u, u)
                with pool.Fori(1, PAIRS // RING) as it:
                    for u in range(RING):
                        pool.wait_ge(s_pv, it * (KT * RING) + KT * (u + 1 - RING))
                        stage_values(pool, it * RING + u, u)

            @block.tensor
            def _(pe):
                pe.wait_ge(s_ones, ONES)
                pe.wait_ge(s_ld[0], 16 * LOADS + CONST)
                for pos, item in enumerate(START):
                    if item == (1, 0):
                        pe.wait_ge(s_ld[1], 16 * LOADS + CONST)
                    use_bank(pe, None, pos, item, 0)
                score(pe, 0, 0, 0, 0, first=True)
                score(pe, 0, 0, 1, 0, first=True)
                with pe.Fori(0, LAST) as it:
                    for u in range(RING):
                        pe_pair(pe, it, it * RING + u, u)
                for u in range(RING):
                    pe_pair(pe, LAST, LAST * RING + u, u, LATE[u])

            @block.vector
            def _(dve):
                for u in range(RING):
                    ones = vs[u][:, :].rearrange("p (k f) -> p k f", f=32)
                    dve.memset(ones[:, :, HD:32], 1.0).then_inc(s_ones, 1)
                    dve.memset(ka[u][R_MAX:R_MAX + 1, :], 1.0).then_inc(s_ones, 1)
                    if not rel:
                        for buf in (qa, ka):
                            dve.memset(buf[u][R_REL:R_QK, :], 0.0).then_inc(s_ones, 1)
                for u in range(RING):
                    dve.sem_inc(s_st[u], 16)
                dve.sem_inc(s_o, 1)
                for pos, item in enumerate(START):
                    if item[1] != "row":
                        dve_max(dve, item[0], item[1], mps[pos % 3])
                with dve.Fori(0, LAST) as it:
                    for u in range(RING):
                        dve_pair(dve, it * RING + u, u)
                for u in range(RING):
                    dve_pair(dve, LAST * RING + u, u, LATE[u])
                dve.wait_ge(s_z, 16)
                dve.reciprocal(rz[0:2 * EARLY_HEADS, :], z[0:2 * EARLY_HEADS, :]).then_inc(s_rz, 1)

            @block.scalar
            def _(act):
                def exp(pair, kt, h):
                    act.wait_ge(s_s, pair * 16 + (2 * kt + h + 1))
                    if kt >= 2:
                        act.wait_ge(s_pv, pair * KT + (kt - 1))
                    act.activation(pr[h][kt % 2][:, :], sps[h][:, :], ACT.Exp).then_inc(s_e, 1)

                def sums(turn, pair, u):
                    act.wait_ge(s_pv, pair * KT + KT)
                    act.wait_ge(s_st[u], (turn + 1) * 16)
                    act.activation(osb[u][:, :], ops[:, :], ACT.Copy).then_inc(s_o, 1)

                def store(pair, u):
                    act.wait_ge(s_o, pair + 2)
                    act.dma_start(scratch["o"][bass.ds(pair, 1)].rearrange("a p n -> (a p) n"),
                                  osb[u][:, :]).then_inc(s_st[u], 16)

                def act_pair(turn, pair, u, first=False, last=False):
                    exp(pair, 0, 0)
                    if not first:
                        sums(turn - (u == 0), pair - 1, (u - 1) % RING)
                    for kt in range(KT):
                        if kt:
                            exp(pair, kt, 0)
                        exp(pair, kt, 1)
                        if kt == 1 and not first:
                            store(pair - 1, (u - 1) % RING)
                        if kt == ROW0 and not last:
                            act_row(act, pair + 1, (u + 1) % RING, 0, bank_of(u, (1, "row", 0)))
                    if not last:
                        act_row(act, pair + 1, (u + 1) % RING, 1, bank_of(u, (1, "row", 1)))

                for h in range(2):
                    act_row(act, 0, 0, h, mps[START.index((0, "row", h)) % 3])
                for u in range(RING):
                    act_pair(0, u, u, first=u == 0)
                with act.Fori(1, LAST) as it:
                    for u in range(RING):
                        act_pair(it, it * RING + u, u)
                for u in range(RING):
                    act_pair(LAST, LAST * RING + u, u, last=u == RING - 1)
                sums(LAST, PAIRS - 1, RING - 1)
                store(PAIRS - 1, RING - 1)
                for u in range(RING):
                    act.wait_ge(s_st[u], 16 * (PAIRS // RING + 1))


def row_sums(scratch):
    return scratch["o"].rearrange("a (s r) n -> (a s) r n", r=32)[:, HD, :]


def project(nc, name, res, w, b, scratch, stats=None):
    with Pool(nc, name) as m:
        rows = 2 * (B * NH - EARLY_HEADS)
        z, rz = m.sb("z", P), m.sb("rz", P)
        pw = [m.sb("pw0", C), m.sb("pw1", C, parts=C1)]
        bias = m.sb("bias", C)
        groups = T // CHUNK
        num = [[m.sb(f"num{k}{n}", CHUNK, parts=(C0, C1)[k]) for k in range(2)] for n in range(groups)]
        inv = [[m.sb(f"inv{k}{n}", CHUNK, parts=(C0, C1)[k]) for k in range(2)] for n in range(groups)]
        yp = [m.ps(f"y{u}") for u in range(4)]
        s_w, s_z, s_rz, s_rzst = m.sem("w"), m.sem("z"), m.sem("rz"), m.sem("rzst")
        s_ld = [m.sem(f"ld{n}") for n in range(groups)]
        s_at, s_y, s_add, s_bias, s_bn = (m.sem(n) for n in ("at", "y", "add", "bias", "bn"))
        heads = scratch["o"].rearrange("a (h c r) n -> (a h) c r n", h=2, c=2)
        zheads = scratch["rz"].rearrange("(h c) n -> h c n", c=2)
        with nc.Block() as block:
            @block.sync
            def _(sp):
                sp.dma_start(z[0:4 * rows, :], row_sums(scratch)[2 * EARLY_HEADS:, :].rearrange(
                    "r (q n) -> r q n", n=P)).then_inc(s_z, 16)
                sp.dma_start(pw[0][:, :], w[0:C0, :]).then_inc(s_w, 16)
                sp.dma_start(pw[1][:, :], w[C0:C, :]).then_inc(s_w, 16)
                sp.dma_start(bias[:, :], b.broadcast_to([P, C])).then_inc(s_w, 16)
                for n in range(groups):
                    if n == EARLY_HEADS // NH * 2:
                        sp.wait_ge(s_rz, 1)
                        sp.dma_start(scratch["rz"][2 * EARLY_HEADS:, :].rearrange("r (q n) -> r q n", n=P),
                                     rz[0:4 * rows, :]).then_inc(s_rzst, 16)
                        sp.wait_ge(s_rzst, 16)
                    for k, (h0, hs) in enumerate(((0, 8), (8, 4))):
                        at = slice(n // 2 * NH + h0, n // 2 * NH + h0 + hs)
                        sp.dma_start(num[n][k][:, :], heads[at, n % 2, 0:HD, :]).then_inc(s_ld[n], 16)
                        sp.dma_start(inv[n][k][:, :],
                                     zheads[at, n % 2, :].unsqueeze(1).broadcast_to([hs, HD, CHUNK])
                                     ).then_inc(s_ld[n], 16)

            @block.gpsimd
            def _(pool):
                pool.wait_ge(s_w, 3 * 16)
                for n in range(groups):
                    tiles = res[:, 4 * n * C:4 * (n + 1) * C].rearrange("p (t f) -> p t f", t=4)
                    pool.tensor_tensor(tiles, tiles, bias[:, :].unsqueeze(1).broadcast_to([P, 4, C]),
                                       ALU.add).then_inc(s_bias, 1)
                    pool.wait_ge(s_bias, n + 1)

            @block.vector
            def _(dve):
                def scale(n):
                    dve.wait_ge(s_ld[n], 64)
                    for k in range(2):
                        dve.tensor_tensor(num[n][k][:, :], num[n][k][:, :], inv[n][k][:, :],
                                          ALU.mult).then_inc(s_at, 1)

                def moments(n):
                    if stats is None:
                        return
                    dve.wait_ge(s_add, 2 * n + 2)
                    for t in range(4 * n, 4 * n + 4):
                        dve.bn_stats(stats[:, ts(t, 6)], res[:, ts(t, C)]).then_inc(s_bn, 1)

                dve.wait_ge(s_z, 16)
                dve.reciprocal(rz[0:4 * rows, :], z[0:4 * rows, :]).then_inc(s_rz, 1)
                for n in range(groups):
                    if n == 0:
                        scale(0)
                    if n + 1 < groups:
                        scale(n + 1)
                    dve.wait_ge(s_bias, n + 1)
                    for i in range(2 * n, 2 * n + 2):
                        dve.wait_ge(s_y, i + 1)
                        pair = res[:, 2 * i * C:2 * (i + 1) * C]
                        dve.tensor_tensor(pair, pair, yp[i % 4][:, 0:2 * C], ALU.add).then_inc(s_add, 1)
                    if n:
                        moments(n - 1)
                moments(groups - 1)

            @block.tensor
            def _(pe):
                pe.wait_ge(s_w, 3 * 16)
                for n in range(groups):
                    pe.wait_ge(s_at, 2 * n + 2)
                    for i in range(2 * n, 2 * n + 2):
                        if i >= 4:
                            pe.wait_ge(s_add, i - 3)
                        for t in range(2 * i, 2 * i + 2):
                            for k in range(2):
                                ins = pe.matmul(yp[i % 4][:, t % 2 * C:(t % 2 + 1) * C],
                                                num[n][k][:, t % 4 * P:(t % 4 + 1) * P], pw[k][:, :],
                                                start=k == 0, stop=k == 1)
                        ins.then_inc(s_y, 1)


E8 = 8


class Gates:

    def __init__(self, m, xt, w, experts, iota, bias=None, b2=None):
        self.xt, self.w, self.experts, self.bias, self.b2 = xt, w, experts, bias, b2
        self.iota = iota.unsqueeze(1).broadcast_to([P, 4, E8])
        self.gw = [m.sb("gw0", 32), m.sb("gw1", 32, parts=C1)]
        self.gb = m.sb("gb", experts) if bias is not None else None
        self.b2s = m.sb("b2", experts * C) if b2 is not None else None
        self.logits, self.value, self.comb, self.scaled = (
            m.sb(n, TILES * E8) for n in ("logits", "value", "comb", "scaled"))
        self.one = m.sb("one", TILES)
        self.few = m.sb("few", 4)
        self.key, self.val, self.top, self.picked, self.eq = (
            m.sb(n, 4 * E8) for n in ("key", "val", "top", "picked", "eq"))
        self.idx = m.sb("idx", 4 * E8, U32)
        self.s_gw, self.s_pad, self.s_begin = m.sem("gw"), m.sem("gwpad"), m.sem("begin")
        self.s_l, self.s_copy, self.s_turned = m.sem("logit"), m.sem("lcopy"), m.sem("lturned")
        self.s_read, self.s_exp, self.s_chain = m.sem("gread"), m.sem("gexp"), m.sem("gchain")
        self.loads = 2 + (bias is not None) + (b2 is not None)
        self.count = (4 if bias is None else 2) + 10 + 5 + (3 if bias is None else 2) + 2
        self.count += 4 * experts if b2 is not None else 0

    @staticmethod
    def cube(t):
        return t.rearrange("p (t e) -> p t e", e=E8)

    def clear(self, pool):
        for t in self.gw:
            pool.memset(t[:, :], 0.0).then_inc(self.s_pad, 1)

    def load(self, act):
        act.wait_ge(self.s_pad, 2)
        for t, src in zip(self.gw, (self.w[0:C0, :], self.w[C0:C, :])):
            act.dma_start(t[:, 0:self.experts], src).then_inc(self.s_gw, 16)
        if self.bias is not None:
            act.dma_start(self.gb[:, :], self.bias.broadcast_to([P, self.experts])).then_inc(self.s_gw, 16)
        if self.b2 is not None:
            act.dma_start(self.b2s[:, :], self.b2.broadcast_to([P, self.experts * C])).then_inc(self.s_gw, 16)

    def products(self, pe, banks, turned, copies, ident):
        pe.wait_ge(self.s_gw, 16 * self.loads)
        for i in range(2):
            for k, n in enumerate((C0, C1)):
                for j in range(4):
                    ins = pe.matmul(banks[i][32 * j:32 * j + 32, :], self.gw[k][:, :],
                                    self.xt[k][0:n, (4 * i + j) * CHUNK:(4 * i + j + 1) * CHUNK],
                                    start=k == 0, stop=k == 1)
            ins.then_inc(self.s_l, 1)
        for i in range(2):
            pe.wait_ge(self.s_copy, i + 1)
            for t in range(4):
                ins = pe.transpose(turned[i][:, t * P:(t + 1) * P],
                                   copies[:, i * CHUNK + t * P:i * CHUNK + (t + 1) * P], ident)
            ins.then_inc(self.s_turned, 1)

    def copy(self, act, banks, copies):
        for i in range(2):
            act.wait_ge(self.s_l, i + 1)
            act.activation(copies[:, i * CHUNK:(i + 1) * CHUNK], banks[i][:, :], ACT.Copy).then_inc(self.s_copy, 1)

    def begin(self, dve, turned, s_free):
        link = linker(dve, self.s_begin)
        logits, value = self.cube(self.logits[:, :]), self.cube(self.value[:, :])
        if self.experts < E8:
            link(dve.memset(self.logits[:, :], -3.0e38))
        dve.wait_ge(self.s_gw, 16 * self.loads)
        for i in range(2):
            dve.wait_ge(self.s_turned, i + 1)
            dst = self.logits[:, i * 16 * E8:(i + 1) * 16 * E8].rearrange("p (j t e) -> p t j e", j=4, e=E8)
            src = turned[i][:, :].rearrange("p (t j e) -> p t j e", t=4, j=4)
            for t in range(4):
                to, psum = dst[:, t, :, 0:self.experts], src[:, t, :, 0:self.experts]
                if self.bias is None:
                    dve.tensor_copy(to, psum).then_inc(self.s_read, 1)
                else:
                    dve.tensor_tensor(to, psum, self.gb[:, :].unsqueeze(1).broadcast_to([P, 4, self.experts]),
                                      ALU.add).then_inc(self.s_read, 1)
        dve.wait_ge(self.s_read, 8)
        dve.sem_inc(s_free, 2)
        link(dve.tensor_reduce(self.one[:, :], logits, AX.X, ALU.max))
        dve.tensor_tensor(value, logits, self.one[:, :].unsqueeze(2).broadcast_to([P, TILES, E8]),
                          ALU.subtract).then_inc(self.s_begin, 1)

    def exp(self, act):
        act.wait_ge(self.s_begin, 2 + (self.experts < E8))
        act.activation(self.value[:, :], self.value[:, :], ACT.Exp).then_inc(self.s_exp, 1)

    def steps(self, dve, chunk, res):
        done = [0]

        def inc(ins):
            ins.then_inc(self.s_chain, 1)
            done[0] += 1

        def link(ins):
            inc(ins)
            dve.wait_ge(self.s_chain, chunk * self.count + done[0])

        comb = self.cube(self.comb[:, ts(chunk, 4 * E8)])
        one = self.few[:, :]
        wide = one.unsqueeze(2).broadcast_to([P, 4, E8])
        top, picked, eq, idx, value = (self.cube(t[:, :]) for t in (
            self.top, self.picked, self.eq, self.idx, self.val))
        key = value if self.bias is None else self.cube(self.key[:, :])

        def softmax():
            link(dve.tensor_copy(self.val[:, :], self.value[:, ts(chunk, 4 * E8)]))
            if self.bias is None:
                link(dve.tensor_reduce(one, value, AX.X, ALU.add))
                link(dve.reciprocal(one, one))
                link(dve.tensor_tensor(value, value, wide, ALU.mult))
            else:
                link(dve.tensor_copy(self.key[:, :], self.logits[:, ts(chunk, 4 * E8)]))

        def hold():
            inc(dve.memset(self.eq[:, 0:1], 0.0))

        def best():
            hold()
            for t in range(4):
                inc(dve.max(out=top[:, t, :], in_=key[:, t, :]))
            dve.wait_ge(self.s_chain, chunk * self.count + done[0])

        def places():
            hold()
            for t in range(4):
                inc(dve.max_index(idx[:, t, :], top[:, t, :], key[:, t, :]))
            dve.wait_ge(self.s_chain, chunk * self.count + done[0])

        def pick():
            link(dve.tensor_copy(top, idx))
            inc(dve.tensor_tensor(eq, self.iota, top[:, :, 0:1].broadcast_to([P, 4, E8]), ALU.is_equal))
            link(dve.tensor_tensor(picked, self.iota, top[:, :, 1:2].broadcast_to([P, 4, E8]), ALU.is_equal))
            link(dve.tensor_tensor(picked, picked, eq, ALU.add))
            link(dve.tensor_tensor(picked, picked, value, ALU.mult))

        def weights():
            link(dve.tensor_reduce(one, picked, AX.X, ALU.add))
            if self.bias is None:
                link(dve.tensor_scalar(one, one, 1e-8, None, ALU.add))
            link(dve.reciprocal(one, one))
            link(dve.tensor_tensor(comb, picked, wide, ALU.mult))
            link(dve.tensor_scalar(self.cube(self.scaled[:, ts(chunk, 4 * E8)]), comb, 1.0 / W_SCALE, None,
                                   ALU.mult))

        def biases():
            for e in range(self.experts if self.b2 is not None else 0):
                for t in range(4):
                    tile = chunk * 4 + t
                    inc(dve.scalar_tensor_tensor(out=res[:, ts(tile, C)], in0=self.b2s[:, e * C:(e + 1) * C],
                                                 scalar=self.comb[:, bass.ds(tile * E8 + e, 1)],
                                                 in1=res[:, ts(tile, C)], op0=ALU.mult, op1=ALU.add))
                dve.wait_ge(self.s_chain, chunk * self.count + done[0])
            assert done[0] == self.count

        return [softmax, best, places, pick, weights, biases]


W_SCALE = 64.0


def feed_forward(nc, name, parts, room, res, blocks, mt, w_up, w_down, ident, gate_bank=None, b_up=None, gate=None,
                 b_down=None, stats=None, final=None):
    gated = gate_bank is not None
    per_turn = 1 if blocks % 2 == 0 else 2
    turns = T // CHUNK // per_turn
    ring = 2 if gated else 4
    mats = (gate_bank, w_up) if gated else (w_up,)
    nm = len(mats)
    bw = mt * P
    hid = blocks * bw
    xa_hi, xa_lo, xb = parts
    assert per_turn * blocks * mt % ring == 0
    with Pool(nc, name) as m:
        ah = [m.sb(f"ah{i}", hid, F16) for i in range(nm)]
        al = [m.sb(f"al{i}", hid, F16) for i in range(nm)]
        bh = [m.sb(f"bh{i}", hid, F16) for i in range(nm)]
        bl = [m.sb(f"bl{i}", hid, F16, parts=C1) for i in range(nm)]
        raw_a = [[m.sb(f"ra{i}{r}", bw) for i in range(nm)] for r in range(2)]
        raw_b = [[m.sb(f"rb{i}{r}", bw) for i in range(nm)] for r in range(2)]
        dh, dl = (m.sb(n, blocks * mt * C, F16) for n in ("dh", "dl"))
        raw_d = [m.sb(f"rd{r}", mt * C) for r in range(2)]
        bu = m.sb("bu", blocks * mt) if b_up is not None else None
        bd = m.sb("bd", C) if b_down is not None else None
        hh, hl = ([t[:, u * mt * CHUNK:(u + 1) * mt * CHUNK] for u in range(2)] for t in room)
        h32 = m.sb("h32", 2 * CHUNK)
        s_buf = [m.sb(f"s{u}", CHUNK) for u in range(2)] if gated else None
        ups = [[m.ps(f"u{i}{k}") for i in range(nm)] for k in range(ring)]
        yps = [[m.ps(f"y{u}{k}") for k in range(2)] for u in range(2)]
        s_raw = [m.sem(f"raw{r}") for r in range(2)]
        s_wh, s_wl, s_b = m.sem("wh"), m.sem("wl"), m.sem("b")
        s_up, s_s, s_h32, s_hh, s_hl = (m.sem(n) for n in ("up", "s", "h32", "hh", "hl"))
        s_down, s_y, s_bias = m.sem("down"), m.sem("y"), m.sem("bias")
        s_fin, s_out = m.sem("fin"), m.sem("out")
        n_b = (b_up is not None) + (b_down is not None)
        gates = Gates(m, **gate) if gate else None

        def unit(it, c, blk, k):
            return it * (per_turn * blocks * mt) + ((c * blocks + blk) * mt + k)

        def block_no(it, c, blk):
            return it * (per_turn * blocks) + (c * blocks + blk)

        LAST_BLOCK = (-1, blocks - 1)
        LAST_UNIT = (-1, blocks - 1, mt - 1)
        SPLITS = 2 * nm + 1

        def cut(blk):
            return slice(blk * bw, (blk + 1) * bw)

        with nc.Block() as block:
            @block.sync
            def _(sp):
                if b_up is not None:
                    sp.dma_start(bu[:, :], b_up).then_inc(s_b, 16)
                if b_down is not None:
                    sp.dma_start(bd[:, :], b_down.broadcast_to([P, C])).then_inc(s_b, 16)
                for blk in range(blocks):
                    r = blk % 2
                    if blk >= 2:
                        sp.wait_ge(s_wl, SPLITS * (blk - 1))
                    for i, src in enumerate(mats):
                        sp.dma_start(raw_a[r][i][:, :], src[0:C0, cut(blk)]).then_inc(s_raw[r], 16)
                        for half in range(2):
                            sp.dma_start(raw_b[r][i][C1 * half:C1 * (half + 1), :],
                                         src[C0:C, cut(blk)]).then_inc(s_raw[r], 16)
                    sp.dma_start(raw_d[r][:, :].rearrange("p (k n) -> p k n", n=C),
                                 w_down[cut(blk), :].rearrange("(k p) n -> p k n", p=P)).then_inc(s_raw[r], 16)
                if final is not None:
                    for n in range(T // CHUNK):
                        sp.wait_ge(s_fin, n + 1)
                        sp.dma_start(final[1][n * CHUNK:(n + 1) * CHUNK, :].rearrange("(t p) f -> p t f", p=P),
                                     res[:, n * 4 * C:(n + 1) * 4 * C].rearrange("p (t f) -> p t f", t=4)
                                     ).then_inc(s_out, 16)
                    sp.wait_ge(s_out, 16 * (T // CHUNK))

            def run(engine, turn_of):
                turn_of(0, True)
                with engine.Fori(1, turns) as it:
                    turn_of(it, False)

            @block.gpsimd
            def _(pool):
                if gates:
                    gates.clear(pool)

            @block.tensor
            def _(pe):
                def rise(it, c, blk, first):
                    cols = ts(it * per_turn + c, CHUNK)
                    if first and c == 0:
                        pe.wait_ge(s_wl, SPLITS * (blk + 1))
                    for k in range(mt):
                        pe.wait_ge(s_h32 if gated else s_hh, unit(it, c, blk, k) + 1)
                        n = (c * blocks + blk) * mt + k
                        w = slice((blk * mt + k) * P, (blk * mt + k + 1) * P)
                        for i in range(nm):
                            bank = ups[n % ring][i][:, :]
                            pe.matmul(bank, ah[i][:, w], xa_hi[:, cols], start=True, stop=False)
                            pe.matmul(bank, al[i][:, w], xa_hi[:, cols], start=False, stop=False)
                            pe.matmul(bank, ah[i][:, w], xa_lo[:, cols], start=False, stop=False)
                            pe.matmul(bank, bh[i][:, w], xb[:, cols], start=False, stop=False)
                            ins = pe.matmul(bank, bl[i][:, w], xb[0:C1, cols], start=False, stop=True)
                        ins.then_inc(s_up, 1)

                def fall(it, c, blk):
                    q = c * blocks + blk
                    pe.wait_ge(s_hl, unit(it, c, blk, mt - 1) + 3)
                    pe.wait_ge(s_y, block_no(it, c, blk) + 1)
                    for t in range(4):
                        for k in range(mt):
                            w = slice((blk * mt + k) * C, (blk * mt + k + 1) * C)
                            x = slice(k * CHUNK + t * P, k * CHUNK + (t + 1) * P)
                            for i, (hidden, down) in enumerate(((hh, dh), (hh, dl), (hl, dh))):
                                ins = pe.matmul(yps[q % 2][t // 2][:, (t % 2) * C:(t % 2 + 1) * C],
                                                hidden[q % 2][:, x], down[:, w],
                                                start=k == 0 and i == 0, stop=k == mt - 1 and i == 2)
                    ins.then_inc(s_down, 1)

                def one_turn(it, first):
                    last = None if first else LAST_BLOCK
                    for c in range(per_turn):
                        for blk in range(blocks):
                            rise(it, c, blk, first)
                            if last is not None:
                                fall(it, *last)
                            last = (c, blk)

                if gates:
                    gates.products(pe, yps[1], yps[0], h32, ident)
                else:
                    pe.sem_inc(s_y, 2)
                pe.sem_inc(s_h32 if gated else s_hh, ring)
                run(pe, one_turn)
                fall(turns, *LAST_BLOCK)

            @block.scalar
            def _(act):
                def split_high(blk):
                    act.wait_ge(s_raw[blk % 2], 16 * (3 * nm + 1) * (blk // 2 + 1))
                    for i in range(nm):
                        for raw, high in ((raw_a, ah), (raw_b, bh)):
                            act.activation(high[i][:, cut(blk)], raw[blk % 2][i][:, :], ACT.Identity,
                                           scale=W_SCALE).then_inc(s_wh, 1)
                    act.activation(dh[:, blk * mt * C:(blk + 1) * mt * C], raw_d[blk % 2][:, :], ACT.Identity,
                                   scale=W_SCALE).then_inc(s_wh, 1)

                def high_part(it, c, blk, k):
                    n = unit(it, c, blk, k)
                    q = c * blocks + blk
                    if k == 0:
                        act.wait_ge(s_down, block_no(it, c, blk) + 1)
                    act.wait_ge(s_h32, n + (1 + ring))
                    i = (q * mt + k) % 2
                    act.activation(hh[q % 2][:, k * CHUNK:(k + 1) * CHUNK], h32[:, i * CHUNK:(i + 1) * CHUNK],
                                   ACT.Identity).then_inc(s_hh, 1)

                def one_turn(it, first):
                    last = None if first else LAST_UNIT
                    for c in range(per_turn):
                        for blk in range(blocks):
                            if first and c == 0 and blk + 1 < blocks:
                                split_high(blk + 1)
                            q = c * blocks + blk
                            if not gated:
                                act.wait_ge(s_down, block_no(it, c, blk) + 1)
                            for k in range(mt):
                                n = unit(it, c, blk, k)
                                i = q * mt + k
                                act.wait_ge(s_up, n + 1)
                                if gated:
                                    act.wait_ge(s_h32, n + 1)
                                    act.activation(s_buf[i % 2][:, :], ups[i % ring][0][:, :],
                                                   ACT.Silu, scale=1.0 / W_SCALE).then_inc(s_s, 1)
                                    if last is not None:
                                        high_part(it, *last)
                                    last = (c, blk, k)
                                else:
                                    act.wait_ge(s_hl, n + 1)
                                    bank, bias = ups[i % ring][0], bu[:, blk * mt + k:blk * mt + k + 1]
                                    act.activation(h32[:, i % 2 * CHUNK:(i % 2 + 1) * CHUNK], bank[:, :],
                                                   ACT.Gelu, bias=bias, scale=1.0 / W_SCALE).then_inc(s_h32, 1)
                                    act.activation(hh[q % 2][:, k * CHUNK:(k + 1) * CHUNK], bank[:, :],
                                                   ACT.Gelu, bias=bias, scale=1.0 / W_SCALE).then_inc(s_hh, 1)

                if gates:
                    gates.load(act)
                    gates.copy(act, yps[1], h32)
                split_high(0)
                if gates:
                    gates.exp(act)
                if n_b:
                    act.wait_ge(s_b, n_b * 16)
                act.sem_inc(s_down, 2)
                run(act, one_turn)
                if gated:
                    high_part(turns, *LAST_UNIT)

            @block.vector
            def _(dve):
                def split_low(blk):
                    dve.wait_ge(s_wh, SPLITS * (blk + 1))
                    for i in range(nm):
                        for raw, high, low, n in ((raw_a, ah, al, P), (raw_b, bh, bl, C1)):
                            dve.scalar_tensor_tensor(out=low[i][0:n, cut(blk)], in0=raw[blk % 2][i][0:n, :],
                                                     scalar=W_SCALE, in1=high[i][0:n, cut(blk)],
                                                     op0=ALU.mult, op1=ALU.subtract).then_inc(s_wl, 1)
                    cols = slice(blk * mt * C, (blk + 1) * mt * C)
                    dve.scalar_tensor_tensor(out=dl[:, cols], in0=raw_d[blk % 2][:, :], scalar=W_SCALE,
                                             in1=dh[:, cols], op0=ALU.mult, op1=ALU.subtract).then_inc(s_wl, 1)

                def low_part(it, c, blk, k):
                    n = unit(it, c, blk, k)
                    q = c * blocks + blk
                    i = (q * mt + k) % 2
                    dve.wait_ge(s_hh, n + (1 if gated else 1 + ring))
                    cols = slice(k * CHUNK, (k + 1) * CHUNK)
                    dve.tensor_tensor(hl[q % 2][:, cols], h32[:, i * CHUNK:(i + 1) * CHUNK], hh[q % 2][:, cols],
                                      ALU.subtract).then_inc(s_hl, 1)

                def collect(it, c, blk):
                    q = c * blocks + blk
                    dve.wait_ge(s_down, block_no(it, c, blk) + 3)
                    dve.wait_ge(s_y, block_no(it, c, blk) + 2)
                    for t in range(4):
                        tile = (it * per_turn + c) * 4 + t
                        y = yps[q % 2][t // 2][:, (t % 2) * C:(t % 2 + 1) * C]
                        dst = res[:, ts(tile, C)]
                        if gates is None:
                            ins = dve.scalar_tensor_tensor(out=dst, in0=y, scalar=1.0 / W_SCALE, in1=dst,
                                                           op0=ALU.mult, op1=ALU.add)
                        else:
                            ins = dve.scalar_tensor_tensor(out=dst, in0=y, scalar=gates.scaled[:, bass.ds(tile * E8 + blk, 1)],
                                                           in1=dst, op0=ALU.mult, op1=ALU.add)
                    ins.then_inc(s_y, 1)
                    if blk == 0 and not (isinstance(it, int) and it == 0 and c == 0):
                        finish(it * per_turn + (c - 1))

                def finish(chunk):
                    if final is not None:
                        cols = ts(chunk, 4 * C)
                        dve.tensor_tensor(res[:, cols], res[:, cols], final[0][:, cols], ALU.add).then_inc(s_fin, 1)
                    elif stats is not None:
                        for t in range(4):
                            tile = chunk * 4 + t
                            dve.bn_stats(stats[:, ts(tile, 6)], res[:, ts(tile, C)]).then_inc(s_fin, 1)

                def one_turn(it, first):
                    last, late = (None, None) if first else (LAST_BLOCK, LAST_UNIT)
                    for c in range(per_turn):
                        steps = gates.steps(dve, it * per_turn + c, res) if gates else []
                        for blk in range(blocks):
                            if first and c == 0 and blk + 1 < blocks:
                                split_low(blk + 1)
                            q = c * blocks + blk
                            for k in range(mt):
                                n = unit(it, c, blk, k)
                                i = q * mt + k
                                if gated:
                                    dve.wait_ge(s_s, n + 1)
                                    dve.wait_ge(s_hl, n + 1)
                                    dve.scalar_tensor_tensor(out=h32[:, i % 2 * CHUNK:(i % 2 + 1) * CHUNK],
                                                             in0=ups[i % ring][1][:, :], scalar=1.0 / W_SCALE,
                                                             in1=s_buf[i % 2][:, :],
                                                             op0=ALU.mult, op1=ALU.mult).then_inc(s_h32, 1)
                                    if steps and blk < 2:
                                        steps.pop(0)()
                                    if late is not None:
                                        low_part(it, *late)
                                    late = (c, blk, k)
                                else:
                                    low_part(it, c, blk, k)
                            if last is not None:
                                collect(it, *last)
                            while steps and blk == (1 if gated else 0):
                                steps.pop(0)()
                            last = (c, blk)

                split_low(0)
                if gates:
                    gates.begin(dve, yps[0], s_y)
                    dve.wait_ge(gates.s_exp, 1)
                if bd is not None:
                    dve.wait_ge(s_b, n_b * 16)
                    dve.tensor_tensor(res[:, :].rearrange("p (t f) -> p t f", t=TILES),
                                      res[:, :].rearrange("p (t f) -> p t f", t=TILES),
                                      bd[:, :].unsqueeze(1).broadcast_to([P, TILES, C]), ALU.add).then_inc(s_bias, 1)
                    dve.wait_ge(s_bias, 1)
                dve.sem_inc(s_hl, 2)
                run(dve, one_turn)
                if gated:
                    low_part(turns, *LAST_UNIT)
                collect(turns, *LAST_BLOCK)
                dve.wait_ge(s_y, T // CHUNK * blocks + 2)
                finish(T // CHUNK - 1)


def turn(nc, name, src, parts, ident):
    xa_hi, xa_lo, xb = parts
    with Pool(nc, name) as m:
        t0 = [m.ps(f"t0{u}") for u in range(2)]
        t1 = [m.ps(f"t1{u}") for u in range(2)]
        s_t, s_hi, s_lo = m.sem("turned"), m.sem("hi"), m.sem("lo")
        with nc.Block() as block:
            @block.tensor
            def _(pe):
                for n in range(TILES // 4):
                    if n >= 2:
                        pe.wait_ge(s_lo, 2 * n - 2)
                    for j in range(4):
                        t = 4 * n + j
                        pe.transpose(t0[n % 2][:, j * P:(j + 1) * P], src[:, t * C:t * C + C0], ident)
                        ins = pe.transpose(t1[n % 2][0:C1, j * P:(j + 1) * P], src[:, t * C + C0:(t + 1) * C], ident)
                    ins.then_inc(s_t, 1)

            @block.scalar
            def _(act):
                for n in range(TILES // 4):
                    act.wait_ge(s_t, n + 1)
                    cols = slice(n * CHUNK, (n + 1) * CHUNK)
                    act.activation(xa_hi[:, cols], t0[n % 2][:, :], ACT.Identity).then_inc(s_hi, 1)
                    act.activation(xb[0:C1, cols], t1[n % 2][0:C1, :], ACT.Identity).then_inc(s_hi, 1)

            @block.vector
            def _(dve):
                for n in range(TILES // 4):
                    cols = slice(n * CHUNK, (n + 1) * CHUNK)
                    dve.wait_ge(s_hi, 2 * n + 2)
                    dve.tensor_tensor(xa_lo[:, cols], t0[n % 2][:, :], xa_hi[:, cols], ALU.subtract).then_inc(s_lo, 1)
                    dve.tensor_tensor(xb[C1:P, cols], t1[n % 2][0:C1, :], xb[0:C1, cols],
                                      ALU.subtract).then_inc(s_lo, 1)


def build(nc, a, out, stop=99):
    with ExitStack() as ctx:
        def sb(name, width, dt=F32, parts=P):
            return ctx.enter_context(nc.sbuf_tensor(name, [parts, width], dt))

        x = sb("x", TILES * C)
        y = sb("y", TILES * C)
        vt = sb("vt", TILES * C)
        xt = [sb("xt0", T), sb("xt1", T)]
        ident, ident16 = sb("ident", P), sb("ident16", P, F16)
        iota, cols = sb("iota", 8), sb("cols", 8)
        stats = sb("stats", TILES * 6)
        scratch = {
            "qk": nc.dram_tensor("qk_parts", [2, B * NH, 2, HD, L], F16, kind="Internal").ap(),
            "rel": nc.dram_tensor("rel_parts", [B * NH, 2, 2, 2, QSIDE, L], F16, kind="Internal").ap(),
            "o": nc.dram_tensor("o_sums", [B * NH // 2, P, CHUNK], F32, kind="Internal").ap(),
            "rz": nc.dram_tensor("rz_rows", [2 * B * NH, CHUNK], F32, kind="Internal").ap(),
        }

        with Pool(nc, "start") as m:
            s_in, s_bn = m.sem("in"), m.sem("bn")
            s_x = [m.sem(f"x{n}") for n in range(4)]
            with nc.Block() as block:
                @block.vector
                def _(dve):
                    for n in range(4):
                        dve.wait_ge(s_x[n], 16)
                        for t in range(8 * n, 8 * n + 8):
                            dve.bn_stats(stats[:, ts(t, 6)], x[:, ts(t, C)]).then_inc(s_bn, 1)

                @block.sync
                def _(sp):
                    for n in range(4):
                        sp.dma_start(x[:, n * 8 * C:(n + 1) * 8 * C].rearrange("p (t f) -> p t f", t=8),
                                     a["x"][n * 8 * P:(n + 1) * 8 * P, :].rearrange("(t p) f -> p t f", p=P)
                                     ).then_inc(s_x[n], 16)
                    sp.dma_start(ident[:, :], a["ident"]).then_inc(s_in, 16)
                    sp.dma_start(ident16[:, :], a["ident16"]).then_inc(s_in, 16)
                    sp.dma_start(iota[:, :], a["iota"].broadcast_to([P, 8])).then_inc(s_in, 16)
                    for k, key in enumerate(("ln1_g", "ln1_b", "ln2_g", "ln2_b")):
                        sp.dma_start(cols[:, 2 * k:2 * k + 1], a[key][0:C0, :]).then_inc(s_in, 16)
                        sp.dma_start(cols[0:C1, 2 * k + 1:2 * k + 2], a[key][C0:C, :]).then_inc(s_in, 16)
                    sp.wait_ge(s_in, 11 * 16)

        idn = ident[:, :]
        vt16 = vt[:, :].bitcast(F16)
        parts = [vt16[:, T * k:T * (k + 1)] for k in range(3)]
        hidden = [t[:, :].bitcast(F16) for t in xt]
        room = [t[:, 0:T].bitcast(F16) for t in (xt[0], xt[1], y)]
        stages = []

        def conv(l):
            w = {k: a[f"{l}_{k}"] for k in ("wqk", "bqk", "wv", "bv", "rel_h", "rel_w")}
            w["own"] = a["own"]
            stages.append(lambda: layer_norm(nc, l + "ln", x, 1e-6, stats, xt, idn))
            stages.append(lambda: qkv(nc, l + "qkv", xt, vt, w, scratch))
            stages.append(lambda: attention(nc, l + "att", vt, True, scratch, a["hot"], ident16[:, :], room))
            stages.append(lambda: project(nc, l + "proj", x, a[f"{l}_wo"], a[f"{l}_bo"], scratch, stats))

        conv("c0")
        stages.append(lambda: layer_norm(nc, "f0ln", x, 1e-5, stats, xt, idn, parts=parts))
        stages.append(lambda: feed_forward(nc, "f0", parts, hidden, x, 8, 3, a["f0_up"], a["f0_down"], idn, gate_bank=a["f0_bank"],
                                           gate=dict(xt=xt, w=a["f0_gate"], experts=8, iota=iota[:, :]),
                                           stats=stats))
        conv("c1")
        stages.append(lambda: layer_norm(nc, "h", y, 1e-5, stats, xt, idn, gain=cols[:, 0:2], shift=cols[:, 2:4],
                                         inner=x))
        w1 = {k: a[f"f1_{k}"] for k in ("wqk", "bqk", "wv", "bv")}
        stages.append(lambda: qkv(nc, "f1qkv", xt, vt, w1, scratch))
        stages.append(lambda: attention(nc, "f1att", vt, False, scratch, None, ident16[:, :]))
        stages.append(lambda: project(nc, "f1proj", y, a["f1_wo"], a["f1_bo"], scratch))
        stages.append(lambda: turn(nc, "f1turn", y, parts, idn))
        stages.append(lambda: feed_forward(nc, "mlp", parts, hidden, y, 1, 6, a["mlp_w1"], a["mlp_w2"], idn, b_up=a["mlp_b1"], b_down=a["mlp_b2"], stats=stats))
        stages.append(lambda: layer_norm(nc, "xm", y, 1e-5, stats, xt, idn, gain=cols[:, 4:6], shift=cols[:, 6:8],
                                         parts=parts))
        stages.append(lambda: feed_forward(nc, "moe", parts, hidden, y, 4, 6, a["exp_w1"], a["exp_w2"], idn, b_up=a["exp_b1"],
                                           gate=dict(xt=xt, w=a["f1_gate"], experts=4, iota=iota[:, :], bias=a["f1_gate_b"],
                                                     b2=a["exp_b2"]), final=(x, out)))
        for s in stages[:stop]:
            s()


def _attn(inputs, l, qkv_w, qkv_b, proj_w, proj_b):
    w, bias = np.asarray(inputs[qkv_w]), np.asarray(inputs[qkv_b])
    q, k, v = w[0:C], w[C:2 * C], w[2 * C:]
    bq, bk = bias[0:C], bias[C:2 * C]
    groups = [slice(GW * g, GW * (g + 1)) for g in range(GROUPS)]
    return {
        f"{l}_wqk": np.concatenate([np.concatenate([q[s], k[s]]) for s in groups]).T,
        f"{l}_bqk": np.stack([np.concatenate([bq[s], bk[s]]) for s in groups], axis=1),
        f"{l}_wv": v.T,
        f"{l}_bv": bias[2 * C:][None],
        f"{l}_wo": np.asarray(inputs[proj_w]).T,
        f"{l}_bo": np.asarray(inputs[proj_b])[None],
    }


def host_arrays(inputs):
    i = {k: np.asarray(v) for k, v in inputs.items()}
    a = {"x": i["x"].reshape(B, 2, QSIDE, 2, QSIDE, C).transpose(0, 1, 3, 2, 4, 5).reshape(T, C)}
    for l, n in (("c0", "L0_conv"), ("c1", "L1_conv")):
        a.update(_attn(i, l, f"{n}_qkv_w", f"{n}_qkv_b", f"{n}_proj_w", f"{n}_proj_b"))
        a[f"{l}_rel_h"] = i[f"{n}_rel_pos_h"][::-1].T
        a[f"{l}_rel_w"] = i[f"{n}_rel_pos_w"][::-1].T
    a.update(_attn(i, "f1", "L1_ffn_in_w", "L1_ffn_in_b", "L1_ffn_out_w", "L1_ffn_out_b"))
    wide = lambda w: w.transpose(1, 0, 2).reshape(C, -1)
    a["f0_gate"] = i["L0_ffn_gate_w"].T
    a["f0_bank"], a["f0_up"] = wide(i["L0_ffn_gate_bank"]), wide(i["L0_ffn_up_bank"])
    a["f0_down"] = i["L0_ffn_down_bank"].reshape(-1, C)
    for k in ("ln1_g", "ln1_b", "ln2_g", "ln2_b"):
        a[k] = i[f"L1_ffn_{k}"][:, None]
    a["mlp_w1"], a["mlp_w2"] = i["L1_ffn_mlp_w1"], i["L1_ffn_mlp_w2"]
    a["mlp_b1"] = i["L1_ffn_mlp_b1"].reshape(-1, P).T
    a["mlp_b2"] = i["L1_ffn_mlp_b2"][None]
    a["f1_gate"] = i["L1_ffn_gate_w"].T
    a["f1_gate_b"] = i["L1_ffn_gate_b"][None]
    a["exp_w1"] = wide(i["L1_ffn_exp_w1"])
    a["exp_b1"] = i["L1_ffn_exp_b1"].reshape(-1, P).T
    a["exp_w2"] = i["L1_ffn_exp_w2"].reshape(-1, C)
    a["exp_b2"] = i["L1_ffn_exp_b2"].reshape(1, -1)
    a["ident"] = np.eye(P, dtype=np.float32)
    a["ident16"] = np.eye(P, dtype=np.float16)
    a["iota"] = np.arange(8, dtype=np.float32)[None]
    a["own"] = (np.arange(GW)[:, None] // HD == np.arange(GH)[None]).astype(np.float32) * np.float32(HD ** 0.5)
    token = np.arange(L)
    row, column = (np.equal.outer(np.arange(QSIDE), t) for t in (token % Q // QSIDE, token % QSIDE))
    a["hot"] = np.concatenate([row, row, column, column]).astype(np.float16)
    return {k: np.ascontiguousarray(v) for k, v in a.items()}


def kernel(**inputs):
    import concourse.bacc as bacc
    from concourse.bass_utils import run_bass_kernel_spmd

    nc = bacc.Bacc("TRN2", target_bir_lowering=False, num_devices=1)
    arrays = host_arrays(inputs)
    aps = {k: nc.dram_tensor(f"in_{k}", v.shape, mybir.dt.from_np(v.dtype), kind="ExternalInput").ap()
           for k, v in arrays.items()}
    out = nc.dram_tensor("out_x", (T, C), F32, kind="ExternalOutput").ap()
    build(nc, aps, out)
    r = run_bass_kernel_spmd(nc, [{f"in_{k}": v for k, v in arrays.items()}], core_ids=[0])
    quarters = r.results[0]["out_x"].reshape(B, 2, 2, QSIDE, QSIDE, C)
    return quarters.transpose(0, 1, 3, 2, 4, 5).reshape(B, SIDE, SIDE, C)
```
